# Optimizing a Trainium2 kernel written in Bass

```python
import numpy as np
import jax
import jax.numpy as jnp

def _softmax(x, axis=-1):
    return jax.nn.softmax(x, axis=axis)

def _gelu(x):
    return jax.nn.gelu(x, approximate=True)

def _silu(x):
    return jax.nn.silu(x)

def _sigmoid(x):
    return jax.nn.sigmoid(x)

def _layernorm(x, axis=-1, eps=1e-05):
    m = jnp.mean(x, axis=axis, keepdims=True)
    v = jnp.var(x, axis=axis, keepdims=True)
    return (x - m) / jnp.sqrt(v + eps)

def _scatter_add(tgt, idx, src, axis=0):
    return tgt.at[idx].add(src)

def _segment_sum(src, seg, n):
    return jax.ops.segment_sum(src, seg, n)
kernel_name = 'mk_decoder_postln_d1_seqx_r2_8003bb'

def setup_inputs(seed: int=0):
    np.random.seed(seed)
    _w = jnp.asarray

    def _rec_inputs():
        import jax
        import jax.numpy as jnp
        _rk = jax.random.key(seed)
        x = 7.22e-05 + 1 * jax.random.normal(jax.random.fold_in(_rk, 1), (8, 512, 512), jnp.float32)
        _lenS = 512 - jax.random.randint(jax.random.fold_in(_rk, 7), (8,), 0, max(1, 512 // 4) + 1, jnp.int32)
        _lenS2 = 77 - jax.random.randint(jax.random.fold_in(_rk, 8), (8,), 0, max(1, 77 // 4) + 1, jnp.int32)
        _ctx_1024P = jax.random.normal(jax.random.fold_in(_rk, 11), (8, 16, 512), jnp.float32)
        _ctx_1024c = jax.random.dirichlet(jax.random.fold_in(_rk, 511), 0.3 * jnp.ones((16,), jnp.float32), (8, 77))
        _ctx_1024t = jnp.einsum('bsk,bkd->bsd', _ctx_1024c, _ctx_1024P)
        _ctx_1024t = _ctx_1024t * jax.lax.rsqrt(jnp.mean(jnp.square(_ctx_1024t)) + 1e-12) * 0.953939
        ctx_1024 = 4.13588e-05 + 0.999923 * (_ctx_1024t + 0.3 * jax.random.normal(jax.random.fold_in(_rk, 611), (8, 77, 512), jnp.float32))
        _validS = jnp.arange(512)[None, :] < _lenS[:, None]
        _validS2 = jnp.arange(77)[None, :] < _lenS2[:, None]
        _causal = jnp.tril(jnp.ones((512, 512), dtype=bool))
        mask_BxSxS2_ik1 = jnp.where(jnp.broadcast_to(_validS2[:, None, :], (8, 512, 77)), 1, 0).astype(jnp.int32)
        return (x, ctx_1024, mask_BxSxS2_ik1)
    x, ctx_1024, mask_BxSxS2_ik1 = _rec_inputs()

    def _L0_attn_setup():
        import jax, jax.numpy as jnp
        import numpy as np
        B, S, D, H = (4, 2048, 512, 8)
        HD = D // H
        key = jax.random.key(seed)
        k1, k2, k3 = jax.random.split(key, 3)
        x = jax.random.normal(k1, (B, S, D), dtype=jnp.float32)
        w_qkv = jax.random.normal(k2, (D, 3 * D), dtype=jnp.float32) * (1.0 / np.sqrt(D))
        w_out = jax.random.normal(k3, (D, D), dtype=jnp.float32) * (1.0 / np.sqrt(D))
        return {'x': x, 'w_qkv': w_qkv, 'w_out': w_out}
    _L0_attn_all = _L0_attn_setup()
    _L0_attn_in = {k: v for k, v in _L0_attn_all.items() if k in ('w_qkv', 'w_out')}
    del _L0_attn_all

    def _L0_xattn_setup():
        import jax, jax.numpy as jnp
        import numpy as np
        HIDDEN = 512
        NUM_HEADS = 16
        HEAD_DIM = HIDDEN // NUM_HEADS

        def _split_heads(x):
            B, S, _ = x.shape
            return x.reshape(B, S, NUM_HEADS, HEAD_DIM).transpose(0, 2, 1, 3)
        key = jax.random.key(seed)
        ks = jax.random.split(key, 13)
        B, S, H = (4, 1024, HIDDEN)
        sc = 1.0 / np.sqrt(H)
        inp = {'queries': jax.random.normal(ks[0], (B, S, H), jnp.float32), 'keys': jax.random.normal(ks[1], (B, S, H), jnp.float32), 'values': jax.random.normal(ks[2], (B, S, H), jnp.float32), 'attention_mask': jax.random.randint(ks[3], (B, S, S), 0, 2, jnp.int32), 'W_q': jax.random.normal(ks[4], (H, H), jnp.float32) * sc, 'b_q': jnp.zeros((H,), jnp.float32), 'W_k': jax.random.normal(ks[5], (H, H), jnp.float32) * sc, 'b_k': jnp.zeros((H,), jnp.float32), 'W_v': jax.random.normal(ks[6], (H, H), jnp.float32) * sc, 'b_v': jnp.zeros((H,), jnp.float32), 'W_o': jax.random.normal(ks[7], (H, H), jnp.float32) * sc, 'b_o': jnp.zeros((H,), jnp.float32)}
        return inp
    _L0_xattn_all = _L0_xattn_setup()
    _L0_xattn_in = {k: v for k, v in _L0_xattn_all.items() if k in ('W_q', 'b_q', 'W_k', 'b_k', 'W_v', 'b_v', 'W_o', 'b_o')}
    del _L0_xattn_all

    def _L0_ffn_setup():
        import jax, jax.numpy as jnp
        import numpy as np
        INT4_QMAX = 7.0

        def simulate_quantize_int4(w):
            scale = jnp.max(jnp.abs(w)) / INT4_QMAX
            q = jnp.clip(jnp.round(w / scale), -8.0, 7.0)
            return q * scale
        key = jax.random.key(seed)
        k_x, k_w, k_bias, k_a, k_b = jax.random.split(key, 5)
        d_in, features, rank = (512, 512, 16)
        x = jax.random.normal(k_x, (4, 4096, d_in), dtype=jnp.float32)
        kernel = jax.random.normal(k_w, (d_in, features), dtype=jnp.float32)
        bias = jax.random.normal(k_bias, (features,), dtype=jnp.float32)
        a = jax.random.normal(k_a, (d_in, rank), dtype=jnp.float32) * (1.0 / np.sqrt(d_in))
        b = jax.random.normal(k_b, (rank, features), dtype=jnp.float32) * 0.01
        return {'x': x, 'kernel': kernel, 'bias': bias, 'a': a, 'b': b}
    _L0_ffn_all = _L0_ffn_setup()
    _L0_ffn_in = {k: v for k, v in _L0_ffn_all.items() if k in ('kernel', 'bias', 'a', 'b')}
    del _L0_ffn_all
    return {'x': x, 'ctx_1024': ctx_1024, 'mask_BxSxS2_ik1': mask_BxSxS2_ik1, 'L0_attn_w_qkv': _L0_attn_in['w_qkv'], 'L0_attn_w_out': _L0_attn_in['w_out'], 'L0_xattn_W_q': _L0_xattn_in['W_q'], 'L0_xattn_b_q': _L0_xattn_in['b_q'], 'L0_xattn_W_k': _L0_xattn_in['W_k'], 'L0_xattn_b_k': _L0_xattn_in['b_k'], 'L0_xattn_W_v': _L0_xattn_in['W_v'], 'L0_xattn_b_v': _L0_xattn_in['b_v'], 'L0_xattn_W_o': _L0_xattn_in['W_o'], 'L0_xattn_b_o': _L0_xattn_in['b_o'], 'L0_ffn_kernel': _L0_ffn_in['kernel'], 'L0_ffn_bias': _L0_ffn_in['bias'], 'L0_ffn_a': _L0_ffn_in['a'], 'L0_ffn_b': _L0_ffn_in['b']}

def reference(x, ctx_1024, mask_BxSxS2_ik1, L0_attn_w_qkv, L0_attn_w_out, L0_xattn_W_q, L0_xattn_b_q, L0_xattn_W_k, L0_xattn_b_k, L0_xattn_W_v, L0_xattn_b_v, L0_xattn_W_o, L0_xattn_b_o, L0_ffn_kernel, L0_ffn_bias, L0_ffn_a, L0_ffn_b):
    import jax
    import jax.numpy as jnp

    def _L0_attn_ref(x, w_qkv, w_out):
        import jax, jax.numpy as jnp
        import numpy as np
        B, S, D, H = (4, 2048, 512, 8)
        HD = D // H
        b, s, d = x.shape
        qkv = x @ w_qkv
        q, k, v = jnp.split(qkv, 3, axis=-1)
        q = q.reshape(b, s, H, HD)
        k = k.reshape(b, s, H, HD)
        v = v.reshape(b, s, H, HD)
        fq = jnp.fft.fft(q, axis=-1)
        fk = jnp.fft.fft(k, axis=-1)
        fv = jnp.fft.fft(v, axis=-1)
        kv = fk * fv
        kv = jnp.cumsum(kv, axis=1)
        vals = jnp.fft.ifft(kv * jnp.conj(fq), axis=-1).real.astype(x.dtype)
        vals = vals.reshape(b, s, d)
        return vals @ w_out

    def _L0_xattn_ref(queries, keys, values, attention_mask, W_q, b_q, W_k, b_k, W_v, b_v, W_o, b_o):
        import jax, jax.numpy as jnp
        import numpy as np
        HIDDEN = 512
        NUM_HEADS = 16
        HEAD_DIM = HIDDEN // NUM_HEADS

        def _split_heads(x):
            B, S, _ = x.shape
            return x.reshape(B, S, NUM_HEADS, HEAD_DIM).transpose(0, 2, 1, 3)
        q = _split_heads(queries @ W_q + b_q)
        k = _split_heads(keys @ W_k + b_k)
        v = _split_heads(values @ W_v + b_v)
        d = q.shape[-1]
        scores = jnp.einsum('bhqd,bhkd->bhqk', q, k) / jnp.sqrt(jnp.float32(d))
        mask = attention_mask[:, None, :, :]
        scores = jnp.where(mask == 0, jnp.float32(-1000000.0), scores)
        attn = jax.nn.softmax(scores, axis=-1)
        out = jnp.einsum('bhqk,bhkd->bhqd', attn, v)
        B, _, S, _ = out.shape
        out = out.transpose(0, 2, 1, 3).reshape(B, S, NUM_HEADS * HEAD_DIM)
        return out @ W_o + b_o

    def _L0_ffn_ref(x, kernel, bias, a, b):
        import jax, jax.numpy as jnp
        import numpy as np
        INT4_QMAX = 7.0

        def simulate_quantize_int4(w):
            scale = jnp.max(jnp.abs(w)) / INT4_QMAX
            q = jnp.clip(jnp.round(w / scale), -8.0, 7.0)
            return q * scale
        w = simulate_quantize_int4(kernel)
        y = jnp.einsum('bsd,df->bsf', x, w) + bias
        lora = jnp.einsum('bsr,rf->bsf', jnp.einsum('bsd,dr->bsr', x, a), b)
        return y + lora
    x = _layernorm(x + _L0_attn_ref(x, L0_attn_w_qkv, L0_attn_w_out), axis=-1)
    x = _layernorm(x + _L0_xattn_ref(x, ctx_1024, ctx_1024, mask_BxSxS2_ik1, L0_xattn_W_q, L0_xattn_b_q, L0_xattn_W_k, L0_xattn_b_k, L0_xattn_W_v, L0_xattn_b_v, L0_xattn_W_o, L0_xattn_b_o), axis=-1)
    x = _layernorm(x + _L0_ffn_ref(x, L0_ffn_kernel, L0_ffn_bias, L0_ffn_a, L0_ffn_b), axis=-1)
    return x

_drawn_inputs = setup_inputs


def setup_inputs(seed=0):
    import zlib

    import numpy as np

    out = dict(_drawn_inputs(seed))
    spreads = {'L0_xattn_b_q': (0.0, 0.406),
     'L0_xattn_b_k': (0.0, 0.8),
     'L0_xattn_b_v': (0.0, 0.1),
     'L0_xattn_b_o': (0.0, 0.1)}
    factors = {'L0_ffn_a': 8.0, 'L0_ffn_b': 8.0}
    for name, (base, spread) in spreads.items():
        noise = np.random.default_rng([zlib.crc32(name.encode()), seed]).standard_normal(out[name].shape)
        drawn = base * np.exp(spread * noise) if base else spread * noise
        out[name] = jnp.asarray(drawn.astype(out[name].dtype))
    for name, factor in factors.items():
        out[name] = (out[name] * factor).astype(out[name].dtype)
    return out
```

```python
from contextlib import ExitStack

import numpy as np
import concourse.bass as bass
from concourse import mybir

F32 = mybir.dt.float32
F32R = mybir.dt.float32r
I32 = mybir.dt.int32
ALU = mybir.AluOpType
ACT = mybir.ActivationFunctionType
AX = mybir.AxisListType

P = 128
B, S, D = 8, 512, 512
NT = S // P
NC = D // P
MIX_HEADS, MIX_HD = 8, 64
PAIRS = 2
XH, XHD = 16, 32
KEYS = 77
GROUPS = D // P
GH = XH // GROUPS
GK = GH * KEYS
KC = [(0, 103), (103, 103), (206, 102)]
RANK = 16
EPS = 1e-5
MASKED = -1000000.0
ROUND_MAGIC = 1.5 * 2.0 ** 23
QMAX = 7.0


def nth(batch, per_batch, index):
    return batch * per_batch + (index + 1)


def two_back(batch, per_batch, index):
    return batch * per_batch + max(index - 1, 0)


def wait_reuse(eng, sem, value):
    if not isinstance(value, int) or value > 0:
        eng.wait_ge(sem, value)


def v_pieces():
    for j in range(GH):
        for c, (at, size) in enumerate(KC):
            a, b = max(j * KEYS, at), min((j + 1) * KEYS, at + size)
            if a < b:
                yield j, c, a - at, a - j * KEYS, b - a


def split_matmuls(nc, out, pieces):
    terms = [(l[a], r[b]) for l, r in pieces for a, b in ((0, 0), (1, 0), (0, 1))]
    for n, (l, r) in enumerate(terms):
        last = nc.tensor.matmul(out, l, r, start=(n == 0), stop=(n == len(terms) - 1))
    return last


def prepare_mixing(nc, w_qkv, w_out, dft_forward, dft_inverse, ident, w_spec, w_back):
    with ExitStack() as ctx:
        sb = lambda n, s, d=F32: ctx.enter_context(nc.sbuf_tensor(n, s, d))
        sem = lambda n: ctx.enter_context(nc.semaphore(n))
        wq_sb = sb("wqkv_sb", [P, NC, 3 * D])
        wo_sb = sb("wout_sb", [P, NC, D])
        fwd = sb("fwd_sb", [P, 2, 256])
        inv = sb("inv_sb", [P, 2, 256])
        wT = sb("wT_sb", [P, 2, NC, P])
        turned = [ctx.enter_context(nc.psum_tensor(f"turned{n}", [P, NC, P], F32)) for n in range(2)]
        prod = [ctx.enter_context(nc.psum_tensor(f"folded{n}", [P, 512], F32)) for n in range(2)]
        qkv_loaded, rest_loaded = sem("qkv_loaded"), sem("rest_loaded")
        turned_ready, wT_ready = sem("turned_ready"), sem("wT_ready")
        folded, hi_ready, lo_ready = sem("folded"), sem("folded_hi"), sem("folded_lo")
        GROUP = [(r, s) for r in range(NC) for s in range(3)]
        NG = len(GROUP)
        block = ctx.enter_context(nc.Block())

        def targets(n):
            if n < NG:
                r, s = GROUP[n]
                return w_spec[0][:, r, s, :], w_spec[1][:, r, s, :]
            return w_back[0][:, n - NG, :], w_back[1][:, n - NG, :]

        @block.sync
        def _(sp):
            sp.dma_start(fwd[:], dft_forward).then_inc(rest_loaded, 16)
            for r in range(NC):
                sp.dma_start(wq_sb[:, r, :], w_qkv[r * P:(r + 1) * P, :]).then_inc(qkv_loaded, 16)
            sp.dma_start(wo_sb[:], w_out.rearrange("(c p) n -> p c n", p=P)).then_inc(rest_loaded, 16)
            sp.dma_start(inv[:], dft_inverse).then_inc(rest_loaded, 16)

        @block.tensor
        def _(pe):
            pe.wait_ge(qkv_loaded, 16 * NC)
            pe.wait_ge(rest_loaded, 48)

            def turn(n):
                r, s = GROUP[n]
                wait_reuse(pe, wT_ready, n - 1)
                for c in range(NC):
                    at = s * D + c * P
                    last = nc.tensor.transpose(turned[n % 2][:, c, :], wq_sb[:, r, at:at + P], ident[:])
                last.then_inc(turned_ready, 1)

            turn(0)
            for n in range(NG):
                if n + 1 < NG:
                    turn(n + 1)
                pe.wait_ge(wT_ready, n + 1)
                wait_reuse(pe, lo_ready, n - 1)
                for p in range(PAIRS):
                    for h in range(2):
                        last = nc.tensor.matmul(prod[n % 2][:, p * 256:(p + 1) * 256], wT[:, n % 2, 2 * p + h, :],
                                                fwd[:, h, :], start=(h == 0), stop=(h == 1))
                last.then_inc(folded, 1)
            for f in range(NC):
                n = NG + f
                p, im = f // 2, f % 2
                pe.wait_ge(lo_ready, n - 1)
                for h in range(2):
                    last = nc.tensor.matmul(prod[n % 2][:], inv[:, h, im * P:(im + 1) * P], wo_sb[:, 2 * p + h, :],
                                            start=(h == 0), stop=(h == 1))
                last.then_inc(folded, 1)

        @block.scalar
        def _(act):
            def copy_turned(n):
                act.wait_ge(turned_ready, n + 1)
                wait_reuse(act, folded, n - 1)
                nc.scalar.activation(wT[:, n % 2, :, :], turned[n % 2][:], ACT.Copy).then_inc(wT_ready, 1)

            copy_turned(0)
            for n in range(NG + NC):
                if n + 1 < NG:
                    copy_turned(n + 1)
                act.wait_ge(folded, n + 1)
                nc.scalar.activation(targets(n)[0], prod[n % 2][:], ACT.Copy).then_inc(hi_ready, 1)

        @block.vector
        def _(dve):
            for n in range(NG + NC):
                dve.wait_ge(hi_ready, n + 1)
                hi, lo = targets(n)
                nc.vector.tensor_tensor(lo, prod[n % 2][:], hi.bitcast(F32), ALU.subtract).then_inc(lo_ready, 1)


def mix_tokens(nc, x, x1_dram, ident, sigma, w_spec, w_back, half_power):
    with ExitStack() as ctx:
        sb = lambda n, s, d=F32: ctx.enter_context(nc.sbuf_tensor(n, s, d))
        ps = lambda n, s: ctx.enter_context(nc.psum_tensor(n, s, F32))
        sem = lambda n: ctx.enter_context(nc.semaphore(n))
        x_tok = [sb(f"x_tok{n}", [P, NT, D]) for n in range(2)]
        x_res = sb("x_res", [P, NT, D])
        xT = [[sb(f"xT_{k}{n}", [P, NC, S], F32R) for k in ("hi", "lo")] for n in range(2)]
        v_sb = sb("v_sb", [P, 2, S])
        kv = sb("kv_prod", [P, 4, S])
        state = sb("state", [P, 2, S])
        qs = sb("qs_prod", [P, 4, S])
        vals = sb("vals", [P, 2, S])
        valsT = [sb(f"vals_{k}", [P, NC, S], F32R) for k in ("hi", "lo")]
        r_sb = sb("mix_r", [P, 2, D])
        x1_sb = sb("mix_x1", [P, 2, D])
        stats = sb("mix_stats", [P, 2, 6])
        mv = sb("mix_mv", [P, 2, 2])
        ve = sb("mix_ve", [P, 2])
        rstd = sb("mix_rstd", [P, 2])
        v_ps = [ps(f"v_ps{h}", [P, S]) for h in range(2)]
        k_ps = [ps(f"k_ps{h}", [P, S]) for h in range(2)]
        q_ps = [ps(f"q_ps{h}", [P, S]) for h in range(2)]
        xT_ps = ps("xT_ps", [P, S])
        out_ps = ps("out_ps", [P, D])
        x_loaded = [sem(f"x_loaded{n}") for n in range(2)]
        xres_loaded = sem("xres_loaded")
        x1_stored = [sem(f"x1_stored{n}") for n in range(2)]
        xT_filled, x_hi, x_lo = sem("xT_filled"), sem("x_hi"), sem("x_lo")
        v_filled, k_filled, q_filled, out_filled = sem("v_filled"), sem("k_filled"), sem("q_filled"), sem("out_filled")
        v_copied, kv_done, scanned, qs_done = sem("v_copied"), sem("kv_done"), sem("scanned"), sem("qs_done")
        vals_summed, vals_hi, vals_lo = sem("vals_summed"), sem("vals_hi"), sem("vals_lo")
        r_added, r_stats, r_aggr = sem("r_added"), sem("r_stats"), sem("r_aggr")
        var_eps, rstd_ready, x1_ready = sem("var_eps"), sem("rstd_ready"), sem("x1_ready")
        stats_seen = sem("stats_seen")
        block = ctx.enter_context(nc.Block())

        def steps(eng, step):
            step(0, 0, True, False)
            with eng.Fori(1, B - 1, 2) as i:
                step(i, 1, True, True)
                step(i + 1, 0, True, True)
            step(B - 1, (B - 1) % 2, False, True)

        @block.sync
        def _(sp):
            def load_x(i, half, reuse):
                if reuse:
                    sp.wait_ge(xT_filled, nth(i - 2, NC, NC - 1))
                sp.dma_start(x_tok[half][:], x[i].rearrange("(t p) d -> p t d", p=P)).then_inc(x_loaded[half], 16)

            def finish(i):
                wait_reuse(sp, r_added, nth(i - 1, NT, NT - 1))
                sp.dma_start(x_res[:], x[i].rearrange("(t p) d -> p t d", p=P)).then_inc(xres_loaded, 16)
                for t in range(NT):
                    sp.wait_ge(x1_ready, nth(i, NT, t))
                    sp.dma_start(x1_dram[i, t * P:(t + 1) * P, :], x1_sb[:, t % 2, :]).then_inc(x1_stored[t % 2], 16)

            load_x(0, 0, False)
            load_x(1, 1, False)
            load_x(2, 0, True)
            with sp.Fori(1, B - 3, 2) as i:
                load_x(i + 2, 1, True)
                finish(i - 1)
                load_x(i + 3, 0, True)
                finish(i)
            load_x(B - 1, 1, True)
            for i in range(B - 4, B):
                finish(i)
            for n in range(2):
                sp.wait_ge(x1_stored[n], 16 * B * NT // 2)

        @block.tensor
        def _(pe):
            def turn(i, half, c):
                if c == 0:
                    pe.wait_ge(x_loaded[half], i_loads(i, half))
                wait_reuse(pe, x_lo, nth(i, NC, c - 1))
                for t in range(NT):
                    last = nc.tensor.transpose(xT_ps[:, t * P:(t + 1) * P], x_tok[half][:, t, c * P:(c + 1) * P], ident[:])
                last.then_inc(xT_filled, 1)

            def i_loads(i, half):
                return (i - half) * 8 + 16

            def project(i, half, s, p, h):
                bank, filled, free, done = {
                    2: (v_ps, v_filled, v_copied, i * 4 + (2 * p + h - 1)),
                    1: (k_ps, k_filled, kv_done, i * 8 + (4 * p + 2 * h - 2)),
                    0: (q_ps, q_filled, qs_done, i * 8 + (4 * p + 2 * h - 2)),
                }[s]
                if p == 0 and s == 2 and h == 0:
                    pe.wait_ge(x_lo, nth(i, NC, NC - 1))
                    pe.wait_ge(x_hi, nth(i, NC, NC - 1))
                wait_reuse(pe, free, done)
                at = p * 256 + h * P
                pieces = [([w[:, c, s, at:at + P] for w in w_spec], [t[:, c, :] for t in xT[half]]) for c in range(NC)]
                split_matmuls(nc, bank[h][:], pieces).then_inc(filled, 1)

            def project_back(i, t):
                if t == 0:
                    pe.wait_ge(vals_lo, nth(i, 4, 3))
                    pe.wait_ge(vals_hi, nth(i, 4, 3))
                wait_reuse(pe, r_added, nth(i, NT, t - 1))
                tok = slice(t * P, (t + 1) * P)
                pieces = [([v[:, c, tok] for v in valsT], [w[:, c, :] for w in w_back]) for c in range(NC)]
                split_matmuls(nc, out_ps[:], pieces).then_inc(out_filled, 1)

            def step(i, half, has_next, has_last):
                project(i, half, 2, 0, 0)
                project(i, half, 2, 0, 1)
                for c, (s, h) in enumerate([(1, 0), (1, 1), (0, 0)]):
                    if has_next:
                        turn(i + 1, 1 - half, c)
                    project(i, half, s, 0, h)
                if has_next:
                    turn(i + 1, 1 - half, 3)
                if has_last:
                    project_back(i - 1, 0)
                project(i, half, 0, 0, 1)
                if has_last:
                    project_back(i - 1, 1)
                project(i, half, 2, 1, 0)
                if has_last:
                    project_back(i - 1, 2)
                project(i, half, 2, 1, 1)
                if has_last:
                    project_back(i - 1, 3)
                for s, h in [(1, 0), (1, 1), (0, 0), (0, 1)]:
                    project(i, half, s, 1, h)

            for c in range(NC):
                turn(0, 0, c)
            steps(pe, step)
            for t in range(NT):
                project_back(B - 1, t)

        @block.scalar
        def _(act):
            def split_x(i, half, c):
                act.wait_ge(xT_filled, nth(i, NC, c))
                nc.scalar.activation(xT[half][0][:, c, :], xT_ps[:], ACT.Copy).then_inc(x_hi, 1)

            def copy_v(i, p, h):
                act.wait_ge(v_filled, nth(i, 4, 2 * p + h))
                wait_reuse(act, kv_done, i * 8 + 4 * p)
                nc.scalar.activation(v_sb[:, h, :], v_ps[h][:], ACT.Copy).then_inc(v_copied, 1)

            def split_vals(i, p, h):
                act.wait_ge(vals_summed, nth(i, 4, 2 * p + h))
                if p == 0 and h == 0:
                    wait_reuse(act, out_filled, i * NT)
                nc.scalar.activation(valsT[0][:, 2 * p + h, :], vals[:, h, :], ACT.Copy).then_inc(vals_hi, 1)

            def step(i, half, has_next, has_last):
                copy_v(i, 0, 0)
                copy_v(i, 0, 1)
                if has_next:
                    for c in range(NC):
                        split_x(i + 1, 1 - half, c)
                copy_v(i, 1, 0)
                copy_v(i, 1, 1)
                for p in range(PAIRS):
                    for h in range(2):
                        split_vals(i, p, h)

            for c in range(NC):
                split_x(0, 0, c)
            steps(act, step)

        @block.gpsimd
        def _(pool):
            def root(i, t):
                pool.wait_ge(var_eps, nth(i, NT, t))
                wait_reuse(pool, x1_ready, two_back(i, NT, t))
                nc.gpsimd.tensor_tensor(rstd[:, t % 2:t % 2 + 1], ve[:, t % 2:t % 2 + 1], half_power[:],
                                        ALU.pow).then_inc(rstd_ready, 1)

            def sum_vals(i, p, h):
                pool.wait_ge(qs_done, nth(i, 8, 4 * p + 3))
                wait_reuse(pool, vals_lo, i * 4 + (2 * p + h - 1))
                wait_reuse(pool, vals_hi, i * 4 + (2 * p + h - 1))
                nc.gpsimd.tensor_tensor(vals[:, h, :], qs[:, 2 * h, :], qs[:, 2 * h + 1, :],
                                        ALU.subtract if h else ALU.add).then_inc(vals_summed, 1)

            def remainder(i, p, h):
                pool.wait_ge(vals_hi, nth(i, 4, 2 * p + h))
                pool.wait_ge(vals_summed, nth(i, 4, 2 * p + h))
                nc.gpsimd.tensor_tensor(valsT[1][:, 2 * p + h, :], vals[:, h, :],
                                        valsT[0][:, 2 * p + h, :].bitcast(F32), ALU.subtract).then_inc(vals_lo, 1)

            def step(i, half, has_next, has_last):
                if has_last:
                    root(i - 1, 0)
                sum_vals(i, 0, 0)
                if has_last:
                    root(i - 1, 1)
                sum_vals(i, 0, 1)
                if has_last:
                    root(i - 1, 2)
                    root(i - 1, 3)
                remainder(i, 0, 0)
                remainder(i, 0, 1)
                sum_vals(i, 1, 0)
                sum_vals(i, 1, 1)
                remainder(i, 1, 0)
                remainder(i, 1, 1)

            steps(pool, step)
            for t in range(NT):
                root(B - 1, t)

        @block.vector
        def _(dve):
            def split_x(i, half, c):
                dve.wait_ge(x_hi, nth(i, NC, c))
                nc.vector.tensor_tensor(xT[half][1][:, c, :], xT_ps[:], xT[half][0][:, c, :].bitcast(F32),
                                        ALU.subtract).then_inc(x_lo, 1)

            def times_k(i, p, h):
                dve.wait_ge(k_filled, nth(i, 4, 2 * p + h))
                dve.wait_ge(v_copied, nth(i, 4, 2 * p + 1))
                wait_reuse(dve, scanned, i * 4 + 2 * p)
                if h == 0:
                    nc.vector.tensor_tensor(kv[:, 0, :], k_ps[0][:], v_sb[:, 0, :], ALU.mult).then_inc(kv_done, 1)
                    nc.vector.tensor_tensor(kv[:, 1, :], k_ps[0][:], v_sb[:, 1, :], ALU.mult).then_inc(kv_done, 1)
                else:
                    nc.vector.scalar_tensor_tensor(out=kv[:, 2, :], in0=k_ps[1][:], scalar=sigma[:], in1=v_sb[:, 1, :],
                                                   op0=ALU.mult, op1=ALU.mult).then_inc(kv_done, 1)
                    nc.vector.tensor_tensor(kv[:, 3, :], k_ps[1][:], v_sb[:, 0, :], ALU.mult).then_inc(kv_done, 1)

            def scan(i, p):
                dve.wait_ge(kv_done, nth(i, 8, 4 * p + 3))
                wait_reuse(dve, qs_done, i * 8 + 4 * p)
                nc.vector.tensor_tensor_scan(state[:, 0, :], kv[:, 0, :], kv[:, 2, :], 0.0, ALU.add,
                                             ALU.subtract).then_inc(scanned, 1)
                nc.vector.tensor_tensor_scan(state[:, 1, :], kv[:, 1, :], kv[:, 3, :], 0.0, ALU.add,
                                             ALU.add).then_inc(scanned, 1)

            def times_q(i, p, h):
                dve.wait_ge(q_filled, nth(i, 4, 2 * p + h))
                dve.wait_ge(scanned, nth(i, 4, 2 * p + 1))
                wait_reuse(dve, vals_summed, i * 4 + 2 * p)
                if h == 0:
                    nc.vector.tensor_tensor(qs[:, 0, :], q_ps[0][:], state[:, 0, :], ALU.mult).then_inc(qs_done, 1)
                    nc.vector.tensor_tensor(qs[:, 2, :], q_ps[0][:], state[:, 1, :], ALU.mult).then_inc(qs_done, 1)
                else:
                    nc.vector.tensor_tensor(qs[:, 1, :], q_ps[1][:], state[:, 1, :], ALU.mult).then_inc(qs_done, 1)
                    nc.vector.scalar_tensor_tensor(out=qs[:, 3, :], in0=q_ps[1][:], scalar=sigma[:], in1=state[:, 0, :],
                                                   op0=ALU.mult, op1=ALU.mult).then_inc(qs_done, 1)

            def add_residual(i, t):
                dve.wait_ge(out_filled, nth(i, NT, t))
                if t == 0:
                    dve.wait_ge(xres_loaded, nth(i, 1, 0) * 16)
                wait_reuse(dve, x1_ready, two_back(i, NT, t))
                k = t % 2
                nc.vector.tensor_tensor(r_sb[:, k, :], out_ps[:], x_res[:, t, :], ALU.add).then_inc(r_added, 1)
                dve.wait_ge(r_added, nth(i, NT, t))
                nc.vector.bn_stats(stats[:, k, :], r_sb[:, k, :]).then_inc(r_stats, 1)
                dve.wait_ge(r_stats, nth(i, NT, t))
                dve.sem_inc(stats_seen, 1)
                nc.vector.bn_aggr(mv[:, k, :], stats[:, k, :]).then_inc(r_aggr, 1)
                dve.wait_ge(r_aggr, nth(i, NT, t))
                wait_reuse(dve, rstd_ready, two_back(i, NT, t))
                nc.vector.tensor_scalar(ve[:, k:k + 1], mv[:, k, 1:2], EPS, None, ALU.add).then_inc(var_eps, 1)

            def normalize(i, t):
                dve.wait_ge(rstd_ready, nth(i, NT, t))
                wait_reuse(dve, x1_stored[t % 2], i * 32 + 16 * (t // 2))
                k = t % 2
                nc.vector.tensor_scalar(x1_sb[:, k, :], r_sb[:, k, :], mv[:, k, 0:1], rstd[:, k:k + 1],
                                        ALU.subtract, ALU.mult).then_inc(x1_ready, 1)

            def step(i, half, has_next, has_last):
                def turned(c):
                    if has_next:
                        split_x(i + 1, 1 - half, c)

                turned(0)
                times_k(i, 0, 0)
                turned(1)
                times_k(i, 0, 1)
                turned(2)
                scan(i, 0)
                turned(3)
                times_q(i, 0, 0)
                if has_last:
                    add_residual(i - 1, 0)
                times_q(i, 0, 1)
                if has_last:
                    add_residual(i - 1, 1)
                    normalize(i - 1, 0)
                    normalize(i - 1, 1)
                    add_residual(i - 1, 2)
                    add_residual(i - 1, 3)
                    normalize(i - 1, 2)
                    normalize(i - 1, 3)
                times_k(i, 1, 0)
                times_k(i, 1, 1)
                scan(i, 1)
                times_q(i, 1, 0)
                times_q(i, 1, 1)

            for c in range(NC):
                split_x(0, 0, c)
            steps(dve, step)
            for t in range(NT):
                add_residual(B - 1, t)
                normalize(B - 1, t)


def build_mixing(nc, x, w_qkv, w_out, dft_forward, dft_inverse, ident_dram, sign_dram, x1_dram):
    with ExitStack() as ctx:
        sb = lambda n, s, d=F32: ctx.enter_context(nc.sbuf_tensor(n, s, d))
        ident = sb("ident_a", [P, P])
        sigma = sb("sigma", [P, 1])
        half_power = sb("half_power_a", [P, 1])
        w_spec = [sb(f"w_spec_{k}", [P, NC, 3, D], F32R) for k in ("hi", "lo")]
        w_back = [sb(f"w_back_{k}", [P, NC, D], F32R) for k in ("hi", "lo")]
        load_constants(nc, ctx, [(ident, ident_dram), (sigma, sign_dram)], [(half_power, -0.5)], "a")
        prepare_mixing(nc, w_qkv, w_out, dft_forward, dft_inverse, ident, w_spec, w_back)
        mix_tokens(nc, x, x1_dram, ident, sigma, w_spec, w_back, half_power)


def load_constants(nc, ctx, loads, fills, tag):
    loaded = ctx.enter_context(nc.semaphore(f"constants_{tag}"))
    with nc.Block() as block:
        @block.sync
        def _(sp):
            for tile, src in loads:
                sp.dma_start(tile[:], src, allow_slow_non_contiguous=True).then_inc(loaded, 16)
            sp.wait_ge(loaded, 16 * len(loads))

        @block.gpsimd
        def _(pool):
            for tile, value in fills:
                nc.gpsimd.memset(tile[:], value)



def prepare_attention(nc, ins, ident, w_q, w_o, w_ffn, k_dram, v_dram, bias_v):
    rows = B * KEYS
    half_rows = rows // 2
    tiles = [(n * P, min(P, rows - n * P)) for n in range((rows + P - 1) // P)]
    with ExitStack() as ctx:
        sb = lambda n, s, d=F32: ctx.enter_context(nc.sbuf_tensor(n, s, d))
        ps = lambda n, s: ctx.enter_context(nc.psum_tensor(n, s, F32))
        sem = lambda n: ctx.enter_context(nc.semaphore(n))
        raw_q, raw_o = sb("raw_q", [P, NC, D]), sb("raw_o", [P, NC, D])
        raw_k, raw_v, raw_f = sb("raw_k", [P, NC, D]), sb("raw_v", [P, NC, D]), sb("raw_f", [P, NC, D])
        ctx_sb = sb("ctx_sb", [P, len(tiles), D])
        ctxT = sb("ctxT", [P, NC, rows])
        a_sb, b_sb, aT = sb("a_sb", [P, NC, RANK]), sb("b_sb", [RANK, D]), sb("aT", [RANK, D])
        bias_k = sb("bias_k", [P, NC])
        k_val = sb("k_val", [P, 2, half_rows])
        k_hi, k_lo = sb("k_hi", [P, 2, half_rows], F32R), sb("k_lo", [P, 2, half_rows], F32R)
        v_hi, v_lo = sb("v_hi", [P, 2, D], F32R), sb("v_lo", [P, 2, D], F32R)
        top, top_all = sb("top", [P, 1]), sb("top_all", [P, 1])
        scale, per_scale = sb("q_scale", [P, 1]), sb("q_per_scale", [P, 1])
        quant = sb("quant", [P, NC, D])
        merged = sb("merged", [P, 2, D])
        turned = [ps(f"turned_b{n}", [P, NC * P]) for n in range(2)]
        prod = [ps(f"prod_b{n}", [P, D]) for n in range(2)]
        ctx_loaded, kv_loaded, qo_loaded, ffn_loaded = sem("ctx_loaded"), sem("kv_loaded"), sem("qo_loaded"), sem("ffn_loaded")
        turned_ready, turned_copied = sem("turned_b"), sem("turned_b_copied")
        prod_ready, prod_used = sem("prod_b"), sem("prod_b_used")
        k_biased, k_hi_ready, k_lo_ready = sem("k_biased"), sem("k_hi_ready"), sem("k_lo_ready")
        v_hi_ready, v_lo_ready = sem("v_hi_ready"), sem("v_lo_ready")
        stored = [sem(f"kv_stored{n}") for n in range(2)]
        w_hi_ready = sem("w_hi_ready")
        top_ready, top_spread, scale_ready, per_ready = sem("top_ready"), sem("top_spread"), sem("scale_ready"), sem("per_ready")
        quantized, merged_ready, merged_hi, merged_lo = sem("quantized"), sem("merged_ready"), sem("merged_hi"), sem("merged_lo")
        block = ctx.enter_context(nc.Block())
        NTURN = NC + 1
        NKEY = 2 * NC
        NVAL = len(tiles)
        by_chunk = lambda w: w.rearrange("(c p) n -> p c n", p=P)

        @block.sync
        def _(sp):
            flat = ins["ctx"].rearrange("b k d -> (b k) d")
            for n, (at, size) in enumerate(tiles):
                sp.dma_start(ctx_sb[0:size, n, :], flat[at:at + size, :]).then_inc(ctx_loaded, 16)
            sp.dma_start(raw_k[:], by_chunk(ins["W_k"])).then_inc(kv_loaded, 16)
            sp.dma_start(bias_k[:], ins["b_k"].rearrange("(c p) -> p c", p=P),
                         allow_slow_non_contiguous=True).then_inc(kv_loaded, 16)
            sp.dma_start(raw_v[:], by_chunk(ins["W_v"])).then_inc(kv_loaded, 16)
            sp.dma_start(raw_f[:], by_chunk(ins["kernel"])).then_inc(ffn_loaded, 16)
            sp.dma_start(a_sb[:], by_chunk(ins["a"])).then_inc(ffn_loaded, 16)
            sp.dma_start(b_sb[:], ins["b"]).then_inc(ffn_loaded, 16)
            sp.dma_start(raw_q[:], by_chunk(ins["W_q"])).then_inc(qo_loaded, 16)
            sp.dma_start(raw_o[:], by_chunk(ins["W_o"])).then_inc(qo_loaded, 16)
            for n in range(NKEY):
                c, h = n // 2, n % 2
                sp.wait_ge(k_lo_ready, n + 1)
                for part, tile in enumerate((k_hi, k_lo)):
                    sp.dma_start(k_dram[part, c * P:(c + 1) * P, h * half_rows:(h + 1) * half_rows],
                                 tile[:, n % 2, :].bitcast(F32)).then_inc(stored[n % 2], 16)
            for n, (at, size) in enumerate(tiles):
                sp.wait_ge(v_lo_ready, n + 1)
                for part, tile in enumerate((v_hi, v_lo)):
                    sp.dma_start(v_dram[part, at:at + size, :], tile[0:size, n % 2, :].bitcast(F32)).then_inc(stored[n % 2], 16)
            for n in range(2):
                sp.wait_ge(stored[n], 32 * (NKEY // 2 + len(range(n, NVAL, 2))))

        @block.tensor
        def _(pe):
            pe.wait_ge(ctx_loaded, 16 * len(tiles))
            for c in range(NC):
                wait_reuse(pe, turned_copied, 2 * (c - 1))
                for n, (at, size) in enumerate(tiles[:NC]):
                    last = nc.tensor.transpose(turned[c % 2][:, n * P:n * P + size], ctx_sb[0:size, n, c * P:(c + 1) * P],
                                               ident[0:size, 0:size])
                last.then_inc(turned_ready, 1)
                at, size = tiles[NC]
                nc.tensor.transpose(prod[c % 2][:, 0:size], ctx_sb[0:size, NC, c * P:(c + 1) * P],
                                    ident[0:size, 0:size]).then_inc(turned_ready, 1)
            pe.wait_ge(ffn_loaded, 48)
            pe.wait_ge(turned_copied, 2 * (NC - 1))
            for c in range(NC):
                last = nc.tensor.transpose(turned[0][0:RANK, c * P:(c + 1) * P], a_sb[:, c, :], ident[:])
            last.then_inc(turned_ready, 1)
            pe.wait_ge(kv_loaded, 48)
            pe.wait_ge(turned_copied, 2 * NC)
            for n in range(NKEY):
                c, h = n // 2, n % 2
                wait_reuse(pe, prod_used, n - 1)
                for k in range(NC):
                    last = nc.tensor.matmul(prod[n % 2][:, 0:half_rows], raw_k[:, k, c * P:(c + 1) * P],
                                            ctxT[:, k, h * half_rows:(h + 1) * half_rows], start=(k == 0), stop=(k == NC - 1))
                last.then_inc(prod_ready, 1)
            for m, (at, size) in enumerate(tiles):
                n = NKEY + m
                pe.wait_ge(prod_used, n - 1)
                for k in range(NC):
                    last = nc.tensor.matmul(prod[n % 2][0:size, :], ctxT[:, k, at:at + size], raw_v[:, k, :],
                                            start=(k == 0), stop=(k == NC - 1))
                last.then_inc(prod_ready, 1)
            pe.wait_ge(turned_copied, 2 * NC + 1)
            for c in range(NC):
                n = NKEY + NVAL + c
                pe.wait_ge(prod_used, n - 1)
                nc.tensor.matmul(prod[n % 2][:], aT[:, c * P:(c + 1) * P], b_sb[:], start=True, stop=True).then_inc(prod_ready, 1)

        @block.scalar
        def _(act):
            at, size = tiles[NC]
            for c in range(NC):
                act.wait_ge(turned_ready, 2 * c + 1)
                nc.scalar.activation(ctxT[:, c, 0:at], turned[c % 2][:], ACT.Copy).then_inc(turned_copied, 1)
                act.wait_ge(turned_ready, 2 * c + 2)
                nc.scalar.activation(ctxT[:, c, at:rows], prod[c % 2][:, 0:size], ACT.Copy).then_inc(turned_copied, 1)
            act.wait_ge(turned_ready, 2 * NC + 1)
            nc.scalar.activation(aT[:], turned[0][0:RANK, :], ACT.Copy).then_inc(turned_copied, 1)
            for n in range(NKEY):
                act.wait_ge(k_biased, n + 1)
                wait_reuse(act, stored[n % 2], 32 * (n // 2))
                nc.scalar.activation(k_hi[:, n % 2, :], k_val[:, n % 2, :], ACT.Copy).then_inc(k_hi_ready, 1)
            for m, (at, size) in enumerate(tiles):
                act.wait_ge(prod_ready, NKEY + m + 1)
                if m >= 2:
                    act.wait_ge(stored[m % 2], 32 * (NKEY // 2 + m // 2))
                nc.scalar.activation(v_hi[0:size, m % 2, :], prod[(NKEY + m) % 2][0:size, :], ACT.Copy).then_inc(v_hi_ready, 1)
            act.wait_ge(qo_loaded, 32)
            nc.scalar.activation(w_q[0][:], raw_q[:], ACT.Copy).then_inc(w_hi_ready, 1)
            nc.scalar.activation(w_o[0][:], raw_o[:], ACT.Copy).then_inc(w_hi_ready, 1)
            for c in range(NC):
                act.wait_ge(merged_ready, c + 1)
                nc.scalar.activation(w_ffn[0][:, c, :], merged[:, c % 2, :], ACT.Copy).then_inc(merged_hi, 1)

        @block.gpsimd
        def _(pool):
            pool.wait_ge(top_ready, 1)
            nc.gpsimd.partition_all_reduce(top_all[:], top[:], P, bass.bass_isa.ReduceOp.max).then_inc(top_spread, 1)
            for n, (w, raw) in enumerate(((w_q, raw_q), (w_o, raw_o))):
                pool.wait_ge(w_hi_ready, n + 1)
                pool.wait_ge(qo_loaded, 32)
                for c in range(NC):
                    last = nc.gpsimd.tensor_tensor(w[1][:, c, :], raw[:, c, :], w[0][:, c, :].bitcast(F32), ALU.subtract)

        @block.vector
        def _(dve):
            dve.wait_ge(ffn_loaded, 48)
            nc.vector.tensor_reduce(top[:], raw_f[:].rearrange("p c n -> p (c n)"), AX.X, ALU.max,
                                    apply_absolute_value=True).then_inc(top_ready, 1)
            for n in range(NKEY):
                c = n // 2
                dve.wait_ge(prod_ready, n + 1)
                if n == 0:
                    dve.wait_ge(kv_loaded, 48)
                wait_reuse(dve, k_lo_ready, n - 1)
                nc.vector.tensor_scalar(k_val[:, n % 2, :], prod[n % 2][:, 0:half_rows], bias_k[:, c:c + 1],
                                        float(XHD) ** -0.5, ALU.add, ALU.mult).then_inc(k_biased, 1)
                dve.wait_ge(k_biased, n + 1)
                dve.sem_inc(prod_used, 1)
                dve.wait_ge(k_hi_ready, n + 1)
                nc.vector.tensor_tensor(k_lo[:, n % 2, :], k_val[:, n % 2, :], k_hi[:, n % 2, :].bitcast(F32),
                                        ALU.subtract).then_inc(k_lo_ready, 1)
            for m, (at, size) in enumerate(tiles):
                dve.wait_ge(v_hi_ready, m + 1)
                nc.vector.tensor_tensor(v_lo[0:size, m % 2, :], prod[(NKEY + m) % 2][0:size, :],
                                        v_hi[0:size, m % 2, :].bitcast(F32), ALU.subtract).then_inc(v_lo_ready, 1)
                dve.wait_ge(v_lo_ready, m + 1)
                dve.sem_inc(prod_used, 1)
            dve.wait_ge(top_spread, 1)
            nc.vector.tensor_scalar(scale[:], top_all[:], 1.0 / QMAX, None, ALU.mult).then_inc(scale_ready, 1)
            dve.wait_ge(scale_ready, 1)
            nc.vector.reciprocal(per_scale[:], scale[:]).then_inc(per_ready, 1)
            dve.wait_ge(per_ready, 1)
            nc.vector.tensor_scalar(quant[:], raw_f[:], per_scale[:], ROUND_MAGIC, ALU.mult, ALU.add).then_inc(quantized, 1)
            dve.wait_ge(quantized, 1)
            nc.vector.tensor_scalar(quant[:], quant[:], ROUND_MAGIC, -QMAX - 1, ALU.subtract, ALU.max).then_inc(quantized, 1)
            dve.wait_ge(quantized, 2)
            nc.vector.tensor_scalar(quant[:], quant[:], QMAX, scale[:], ALU.min, ALU.mult).then_inc(quantized, 1)
            dve.wait_ge(quantized, 3)
            for c in range(NC):
                n = NKEY + NVAL + c
                dve.wait_ge(prod_ready, n + 1)
                wait_reuse(dve, merged_lo, c - 1)
                nc.vector.tensor_tensor(merged[:, c % 2, :], prod[n % 2][:], quant[:, c, :], ALU.add).then_inc(merged_ready, 1)
                dve.wait_ge(merged_ready, c + 1)
                dve.sem_inc(prod_used, 1)
                dve.wait_ge(merged_hi, c + 1)
                nc.vector.tensor_tensor(w_ffn[1][:, c, :], merged[:, c % 2, :], w_ffn[0][:, c, :].bitcast(F32),
                                        ALU.subtract).then_inc(merged_lo, 1)


FRONT, BACK = "XQV", "OTF"
BANK_ORDER = ["X0", "X1", "X2", "X3", "O0", "Q0", "Q1", "Q2", "Q3", "O1", "T0", "O2", "F0", "T1",
              "O3", "F1", "T2", "F2", "T3", "F3", "V0", "V1", "V2", "V3"]


class Shared:

    def __init__(self, i, front, back):
        kinds = (FRONT if front else "") + (BACK if back else "")
        order = [u for u in BANK_ORDER if u[0] in kinds]
        self.at = {u: n for n, u in enumerate(order)}
        self.before = 0 if isinstance(i, int) and i == 0 else i * len(BANK_ORDER) - len(BANK_ORDER) // 2

    def bank(self, use):
        return self.at[use] % 2

    def filled(self, use):
        return self.before + (self.at[use] + 1)

    def freed(self, use):
        return self.before + (self.at[use] - 1)


def attend(nc, ins, out, x1_dram, k_dram, v_dram, ident, half_power, w_q, w_o, w_ffn, bias_q, bias_v, bias_o, bias_f):
    with ExitStack() as ctx:
        sb = lambda n, s, d=F32: ctx.enter_context(nc.sbuf_tensor(n, s, d))
        ps = lambda n, s: ctx.enter_context(nc.psum_tensor(n, s, F32))
        sem = lambda n: ctx.enter_context(nc.semaphore(n))
        pair = lambda n, s: [sb(f"{n}_hi", s, F32R), sb(f"{n}_lo", s, F32R)]
        x1 = sb("x1", [P, NT, D])
        mask = sb("mask", [P, NT, KEYS], I32)
        hidden = sb("hidden", [P, NT, KEYS], I32)
        masked = sb("masked", [P, KEYS])
        k_block, v_block = pair("k_block", [P, GROUPS, GK]), pair("v_block", [KC[0][1], len(KC), GROUPS, P])
        qT, oT = pair("qT", [P, NC, S]), pair("oT", [P, NC, S])
        x2T = pair("x2T", [P, NC, P])
        pT = pair("pT", [P, len(KC), GROUPS, S])
        x1T = [p[:, len(KC) - 1, :, :] for p in pT]
        probs = sb("probs", [P, 2, XH * KEYS])
        top, total, per_total = sb("top_s", [P, 2, XH]), sb("total", [P, 2, XH]), sb("per_total", [P, 2, XH])
        res1 = sb("res1", [P, NT, D])
        y, x2, res2, y_out = sb("y", [P, 2, D]), sb("x2", [P, 2, D]), sb("res2", [P, 2, D]), sb("y_out", [P, 2, D])
        stats, mv = sb("stats", [P, 2, 6]), sb("mv", [P, 2, 2])
        ve, rstd = sb("ve", [P, 2]), sb("rstd", [P, 2])
        score_ps = ps("score_ps", [P, GROUPS, 512])
        turn_ps = [ps(f"turn_ps{n}", [P, GROUPS, P]) for n in range(2)]
        shared_ps = [ps(f"shared_ps{n}", [P, 512]) for n in range(2)]

        blocks_cleared, masked_set = sem("blocks_cleared"), sem("masked_set")
        x1_loaded, mask_loaded, k_loaded, v_loaded = sem("x1_loaded"), sem("mask_loaded"), sem("k_loaded"), sem("v_loaded")
        hidden_ready, res1_ready, res2_ready = sem("hidden_ready"), sem("res1_ready"), sem("res2_ready")
        filled, freed = sem("shared_filled"), sem("shared_freed")
        x1T_hi, q_hi, oT_hi, x2T_hi = sem("x1T_hi_ready"), sem("q_hi_ready"), sem("oT_hi_ready"), sem("x2T_hi_ready")
        scored, hid, topped, exped, totalled, normed = (sem("scored"), sem("hid"), sem("topped"), sem("exped"),
                                                       sem("per_total_ready"), sem("normed"))
        turned, turned_hi, turned_lo = sem("turned_p"), sem("pT_hi_ready"), sem("pT_lo_ready")
        added, stat_done, stat_seen, aggr_done = sem("y_added"), sem("stat_done"), sem("stat_seen"), sem("aggr_done")
        var_eps, rstd_ready, x2_ready, y_ready = sem("var_eps_b"), sem("rstd_b"), sem("x2_ready"), sem("y_ready")
        y_stored = [sem(f"y_stored{n}") for n in range(2)]
        block = ctx.enter_context(nc.Block())

        def steps(eng, step):
            step(0, True, False)
            with eng.Fori(1, B) as i:
                step(i, True, True)
            step(B, False, True)

        LN = ["O0", "O1", "O2", "F0", "O3", "F1", "F2", "F3"]

        def ln_count(i, use):
            return nth(i - 1, len(LN), LN.index(use))

        @block.sync
        def _(sp):
            def load_mask(i):
                wait_reuse(sp, hidden_ready, i)
                sp.dma_start(mask[:], ins["mask"][i].rearrange("(t p) k -> p t k", p=P)).then_inc(mask_loaded, 16)

            def load_x1(i):
                wait_reuse(sp, res1_ready, i * NT)
                wait_reuse(sp, x1T_hi, i * NC)
                sp.dma_start(x1[:], x1_dram[i].rearrange("(t p) d -> p t d", p=P)).then_inc(x1_loaded, 16)

            def load_keys(i):
                wait_reuse(sp, scored, i * NT * 2)
                for part in range(2):
                    src = k_dram[part].rearrange("(g j d) r -> j d g r", j=GH, d=XHD)
                    for j in range(GH):
                        sp.dma_start(k_block[part][j * XHD:(j + 1) * XHD, :, j * KEYS:(j + 1) * KEYS].bitcast(F32),
                                     src[j][:, :, bass.ds(i * KEYS, KEYS)]).then_inc(k_loaded, 16)

            def load_values(i):
                wait_reuse(sp, oT_hi, i * NC)
                for part in range(2):
                    src = v_dram[part].rearrange("r (g j d) -> r g j d", g=GROUPS, j=GH)
                    for j, c, row, key, n in v_pieces():
                        sp.dma_start(v_block[part][row:row + n, c, :, j * XHD:(j + 1) * XHD].bitcast(F32),
                                     src[bass.ds(i * KEYS + key, n)][:, :, j, :]).then_inc(v_loaded, 16)

            def store(i, t):
                sp.wait_ge(y_ready, nth(i, NT, t))
                sp.dma_start(out[i, t * P:(t + 1) * P, :], y_out[:, t % 2, :]).then_inc(y_stored[t % 2], 16)

            load_mask(0)
            load_x1(0)
            sp.wait_ge(blocks_cleared, 4)
            load_keys(0)
            load_values(0)

            def step(i, load, back):
                if load:
                    load_mask(i + 1)
                if back:
                    store(i - 1, 0)
                if load:
                    load_x1(i + 1)
                if back:
                    store(i - 1, 1)
                if load:
                    load_keys(i + 1)
                if back:
                    store(i - 1, 2)
                    store(i - 1, 3)
                if load:
                    load_values(i + 1)

            step(0, True, False)
            with sp.Fori(1, B - 1) as i:
                step(i, True, True)
            step(B - 1, False, True)
            step(B, False, True)
            for n in range(2):
                sp.wait_ge(y_stored[n], 16 * B * NT // 2)

        @block.tensor
        def _(pe):
            def turn_x1(i, s, c):
                if c == 0:
                    pe.wait_ge(x1_loaded, nth(i, 1, 0) * 16)
                use = f"X{c}"
                wait_reuse(pe, freed, s.freed(use))
                for t in range(NT):
                    last = nc.tensor.transpose(shared_ps[s.bank(use)][:, t * P:(t + 1) * P],
                                               x1[:, t, c * P:(c + 1) * P], ident[:])
                last.then_inc(filled, 1)

            def project_q(i, s, c):
                use = f"Q{c}"
                if c == 0:
                    pe.wait_ge(x1T_hi, nth(i, NC, NC - 1))
                    pe.wait_ge(freed, s.filled("X3"))
                wait_reuse(pe, freed, s.freed(use))
                pieces = [([w[:, k, c * P:(c + 1) * P] for w in w_q], [x[:, k, :] for x in x1T]) for k in range(NC)]
                split_matmuls(nc, shared_ps[s.bank(use)][:], pieces).then_inc(filled, 1)

            def score(i, s, t, h):
                if t == 0 and h == 0:
                    pe.wait_ge(k_loaded, nth(i, 1, 0) * (16 * 2 * GH))
                    pe.wait_ge(q_hi, nth(i, NC, NC - 1))
                    pe.wait_ge(freed, s.filled("Q3"))
                wait_reuse(pe, exped, i * (NT * XH) + ((t - 1) * XH + (h + 1) * XH // 2))
                tok = slice(t * P, (t + 1) * P)
                for g in (2 * h, 2 * h + 1):
                    last = split_matmuls(nc, score_ps[:, g, 0:GK],
                                         [([q[:, g, tok] for q in qT], [k[:, g, :] for k in k_block])])
                last.then_inc(scored, 1)

            def turn_probs(i, t, c):
                if c == 0:
                    pe.wait_ge(normed, nth(i, NT * 2, 2 * t + 1))
                wait_reuse(pe, turned_lo, i * NT * 3 + (t * 3 + c - 1))
                at, size = KC[c]
                n = (t * 3 + c) % 2
                for g in range(GROUPS):
                    last = nc.tensor.transpose(turn_ps[n][0:size, g, :],
                                               probs[:, t % 2, g * GK + at:g * GK + at + size], ident[:])
                last.then_inc(turned, 1)

            def weigh_values(i, s, g):
                use = f"V{g}"
                if g == 0:
                    pe.wait_ge(v_loaded, nth(i, 1, 0) * (16 * 2 * len(list(v_pieces()))))
                    pe.wait_ge(turned_lo, nth(i, NT * 3, NT * 3 - 1))
                    pe.wait_ge(turned_hi, nth(i, NT * 3, NT * 3 - 1))
                wait_reuse(pe, freed, s.freed(use))
                pieces = [([v[0:size, c, g, :] for v in v_block], [p[0:size, c, g, :] for p in pT])
                          for c, (_, size) in enumerate(KC)]
                split_matmuls(nc, shared_ps[s.bank(use)][:], pieces).then_inc(filled, 1)

            def project_o(i, s, t):
                use = f"O{t}"
                if t == 0:
                    pe.wait_ge(oT_hi, nth(i - 1, NC, NC - 1))
                    pe.wait_ge(freed, s.before)
                wait_reuse(pe, freed, s.freed(use))
                tok = slice(t * P, (t + 1) * P)
                pieces = [([o[:, k, tok] for o in oT], [w[:, k, :] for w in w_o]) for k in range(NC)]
                split_matmuls(nc, shared_ps[s.bank(use)][:], pieces).then_inc(filled, 1)

            def turn_x2(i, s, t):
                use = f"T{t}"
                pe.wait_ge(x2_ready, nth(i - 1, NT, t))
                wait_reuse(pe, freed, s.freed(use))
                for c in range(NC):
                    last = nc.tensor.transpose(shared_ps[s.bank(use)][:, c * P:(c + 1) * P],
                                               x2[:, t % 2, c * P:(c + 1) * P], ident[:])
                last.then_inc(filled, 1)

            def project_f(i, s, t):
                use = f"F{t}"
                pe.wait_ge(x2T_hi, nth(i - 1, NT, t))
                pe.wait_ge(freed, s.filled(f"T{t}"))
                wait_reuse(pe, freed, s.freed(use))
                pieces = [([x[:, k, :] for x in x2T], [w[:, k, :] for w in w_ffn]) for k in range(NC)]
                split_matmuls(nc, shared_ps[s.bank(use)][:], pieces).then_inc(filled, 1)

            def step(i, front, back):
                s = Shared(i, front, back)
                if front:
                    for c in range(NC):
                        turn_x1(i, s, c)
                if back:
                    project_o(i, s, 0)
                if front:
                    for c in range(NC):
                        project_q(i, s, c)
                    score(i, s, 0, 0)
                    score(i, s, 0, 1)
                if back:
                    project_o(i, s, 1)
                    turn_x2(i, s, 0)
                if front:
                    score(i, s, 1, 0)
                    score(i, s, 1, 1)
                if back:
                    project_o(i, s, 2)
                    project_f(i, s, 0)
                    turn_x2(i, s, 1)
                if front:
                    for c in range(3):
                        turn_probs(i, 0, c)
                    score(i, s, 2, 0)
                    score(i, s, 2, 1)
                if back:
                    project_o(i, s, 3)
                    project_f(i, s, 1)
                    turn_x2(i, s, 2)
                if front:
                    for c in range(3):
                        turn_probs(i, 1, c)
                    score(i, s, 3, 0)
                    score(i, s, 3, 1)
                if back:
                    project_f(i, s, 2)
                    turn_x2(i, s, 3)
                if front:
                    for c in range(3):
                        turn_probs(i, 2, c)
                if back:
                    project_f(i, s, 3)
                if front:
                    for c in range(3):
                        turn_probs(i, 3, c)
                    for g in range(GROUPS):
                        weigh_values(i, s, g)

            steps(pe, step)

        @block.scalar
        def _(act):
            def split_x1(i, s, c):
                use = f"X{c}"
                act.wait_ge(filled, s.filled(use))
                nc.scalar.activation(x1T[0][:, c, :], shared_ps[s.bank(use)][:], ACT.Copy).then_inc(x1T_hi, 1)

            def split_q(i, s, c):
                use = f"Q{c}"
                act.wait_ge(filled, s.filled(use))
                nc.scalar.activation(qT[0][:, c, :], shared_ps[s.bank(use)][:], ACT.Identity,
                                     bias=bias_q[:, c:c + 1]).then_inc(q_hi, 1)

            def exponentials(i, t):
                for j in range(XH):
                    if j % (XH // 2) == 0:
                        act.wait_ge(topped, nth(i, NT * 2, 2 * t + j // (XH // 2)))
                    if j == 0:
                        wait_reuse(act, turned, i * NT * 3 + (3 * (t - 1)))
                        wait_reuse(act, totalled, i * NT + (t - 1))
                    g, h = j // GH, j % GH
                    nc.scalar.activation(probs[:, t % 2, j * KEYS:(j + 1) * KEYS],
                                         score_ps[:, g, h * KEYS:(h + 1) * KEYS], ACT.Exp, bias=top[:, t % 2, j:j + 1],
                                         accum_out=total[:, t % 2, j:j + 1]).then_inc(exped, 1)

            def split_probs(i, t, c):
                act.wait_ge(turned, nth(i, NT * 3, 3 * t + c))
                size = KC[c][1]
                nc.scalar.activation(pT[0][0:size, c, :, t * P:(t + 1) * P], turn_ps[(t * 3 + c) % 2][0:size, :, :],
                                     ACT.Copy).then_inc(turned_hi, 1)

            def split_o(i, s, g):
                use = f"V{g}"
                act.wait_ge(filled, s.filled(use))
                nc.scalar.activation(oT[0][:, g, :], shared_ps[s.bank(use)][:], ACT.Identity,
                                     bias=bias_v[:, g:g + 1]).then_inc(oT_hi, 1)

            def split_x2(i, s, t):
                use = f"T{t}"
                act.wait_ge(filled, s.filled(use))
                nc.scalar.activation(x2T[0][:], shared_ps[s.bank(use)][:].rearrange("p (c n) -> p c n", c=NC),
                                     ACT.Copy).then_inc(x2T_hi, 1)

            def step(i, front, back):
                s = Shared(i, front, back)
                if front:
                    for c in range(NC):
                        split_x1(i, s, c)
                    for c in range(NC):
                        split_q(i, s, c)
                    exponentials(i, 0)
                if back:
                    split_x2(i, s, 0)
                if front:
                    exponentials(i, 1)
                if back:
                    split_x2(i, s, 1)
                if front:
                    for c in range(3):
                        split_probs(i, 0, c)
                    exponentials(i, 2)
                if back:
                    split_x2(i, s, 2)
                if front:
                    for c in range(3):
                        split_probs(i, 1, c)
                    exponentials(i, 3)
                if back:
                    split_x2(i, s, 3)
                if front:
                    for t in (2, 3):
                        for c in range(3):
                            split_probs(i, t, c)
                    for g in range(GROUPS):
                        split_o(i, s, g)

            steps(act, step)

        @block.gpsimd
        def _(pool):
            def root(i, use):
                n = LN.index(use) % 2
                pool.wait_ge(var_eps, ln_count(i, use))
                nc.gpsimd.tensor_tensor(rstd[:, n:n + 1], ve[:, n:n + 1], half_power[:], ALU.pow).then_inc(rstd_ready, 1)

            def normalize_probs(i, t, h):
                pool.wait_ge(totalled, nth(i, NT, t))
                pool.wait_ge(exped, nth(i, NT * XH, t * XH + XH - 1))
                heads = XH // 2
                p = probs[:, t % 2, h * heads * KEYS:(h + 1) * heads * KEYS].rearrange("p (j k) -> p j k", j=heads)
                nc.gpsimd.tensor_tensor(p, p, per_total[:, t % 2, h * heads:(h + 1) * heads].unsqueeze(2)
                                        .to_broadcast([P, heads, KEYS]), ALU.mult).then_inc(normed, 1)

            def bias_residual(i, t, back):
                if t == 0:
                    pool.wait_ge(x1_loaded, nth(i, 1, 0) * 16)
                if back:
                    pool.wait_ge(added, ln_count(i, f"O{t}"))
                nc.gpsimd.tensor_tensor(res1[:, t, :], x1[:, t, :], bias_o[:], ALU.add).then_inc(res1_ready, 1)

            def bias_x2(i, t):
                pool.wait_ge(x2_ready, nth(i - 1, NT, t))
                if t >= 2:
                    pool.wait_ge(added, ln_count(i, f"F{t - 2}"))
                nc.gpsimd.tensor_tensor(res2[:, t % 2, :], x2[:, t % 2, :], bias_f[:], ALU.add).then_inc(res2_ready, 1)

            def step(i, front, back):
                if back:
                    root(i, "O0")
                    bias_x2(i, 0)
                if front:
                    bias_residual(i, 0, back)
                if back:
                    root(i, "O1")
                    bias_x2(i, 1)
                if front:
                    normalize_probs(i, 0, 0)
                    normalize_probs(i, 0, 1)
                    bias_residual(i, 1, back)
                if back:
                    root(i, "O2")
                    root(i, "F0")
                    bias_x2(i, 2)
                if front:
                    normalize_probs(i, 1, 0)
                    normalize_probs(i, 1, 1)
                    bias_residual(i, 2, back)
                if back:
                    root(i, "O3")
                    root(i, "F1")
                    bias_x2(i, 3)
                if front:
                    bias_residual(i, 3, back)
                    normalize_probs(i, 2, 0)
                    normalize_probs(i, 2, 1)
                if back:
                    root(i, "F2")
                    root(i, "F3")
                if front:
                    normalize_probs(i, 3, 0)
                    normalize_probs(i, 3, 1)

            steps(pool, step)

        @block.vector
        def _(dve):
            nc.vector.memset(masked[:], MASKED).then_inc(masked_set, 1)
            for tile in (*k_block, *v_block):
                nc.vector.memset(tile[:].bitcast(F32), 0.0).then_inc(blocks_cleared, 1)
            dve.wait_ge(masked_set, 1)

            def remainder(s, use, hi_ready, count, hi, lo, psum):
                dve.wait_ge(hi_ready, count)
                nc.vector.tensor_tensor(lo, psum, hi.bitcast(F32), ALU.subtract).then_inc(freed, 1)

            def split_x1(i, s, c):
                remainder(s, f"X{c}", x1T_hi, nth(i, NC, c), x1T[0][:, c, :], x1T[1][:, c, :],
                          shared_ps[s.bank(f"X{c}")][:])

            def biased_remainder(hi_ready, count, hi, lo, psum, bias):
                dve.wait_ge(hi_ready, count)
                nc.vector.scalar_tensor_tensor(out=lo, in0=psum, scalar=bias, in1=hi.bitcast(F32), op0=ALU.add,
                                               op1=ALU.subtract).then_inc(freed, 1)

            def split_q(i, s, c):
                biased_remainder(q_hi, nth(i, NC, c), qT[0][:, c, :], qT[1][:, c, :], shared_ps[s.bank(f"Q{c}")][:],
                                 bias_q[:, c:c + 1])

            def split_o(i, s, g):
                biased_remainder(oT_hi, nth(i, NC, g), oT[0][:, g, :], oT[1][:, g, :], shared_ps[s.bank(f"V{g}")][:],
                                 bias_v[:, g:g + 1])

            def split_x2(i, s, t):
                remainder(s, f"T{t}", x2T_hi, nth(i - 1, NT, t), x2T[0][:], x2T[1][:],
                          shared_ps[s.bank(f"T{t}")][:].rearrange("p (c n) -> p c n", c=NC))

            def split_probs(i, t, c):
                size = KC[c][1]
                dve.wait_ge(turned_hi, nth(i, NT * 3, 3 * t + c))
                tok = slice(t * P, (t + 1) * P)
                nc.vector.tensor_tensor(pT[1][0:size, c, :, tok], turn_ps[(t * 3 + c) % 2][0:size, :, :],
                                        pT[0][0:size, c, :, tok].bitcast(F32), ALU.subtract).then_inc(turned_lo, 1)

            def find_hidden(i):
                dve.wait_ge(mask_loaded, nth(i, 1, 0) * 16)
                wait_reuse(dve, hid, i * NT * 2)
                nc.vector.tensor_scalar(hidden[:], mask[:], 0.0, None, ALU.is_equal).then_inc(hidden_ready, 1)

            def softmax_top(i, t, h):
                dve.wait_ge(scored, nth(i, NT * 2, 2 * t + h))
                dve.wait_ge(hidden_ready, nth(i, 1, 0))
                dve.sem_inc(stat_seen, 1)
                shape = [P, GROUPS // 2, GH, KEYS]
                s4 = score_ps[:, 2 * h:2 * h + 2, 0:GK].rearrange("p g (j k) -> p g j k", j=GH)
                nc.vector.copy_predicated(s4, hidden[:, t, :].unsqueeze(1).unsqueeze(1).to_broadcast(shape),
                                          masked[:].unsqueeze(1).unsqueeze(1).to_broadcast(shape)).then_inc(hid, 1)
                dve.wait_ge(hid, nth(i, NT * 2, 2 * t + h))
                wait_reuse(dve, exped, i * NT * XH + (t - 1) * XH)
                nc.vector.tensor_reduce(top[:, t % 2, h * 8:(h + 1) * 8].rearrange("p (g j) -> p g j", j=GH), s4, AX.X,
                                        ALU.max, negate=True).then_inc(topped, 1)

            def invert_totals(i, t):
                dve.wait_ge(exped, nth(i, NT * XH, t * XH + XH - 1))
                wait_reuse(dve, normed, i * NT * 2 + 2 * (t - 1))
                nc.vector.reciprocal(per_total[:, t % 2, :], total[:, t % 2, :]).then_inc(totalled, 1)

            def add(i, s, use, residual, res_ready, res_count):
                n = LN.index(use) % 2
                dve.wait_ge(filled, s.filled(use))
                dve.wait_ge(res_ready, res_count)
                if LN.index(use) < 2:
                    wait_reuse(dve, y_ready, (i - 1) * NT)
                else:
                    before = LN[LN.index(use) - 2]
                    dve.wait_ge(x2_ready if before[0] == "O" else y_ready, nth(i - 1, NT, int(before[1])))
                nc.vector.tensor_tensor(y[:, n, :], shared_ps[s.bank(use)][:], residual, ALU.add).then_inc(added, 1)
                dve.wait_ge(added, ln_count(i, use))
                dve.sem_inc(freed, 1)
                nc.vector.bn_stats(stats[:, n, :], y[:, n, :]).then_inc(stat_done, 1)
                dve.wait_ge(stat_done, ln_count(i, use))
                dve.sem_inc(stat_seen, 1)
                nc.vector.bn_aggr(mv[:, n, :], stats[:, n, :]).then_inc(aggr_done, 1)
                dve.wait_ge(aggr_done, ln_count(i, use))
                nc.vector.tensor_scalar(ve[:, n:n + 1], mv[:, n, 1:2], EPS, None, ALU.add).then_inc(var_eps, 1)

            def add_o(i, s, t):
                add(i, s, f"O{t}", res1[:, t, :], res1_ready, nth(i - 1, NT, t))

            def add_f(i, s, t):
                add(i, s, f"F{t}", res2[:, t % 2, :], res2_ready, nth(i - 1, NT, t))

            def normalize(i, use, target, ready):
                n = LN.index(use) % 2
                dve.wait_ge(rstd_ready, ln_count(i, use))
                nc.vector.tensor_scalar(target, y[:, n, :], mv[:, n, 0:1], rstd[:, n:n + 1], ALU.subtract,
                                        ALU.mult).then_inc(ready, 1)

            def normalize_o(i, t):
                wait_reuse(dve, res2_ready, two_back(i - 1, NT, t))
                wait_reuse(dve, x2T_hi, two_back(i - 1, NT, t))
                normalize(i, f"O{t}", x2[:, t % 2, :], x2_ready)

            def normalize_f(i, t):
                wait_reuse(dve, y_stored[t % 2], (i - 1) * 32 + 16 * (t // 2))
                normalize(i, f"F{t}", y_out[:, t % 2, :], y_ready)

            def top_both(i, t):
                softmax_top(i, t, 0)
                softmax_top(i, t, 1)

            def step(i, front, back):
                s = Shared(i, front, back)
                if front:
                    find_hidden(i)
                    for c in range(NC):
                        split_x1(i, s, c)
                if back:
                    add_o(i, s, 0)
                if front:
                    split_q(i, s, 0)
                    split_q(i, s, 1)
                if back:
                    normalize_o(i, 0)
                if front:
                    split_q(i, s, 2)
                    split_q(i, s, 3)
                    top_both(i, 0)
                if back:
                    add_o(i, s, 1)
                    split_x2(i, s, 0)
                    normalize_o(i, 1)
                if front:
                    invert_totals(i, 0)
                    top_both(i, 1)
                if back:
                    add_o(i, s, 2)
                    add_f(i, s, 0)
                    normalize_o(i, 2)
                    split_x2(i, s, 1)
                    normalize_f(i, 0)
                if front:
                    for c in range(3):
                        split_probs(i, 0, c)
                    invert_totals(i, 1)
                    top_both(i, 2)
                if back:
                    add_o(i, s, 3)
                    add_f(i, s, 1)
                    normalize_o(i, 3)
                    split_x2(i, s, 2)
                    normalize_f(i, 1)
                if front:
                    for c in range(3):
                        split_probs(i, 1, c)
                    invert_totals(i, 2)
                    top_both(i, 3)
                if back:
                    add_f(i, s, 2)
                    split_x2(i, s, 3)
                    normalize_f(i, 2)
                if front:
                    for c in range(3):
                        split_probs(i, 2, c)
                    invert_totals(i, 3)
                if back:
                    add_f(i, s, 3)
                    normalize_f(i, 3)
                if front:
                    for c in range(3):
                        split_probs(i, 3, c)
                    for g in range(GROUPS):
                        split_o(i, s, g)

            steps(dve, step)


def build_attention(nc, ins, out, ident_dram, x1_dram):
    with ExitStack() as ctx:
        sb = lambda n, s, d=F32: ctx.enter_context(nc.sbuf_tensor(n, s, d))
        ident, half_power = sb("ident_b", [P, P]), sb("half_power_b", [P, 1])
        bias_q, bias_v = sb("bias_q", [P, NC]), sb("bias_v", [P, NC])
        bias_o, bias_f = sb("bias_o", [P, D]), sb("bias_f", [P, D])
        w_q, w_o, w_ffn = ([sb(f"{w}_{k}", [P, NC, D], F32R) for k in ("hi", "lo")] for w in ("w_q", "w_o", "w_ffn"))
        k_dram = nc.dram_tensor("keys_split", (2, D, B * KEYS), F32).ap()
        v_dram = nc.dram_tensor("values_split", (2, B * KEYS, D), F32).ap()
        wide = lambda b: b.rearrange("(a n) -> a n", a=1).to_broadcast([P, D])
        rows = lambda b: b.rearrange("(c p) -> p c", p=P)
        load_constants(nc, ctx, [(ident, ident_dram), (bias_q, rows(ins["b_q"])), (bias_v, rows(ins["b_v"])),
                                 (bias_o, wide(ins["b_o"])), (bias_f, wide(ins["bias"]))], [(half_power, -0.5)], "b")
        prepare_attention(nc, ins, ident, w_q, w_o, w_ffn, k_dram, v_dram, bias_v)
        attend(nc, ins, out, x1_dram, k_dram, v_dram, ident, half_power, w_q, w_o, w_ffn, bias_q, bias_v, bias_o, bias_f)


def build(nc, ins, out):
    x1_dram = nc.dram_tensor("x1_between", (B, S, D), F32).ap()
    build_mixing(nc, ins["x"], ins["w_qkv"], ins["w_out"], ins["dft_forward"], ins["dft_inverse"], ins["identity"],
                 ins["product_sign"], x1_dram)
    build_attention(nc, ins, out, ins["identity"], x1_dram)


_INS = {"x": "x", "ctx": "ctx_1024", "mask": "mask_BxSxS2_ik1", "w_qkv": "L0_attn_w_qkv", "w_out": "L0_attn_w_out",
        "W_q": "L0_xattn_W_q", "b_q": "L0_xattn_b_q", "W_k": "L0_xattn_W_k", "b_k": "L0_xattn_b_k",
        "W_v": "L0_xattn_W_v", "b_v": "L0_xattn_b_v", "W_o": "L0_xattn_W_o", "b_o": "L0_xattn_b_o",
        "kernel": "L0_ffn_kernel", "bias": "L0_ffn_bias", "a": "L0_ffn_a", "b": "L0_ffn_b"}


def _constants():
    n, k = np.arange(MIX_HD)[:, None], np.arange(1, MIX_HD // 2)[None, :]
    angle = 2 * np.pi * n * k / MIX_HD
    even, odd = (1.0 + (-1.0) ** n) / 2, (1.0 - (-1.0) ** n) / 2
    fwd, inv = np.zeros((P, 2, 256)), np.zeros((P, 2, 256))
    nf = MIX_HD // 2 - 1
    for half in range(2):
        for local in range(2):
            head = 2 * half + local
            rows = slice(local * MIX_HD, (local + 1) * MIX_HD)
            re, im = slice(head * nf, (head + 1) * nf), slice(P + head * nf, P + (head + 1) * nf)
            u, w = 4 * nf + head, P + 4 * nf + head
            fwd[rows, half, re], fwd[rows, half, im] = np.cos(angle), -np.sin(angle)
            fwd[rows, half, u], fwd[rows, half, w] = even[:, 0], odd[:, 0]
            inv[rows, half, re] = np.cos(angle) * (2 / MIX_HD)
            inv[rows, half, im] = -np.sin(angle) * (2 / MIX_HD)
            inv[rows, half, u], inv[rows, half, w] = even[:, 0] * (2 / MIX_HD), odd[:, 0] * (2 / MIX_HD)
    sign = np.ones((P, 1))
    sign[4 * nf:] = -1.0
    return {"dft_forward": fwd.astype(np.float32), "dft_inverse": inv.astype(np.float32),
            "identity": np.eye(P, dtype=np.float32), "product_sign": sign.astype(np.float32)}


def kernel(**inputs):
    import concourse.bacc as bacc
    from concourse.bass_utils import run_bass_kernel_spmd

    nc = bacc.Bacc("TRN2", target_bir_lowering=False, num_devices=1)
    arrays = {short: np.ascontiguousarray(inputs[name]) for short, name in _INS.items()}
    arrays.update(_constants())
    aps = {n: nc.dram_tensor(f"in_{n}", a.shape, mybir.dt.from_np(a.dtype), kind="ExternalInput").ap()
           for n, a in arrays.items()}
    out = nc.dram_tensor("out_0", (B, S, D), F32, kind="ExternalOutput").ap()
    build(nc, aps, out)
    r = run_bass_kernel_spmd(nc, [{f"in_{n}": a for n, a in arrays.items()}], core_ids=[0])
    return r.results[0]["out_0"]
```

```python
from contextlib import ExitStack

import numpy as np
import concourse.bass as bass
from concourse import mybir

F32 = mybir.dt.float32
F32R = mybir.dt.float32r
I32 = mybir.dt.int32
ALU = mybir.AluOpType
ACT = mybir.ActivationFunctionType
AX = mybir.AxisListType

P = 128
B, S, D = 8, 512, 512
NT = S // P
NC = D // P
MIX_HEADS, MIX_HD = 8, 64
PAIRS = 2
XH, XHD = 16, 32
KEYS = 77
GROUPS = D // P
GH = XH // GROUPS
GK = GH * KEYS
KC = [(0, 103), (103, 103), (206, 102)]
RANK = 16
EPS = 1e-5
MASKED = -1000000.0
ROUND_MAGIC = 1.5 * 2.0 ** 23
QMAX = 7.0


def nth(batch, per_batch, index):
    return batch * per_batch + (index + 1)


def two_back(batch, per_batch, index):
    return batch * per_batch + max(index - 1, 0)


def wait_reuse(eng, sem, value):
    if not isinstance(value, int) or value > 0:
        eng.wait_ge(sem, value)


def v_pieces():
    for j in range(GH):
        for c, (at, size) in enumerate(KC):
            a, b = max(j * KEYS, at), min((j + 1) * KEYS, at + size)
            if a < b:
                yield j, c, a - at, a - j * KEYS, b - a


def split_matmuls(nc, out, pieces):
    terms = [(l[a], r[b]) for l, r in pieces for a, b in ((0, 0), (1, 0), (0, 1))]
    for n, (l, r) in enumerate(terms):
        last = nc.tensor.matmul(out, l, r, start=(n == 0), stop=(n == len(terms) - 1))
    return last


def prepare_mixing(nc, w_qkv, w_out, dft_forward, dft_inverse, ident, w_spec, w_back):
    with ExitStack() as ctx:
        sb = lambda n, s, d=F32: ctx.enter_context(nc.sbuf_tensor(n, s, d))
        sem = lambda n: ctx.enter_context(nc.semaphore(n))
        wq_sb = sb("wqkv_sb", [P, NC, 3 * D])
        wo_sb = sb("wout_sb", [P, NC, D])
        fwd = sb("fwd_sb", [P, 2, 256])
        inv = sb("inv_sb", [P, 2, 256])
        wT = sb("wT_sb", [P, 2, NC, P])
        turned = [ctx.enter_context(nc.psum_tensor(f"turned{n}", [P, NC, P], F32)) for n in range(2)]
        prod = [ctx.enter_context(nc.psum_tensor(f"folded{n}", [P, 512], F32)) for n in range(2)]
        qkv_loaded, rest_loaded = sem("qkv_loaded"), sem("rest_loaded")
        turned_ready, wT_ready = sem("turned_ready"), sem("wT_ready")
        folded, hi_ready, lo_ready = sem("folded"), sem("folded_hi"), sem("folded_lo")
        GROUP = [(r, s) for r in range(NC) for s in range(3)]
        NG = len(GROUP)
        block = ctx.enter_context(nc.Block())

        def targets(n):
            if n < NG:
                r, s = GROUP[n]
                return w_spec[0][:, r, s, :], w_spec[1][:, r, s, :]
            return w_back[0][:, n - NG, :], w_back[1][:, n - NG, :]

        @block.sync
        def _(sp):
            sp.dma_start(fwd[:], dft_forward).then_inc(rest_loaded, 16)
            for r in range(NC):
                sp.dma_start(wq_sb[:, r, :], w_qkv[r * P:(r + 1) * P, :]).then_inc(qkv_loaded, 16)
            sp.dma_start(wo_sb[:], w_out.rearrange("(c p) n -> p c n", p=P)).then_inc(rest_loaded, 16)
            sp.dma_start(inv[:], dft_inverse).then_inc(rest_loaded, 16)

        @block.tensor
        def _(pe):
            pe.wait_ge(qkv_loaded, 16 * NC)
            pe.wait_ge(rest_loaded, 48)

            def turn(n):
                r, s = GROUP[n]
                wait_reuse(pe, wT_ready, n - 1)
                for c in range(NC):
                    at = s * D + c * P
                    last = nc.tensor.transpose(turned[n % 2][:, c, :], wq_sb[:, r, at:at + P], ident[:])
                last.then_inc(turned_ready, 1)

            turn(0)
            for n in range(NG):
                if n + 1 < NG:
                    turn(n + 1)
                pe.wait_ge(wT_ready, n + 1)
                wait_reuse(pe, lo_ready, n - 1)
                for p in range(PAIRS):
                    for h in range(2):
                        last = nc.tensor.matmul(prod[n % 2][:, p * 256:(p + 1) * 256], wT[:, n % 2, 2 * p + h, :],
                                                fwd[:, h, :], start=(h == 0), stop=(h == 1))
                last.then_inc(folded, 1)
            for f in range(NC):
                n = NG + f
                p, im = f // 2, f % 2
                pe.wait_ge(lo_ready, n - 1)
                for h in range(2):
                    last = nc.tensor.matmul(prod[n % 2][:], inv[:, h, im * P:(im + 1) * P], wo_sb[:, 2 * p + h, :],
                                            start=(h == 0), stop=(h == 1))
                last.then_inc(folded, 1)

        @block.scalar
        def _(act):
            def copy_turned(n):
                act.wait_ge(turned_ready, n + 1)
                wait_reuse(act, folded, n - 1)
                nc.scalar.activation(wT[:, n % 2, :, :], turned[n % 2][:], ACT.Copy).then_inc(wT_ready, 1)

            copy_turned(0)
            for n in range(NG + NC):
                if n + 1 < NG:
                    copy_turned(n + 1)
                act.wait_ge(folded, n + 1)
                nc.scalar.activation(targets(n)[0], prod[n % 2][:], ACT.Copy).then_inc(hi_ready, 1)

        @block.vector
        def _(dve):
            for n in range(NG + NC):
                dve.wait_ge(hi_ready, n + 1)
                hi, lo = targets(n)
                nc.vector.tensor_tensor(lo, prod[n % 2][:], hi.bitcast(F32), ALU.subtract).then_inc(lo_ready, 1)


def mix_tokens(nc, x, x1_dram, ident, sigma, w_spec, w_back, half_power):
    with ExitStack() as ctx:
        sb = lambda n, s, d=F32: ctx.enter_context(nc.sbuf_tensor(n, s, d))
        ps = lambda n, s: ctx.enter_context(nc.psum_tensor(n, s, F32))
        sem = lambda n: ctx.enter_context(nc.semaphore(n))
        x_tok = [sb(f"x_tok{n}", [P, NT, D]) for n in range(2)]
        x_res = sb("x_res", [P, NT, D])
        xT = [[sb(f"xT_{k}{n}", [P, NC, S], F32R) for k in ("hi", "lo")] for n in range(2)]
        v_sb = sb("v_sb", [P, 2, S])
        kv = sb("kv_prod", [P, 4, S])
        state = sb("state", [P, 2, S])
        qs = sb("qs_prod", [P, 4, S])
        vals = sb("vals", [P, 2, S])
        valsT = [sb(f"vals_{k}", [P, NC, S], F32R) for k in ("hi", "lo")]
        r_sb = sb("mix_r", [P, 2, D])
        x1_sb = sb("mix_x1", [P, 2, D])
        stats = sb("mix_stats", [P, 2, 6])
        mv = sb("mix_mv", [P, 2, 2])
        ve = sb("mix_ve", [P, 2])
        rstd = sb("mix_rstd", [P, 2])
        v_ps = [ps(f"v_ps{h}", [P, S]) for h in range(2)]
        k_ps = [ps(f"k_ps{h}", [P, S]) for h in range(2)]
        q_ps = [ps(f"q_ps{h}", [P, S]) for h in range(2)]
        xT_ps = ps("xT_ps", [P, S])
        out_ps = ps("out_ps", [P, D])
        x_loaded = [sem(f"x_loaded{n}") for n in range(2)]
        xres_loaded = sem("xres_loaded")
        x1_stored = [sem(f"x1_stored{n}") for n in range(2)]
        xT_filled, x_hi, x_lo = sem("xT_filled"), sem("x_hi"), sem("x_lo")
        v_filled, k_filled, q_filled, out_filled = sem("v_filled"), sem("k_filled"), sem("q_filled"), sem("out_filled")
        v_copied, kv_done, scanned, qs_done = sem("v_copied"), sem("kv_done"), sem("scanned"), sem("qs_done")
        vals_summed, vals_hi, vals_lo = sem("vals_summed"), sem("vals_hi"), sem("vals_lo")
        r_added, r_stats, r_aggr = sem("r_added"), sem("r_stats"), sem("r_aggr")
        var_eps, rstd_ready, x1_ready = sem("var_eps"), sem("rstd_ready"), sem("x1_ready")
        stats_seen = sem("stats_seen")
        block = ctx.enter_context(nc.Block())

        def steps(eng, step):
            step(0, 0, True, False)
            step(1, 1, True, True)
            with eng.Fori(2, B - 2, 2) as i:
                step(i, 0, True, True)
                step(i + 1, 1, True, True)
            step(B - 2, 0, True, True)
            step(B - 1, 1, False, True)

        @block.sync
        def _(sp):
            def load_x(i, half, reuse):
                if reuse:
                    sp.wait_ge(xT_filled, nth(i - 2, NC, NC - 1))
                sp.dma_start(x_tok[half][:], x[i].rearrange("(t p) d -> p t d", p=P)).then_inc(x_loaded[half], 16)

            def finish(i):
                wait_reuse(sp, r_added, nth(i - 1, NT, NT - 1))
                sp.dma_start(x_res[:], x[i].rearrange("(t p) d -> p t d", p=P)).then_inc(xres_loaded, 16)
                for t in range(NT):
                    sp.wait_ge(x1_ready, nth(i, NT, t))
                    sp.dma_start(x1_dram[i, t * P:(t + 1) * P, :], x1_sb[:, t % 2, :]).then_inc(x1_stored[t % 2], 16)

            load_x(0, 0, False)
            load_x(1, 1, False)
            load_x(2, 0, True)
            load_x(3, 1, True)
            finish(0)
            with sp.Fori(2, B - 3, 2) as i:
                load_x(i + 2, 0, True)
                finish(i - 1)
                load_x(i + 3, 1, True)
                finish(i)
            for i in range(B - 3, B):
                finish(i)
            for n in range(2):
                sp.wait_ge(x1_stored[n], 16 * B * NT // 2)

        @block.tensor
        def _(pe):
            def turn(i, half, c):
                if c == 0:
                    pe.wait_ge(x_loaded[half], i_loads(i, half))
                wait_reuse(pe, x_lo, nth(i, NC, c - 1))
                for t in range(NT):
                    last = nc.tensor.transpose(xT_ps[:, t * P:(t + 1) * P], x_tok[half][:, t, c * P:(c + 1) * P], ident[:])
                last.then_inc(xT_filled, 1)

            def i_loads(i, half):
                return (i - half) * 8 + 16

            def project(i, half, s, p, h):
                bank, filled, free, done = {
                    2: (v_ps, v_filled, v_copied, i * 4 + (2 * p + h - 1)),
                    1: (k_ps, k_filled, kv_done, i * 8 + (4 * p + 2 * h - 2)),
                    0: (q_ps, q_filled, qs_done, i * 8 + (4 * p + 2 * h - 2)),
                }[s]
                if p == 0 and s == 2 and h == 0:
                    pe.wait_ge(x_lo, nth(i, NC, NC - 1))
                    pe.wait_ge(x_hi, nth(i, NC, NC - 1))
                wait_reuse(pe, free, done)
                at = p * 256 + h * P
                pieces = [([w[:, c, s, at:at + P] for w in w_spec], [t[:, c, :] for t in xT[half]]) for c in range(NC)]
                split_matmuls(nc, bank[h][:], pieces).then_inc(filled, 1)

            def project_back(i, t):
                if t == 0:
                    pe.wait_ge(vals_lo, nth(i, 4, 3))
                    pe.wait_ge(vals_hi, nth(i, 4, 3))
                wait_reuse(pe, r_added, nth(i, NT, t - 1))
                tok = slice(t * P, (t + 1) * P)
                pieces = [([v[:, c, tok] for v in valsT], [w[:, c, :] for w in w_back]) for c in range(NC)]
                split_matmuls(nc, out_ps[:], pieces).then_inc(out_filled, 1)

            def step(i, half, has_next, has_last):
                project(i, half, 2, 0, 0)
                project(i, half, 2, 0, 1)
                for c, (s, h) in enumerate([(1, 0), (1, 1), (0, 0)]):
                    if has_next:
                        turn(i + 1, 1 - half, c)
                    project(i, half, s, 0, h)
                if has_next:
                    turn(i + 1, 1 - half, 3)
                if has_last:
                    project_back(i - 1, 0)
                project(i, half, 0, 0, 1)
                if has_last:
                    project_back(i - 1, 1)
                project(i, half, 2, 1, 0)
                if has_last:
                    project_back(i - 1, 2)
                project(i, half, 2, 1, 1)
                if has_last:
                    project_back(i - 1, 3)
                for s, h in [(1, 0), (1, 1), (0, 0), (0, 1)]:
                    project(i, half, s, 1, h)

            for c in range(NC):
                turn(0, 0, c)
            steps(pe, step)
            for t in range(NT):
                project_back(B - 1, t)

        @block.scalar
        def _(act):
            def split_x(i, half, c):
                act.wait_ge(xT_filled, nth(i, NC, c))
                nc.scalar.activation(xT[half][0][:, c, :], xT_ps[:], ACT.Copy).then_inc(x_hi, 1)

            def copy_v(i, p, h):
                act.wait_ge(v_filled, nth(i, 4, 2 * p + h))
                wait_reuse(act, kv_done, i * 8 + 4 * p)
                nc.scalar.activation(v_sb[:, h, :], v_ps[h][:], ACT.Copy).then_inc(v_copied, 1)

            def split_vals(i, p, h):
                act.wait_ge(vals_summed, nth(i, 4, 2 * p + h))
                if p == 0 and h == 0:
                    wait_reuse(act, out_filled, i * NT)
                nc.scalar.activation(valsT[0][:, 2 * p + h, :], vals[:, h, :], ACT.Copy).then_inc(vals_hi, 1)

            def step(i, half, has_next, has_last):
                copy_v(i, 0, 0)
                copy_v(i, 0, 1)
                if has_next:
                    for c in range(NC):
                        split_x(i + 1, 1 - half, c)
                copy_v(i, 1, 0)
                copy_v(i, 1, 1)
                for p in range(PAIRS):
                    for h in range(2):
                        split_vals(i, p, h)

            for c in range(NC):
                split_x(0, 0, c)
            steps(act, step)

        @block.gpsimd
        def _(pool):
            def root(i, t):
                pool.wait_ge(var_eps, nth(i, NT, t))
                wait_reuse(pool, x1_ready, two_back(i, NT, t))
                nc.gpsimd.tensor_tensor(rstd[:, t % 2:t % 2 + 1], ve[:, t % 2:t % 2 + 1], half_power[:],
                                        ALU.pow).then_inc(rstd_ready, 1)

            def sum_vals(i, p, h):
                pool.wait_ge(qs_done, nth(i, 8, 4 * p + 3))
                wait_reuse(pool, vals_lo, i * 4 + (2 * p + h - 1))
                wait_reuse(pool, vals_hi, i * 4 + (2 * p + h - 1))
                nc.gpsimd.tensor_tensor(vals[:, h, :], qs[:, 2 * h, :], qs[:, 2 * h + 1, :],
                                        ALU.subtract if h else ALU.add).then_inc(vals_summed, 1)

            def remainder(i, p, h):
                pool.wait_ge(vals_hi, nth(i, 4, 2 * p + h))
                pool.wait_ge(vals_summed, nth(i, 4, 2 * p + h))
                nc.gpsimd.tensor_tensor(valsT[1][:, 2 * p + h, :], vals[:, h, :],
                                        valsT[0][:, 2 * p + h, :].bitcast(F32), ALU.subtract).then_inc(vals_lo, 1)

            def step(i, half, has_next, has_last):
                if has_last:
                    root(i - 1, 0)
                sum_vals(i, 0, 0)
                if has_last:
                    root(i - 1, 1)
                sum_vals(i, 0, 1)
                if has_last:
                    root(i - 1, 2)
                    root(i - 1, 3)
                remainder(i, 0, 0)
                remainder(i, 0, 1)
                sum_vals(i, 1, 0)
                sum_vals(i, 1, 1)
                remainder(i, 1, 0)
                remainder(i, 1, 1)

            steps(pool, step)
            for t in range(NT):
                root(B - 1, t)

        @block.vector
        def _(dve):
            def split_x(i, half, c):
                dve.wait_ge(x_hi, nth(i, NC, c))
                nc.vector.tensor_tensor(xT[half][1][:, c, :], xT_ps[:], xT[half][0][:, c, :].bitcast(F32),
                                        ALU.subtract).then_inc(x_lo, 1)

            def times_k(i, p, h):
                dve.wait_ge(k_filled, nth(i, 4, 2 * p + h))
                dve.wait_ge(v_copied, nth(i, 4, 2 * p + 1))
                wait_reuse(dve, scanned, i * 4 + 2 * p)
                if h == 0:
                    nc.vector.tensor_tensor(kv[:, 0, :], k_ps[0][:], v_sb[:, 0, :], ALU.mult).then_inc(kv_done, 1)
                    nc.vector.tensor_tensor(kv[:, 1, :], k_ps[0][:], v_sb[:, 1, :], ALU.mult).then_inc(kv_done, 1)
                else:
                    nc.vector.scalar_tensor_tensor(out=kv[:, 2, :], in0=k_ps[1][:], scalar=sigma[:], in1=v_sb[:, 1, :],
                                                   op0=ALU.mult, op1=ALU.mult).then_inc(kv_done, 1)
                    nc.vector.tensor_tensor(kv[:, 3, :], k_ps[1][:], v_sb[:, 0, :], ALU.mult).then_inc(kv_done, 1)

            def scan(i, p):
                dve.wait_ge(kv_done, nth(i, 8, 4 * p + 3))
                wait_reuse(dve, qs_done, i * 8 + 4 * p)
                nc.vector.tensor_tensor_scan(state[:, 0, :], kv[:, 0, :], kv[:, 2, :], 0.0, ALU.add,
                                             ALU.subtract).then_inc(scanned, 1)
                nc.vector.tensor_tensor_scan(state[:, 1, :], kv[:, 1, :], kv[:, 3, :], 0.0, ALU.add,
                                             ALU.add).then_inc(scanned, 1)

            def times_q(i, p, h):
                dve.wait_ge(q_filled, nth(i, 4, 2 * p + h))
                dve.wait_ge(scanned, nth(i, 4, 2 * p + 1))
                wait_reuse(dve, vals_summed, i * 4 + 2 * p)
                if h == 0:
                    nc.vector.tensor_tensor(qs[:, 0, :], q_ps[0][:], state[:, 0, :], ALU.mult).then_inc(qs_done, 1)
                    nc.vector.tensor_tensor(qs[:, 2, :], q_ps[0][:], state[:, 1, :], ALU.mult).then_inc(qs_done, 1)
                else:
                    nc.vector.tensor_tensor(qs[:, 1, :], q_ps[1][:], state[:, 1, :], ALU.mult).then_inc(qs_done, 1)
                    nc.vector.scalar_tensor_tensor(out=qs[:, 3, :], in0=q_ps[1][:], scalar=sigma[:], in1=state[:, 0, :],
                                                   op0=ALU.mult, op1=ALU.mult).then_inc(qs_done, 1)

            def add_residual(i, t):
                dve.wait_ge(out_filled, nth(i, NT, t))
                if t == 0:
                    dve.wait_ge(xres_loaded, nth(i, 1, 0) * 16)
                wait_reuse(dve, x1_ready, two_back(i, NT, t))
                k = t % 2
                nc.vector.tensor_tensor(r_sb[:, k, :], out_ps[:], x_res[:, t, :], ALU.add).then_inc(r_added, 1)
                dve.wait_ge(r_added, nth(i, NT, t))
                nc.vector.bn_stats(stats[:, k, :], r_sb[:, k, :]).then_inc(r_stats, 1)
                dve.wait_ge(r_stats, nth(i, NT, t))
                dve.sem_inc(stats_seen, 1)
                nc.vector.bn_aggr(mv[:, k, :], stats[:, k, :]).then_inc(r_aggr, 1)
                dve.wait_ge(r_aggr, nth(i, NT, t))
                wait_reuse(dve, rstd_ready, two_back(i, NT, t))
                nc.vector.tensor_scalar(ve[:, k:k + 1], mv[:, k, 1:2], EPS, None, ALU.add).then_inc(var_eps, 1)

            def normalize(i, t):
                dve.wait_ge(rstd_ready, nth(i, NT, t))
                wait_reuse(dve, x1_stored[t % 2], i * 32 + 16 * (t // 2))
                k = t % 2
                nc.vector.tensor_scalar(x1_sb[:, k, :], r_sb[:, k, :], mv[:, k, 0:1], rstd[:, k:k + 1],
                                        ALU.subtract, ALU.mult).then_inc(x1_ready, 1)

            def step(i, half, has_next, has_last):
                def turned(c):
                    if has_next:
                        split_x(i + 1, 1 - half, c)

                turned(0)
                times_k(i, 0, 0)
                turned(1)
                times_k(i, 0, 1)
                turned(2)
                scan(i, 0)
                turned(3)
                times_q(i, 0, 0)
                if has_last:
                    add_residual(i - 1, 0)
                times_q(i, 0, 1)
                if has_last:
                    add_residual(i - 1, 1)
                    normalize(i - 1, 0)
                    normalize(i - 1, 1)
                    add_residual(i - 1, 2)
                    add_residual(i - 1, 3)
                    normalize(i - 1, 2)
                    normalize(i - 1, 3)
                times_k(i, 1, 0)
                times_k(i, 1, 1)
                scan(i, 1)
                times_q(i, 1, 0)
                times_q(i, 1, 1)

            for c in range(NC):
                split_x(0, 0, c)
            steps(dve, step)
            for t in range(NT):
                add_residual(B - 1, t)
                normalize(B - 1, t)


def build_mixing(nc, x, w_qkv, w_out, dft_forward, dft_inverse, ident_dram, sign_dram, x1_dram):
    with ExitStack() as ctx:
        sb = lambda n, s, d=F32: ctx.enter_context(nc.sbuf_tensor(n, s, d))
        ident = sb("ident_a", [P, P])
        sigma = sb("sigma", [P, 1])
        half_power = sb("half_power_a", [P, 1])
        w_spec = [sb(f"w_spec_{k}", [P, NC, 3, D], F32R) for k in ("hi", "lo")]
        w_back = [sb(f"w_back_{k}", [P, NC, D], F32R) for k in ("hi", "lo")]
        load_constants(nc, ctx, [(ident, ident_dram), (sigma, sign_dram)], [(half_power, -0.5)], "a")
        prepare_mixing(nc, w_qkv, w_out, dft_forward, dft_inverse, ident, w_spec, w_back)
        mix_tokens(nc, x, x1_dram, ident, sigma, w_spec, w_back, half_power)


def load_constants(nc, ctx, loads, fills, tag):
    loaded = ctx.enter_context(nc.semaphore(f"constants_{tag}"))
    with nc.Block() as block:
        @block.sync
        def _(sp):
            for tile, src in loads:
                sp.dma_start(tile[:], src, allow_slow_non_contiguous=True).then_inc(loaded, 16)
            sp.wait_ge(loaded, 16 * len(loads))

        @block.gpsimd
        def _(pool):
            for tile, value in fills:
                nc.gpsimd.memset(tile[:], value)



def prepare_attention(nc, ins, ident, w_q, w_o, w_ffn, k_dram, v_dram, bias_v):
    rows = B * KEYS
    half_rows = rows // 2
    tiles = [(n * P, min(P, rows - n * P)) for n in range((rows + P - 1) // P)]
    with ExitStack() as ctx:
        sb = lambda n, s, d=F32: ctx.enter_context(nc.sbuf_tensor(n, s, d))
        ps = lambda n, s: ctx.enter_context(nc.psum_tensor(n, s, F32))
        sem = lambda n: ctx.enter_context(nc.semaphore(n))
        raw_q, raw_o = sb("raw_q", [P, NC, D]), sb("raw_o", [P, NC, D])
        raw_k, raw_v, raw_f = sb("raw_k", [P, NC, D]), sb("raw_v", [P, NC, D]), sb("raw_f", [P, NC, D])
        ctx_sb = sb("ctx_sb", [P, len(tiles), D])
        ctxT = sb("ctxT", [P, NC, rows])
        a_sb, b_sb, aT = sb("a_sb", [P, NC, RANK]), sb("b_sb", [RANK, D]), sb("aT", [RANK, D])
        bias_k = sb("bias_k", [P, NC])
        k_val = sb("k_val", [P, 2, half_rows])
        k_hi, k_lo = sb("k_hi", [P, 2, half_rows], F32R), sb("k_lo", [P, 2, half_rows], F32R)
        v_hi, v_lo = sb("v_hi", [P, 2, D], F32R), sb("v_lo", [P, 2, D], F32R)
        top, top_all = sb("top", [P, 1]), sb("top_all", [P, 1])
        scale, per_scale = sb("q_scale", [P, 1]), sb("q_per_scale", [P, 1])
        quant = sb("quant", [P, NC, D])
        merged = sb("merged", [P, 2, D])
        turned = [ps(f"turned_b{n}", [P, NC * P]) for n in range(2)]
        prod = [ps(f"prod_b{n}", [P, D]) for n in range(2)]
        ctx_loaded, kv_loaded, qo_loaded, ffn_loaded = sem("ctx_loaded"), sem("kv_loaded"), sem("qo_loaded"), sem("ffn_loaded")
        turned_ready, turned_copied = sem("turned_b"), sem("turned_b_copied")
        prod_ready, prod_used = sem("prod_b"), sem("prod_b_used")
        k_biased, k_hi_ready, k_lo_ready = sem("k_biased"), sem("k_hi_ready"), sem("k_lo_ready")
        v_hi_ready, v_lo_ready = sem("v_hi_ready"), sem("v_lo_ready")
        stored = [sem(f"kv_stored{n}") for n in range(2)]
        w_hi_ready = sem("w_hi_ready")
        top_ready, top_spread, scale_ready, per_ready = sem("top_ready"), sem("top_spread"), sem("scale_ready"), sem("per_ready")
        quantized, merged_ready, merged_hi, merged_lo = sem("quantized"), sem("merged_ready"), sem("merged_hi"), sem("merged_lo")
        block = ctx.enter_context(nc.Block())
        NTURN = NC + 1
        NKEY = 2 * NC
        NVAL = len(tiles)
        by_chunk = lambda w: w.rearrange("(c p) n -> p c n", p=P)

        @block.sync
        def _(sp):
            flat = ins["ctx"].rearrange("b k d -> (b k) d")
            for n, (at, size) in enumerate(tiles):
                sp.dma_start(ctx_sb[0:size, n, :], flat[at:at + size, :]).then_inc(ctx_loaded, 16)
            sp.dma_start(raw_k[:], by_chunk(ins["W_k"])).then_inc(kv_loaded, 16)
            sp.dma_start(bias_k[:], ins["b_k"].rearrange("(c p) -> p c", p=P),
                         allow_slow_non_contiguous=True).then_inc(kv_loaded, 16)
            sp.dma_start(raw_v[:], by_chunk(ins["W_v"])).then_inc(kv_loaded, 16)
            sp.dma_start(raw_f[:], by_chunk(ins["kernel"])).then_inc(ffn_loaded, 16)
            sp.dma_start(a_sb[:], by_chunk(ins["a"])).then_inc(ffn_loaded, 16)
            sp.dma_start(b_sb[:], ins["b"]).then_inc(ffn_loaded, 16)
            sp.dma_start(raw_q[:], by_chunk(ins["W_q"])).then_inc(qo_loaded, 16)
            sp.dma_start(raw_o[:], by_chunk(ins["W_o"])).then_inc(qo_loaded, 16)
            for n in range(NKEY):
                c, h = n // 2, n % 2
                sp.wait_ge(k_lo_ready, n + 1)
                for part, tile in enumerate((k_hi, k_lo)):
                    sp.dma_start(k_dram[part, c * P:(c + 1) * P, h * half_rows:(h + 1) * half_rows],
                                 tile[:, n % 2, :].bitcast(F32)).then_inc(stored[n % 2], 16)
            for n, (at, size) in enumerate(tiles):
                sp.wait_ge(v_lo_ready, n + 1)
                for part, tile in enumerate((v_hi, v_lo)):
                    sp.dma_start(v_dram[part, at:at + size, :], tile[0:size, n % 2, :].bitcast(F32)).then_inc(stored[n % 2], 16)
            for n in range(2):
                sp.wait_ge(stored[n], 32 * (NKEY // 2 + len(range(n, NVAL, 2))))

        @block.tensor
        def _(pe):
            pe.wait_ge(ctx_loaded, 16 * len(tiles))
            for c in range(NC):
                wait_reuse(pe, turned_copied, 2 * (c - 1))
                for n, (at, size) in enumerate(tiles[:NC]):
                    last = nc.tensor.transpose(turned[c % 2][:, n * P:n * P + size], ctx_sb[0:size, n, c * P:(c + 1) * P],
                                               ident[0:size, 0:size])
                last.then_inc(turned_ready, 1)
                at, size = tiles[NC]
                nc.tensor.transpose(prod[c % 2][:, 0:size], ctx_sb[0:size, NC, c * P:(c + 1) * P],
                                    ident[0:size, 0:size]).then_inc(turned_ready, 1)
            pe.wait_ge(ffn_loaded, 48)
            pe.wait_ge(turned_copied, 2 * (NC - 1))
            for c in range(NC):
                last = nc.tensor.transpose(turned[0][0:RANK, c * P:(c + 1) * P], a_sb[:, c, :], ident[:])
            last.then_inc(turned_ready, 1)
            pe.wait_ge(kv_loaded, 48)
            pe.wait_ge(turned_copied, 2 * NC)
            for n in range(NKEY):
                c, h = n // 2, n % 2
                wait_reuse(pe, prod_used, n - 1)
                for k in range(NC):
                    last = nc.tensor.matmul(prod[n % 2][:, 0:half_rows], raw_k[:, k, c * P:(c + 1) * P],
                                            ctxT[:, k, h * half_rows:(h + 1) * half_rows], start=(k == 0), stop=(k == NC - 1))
                last.then_inc(prod_ready, 1)
            for m, (at, size) in enumerate(tiles):
                n = NKEY + m
                pe.wait_ge(prod_used, n - 1)
                for k in range(NC):
                    last = nc.tensor.matmul(prod[n % 2][0:size, :], ctxT[:, k, at:at + size], raw_v[:, k, :],
                                            start=(k == 0), stop=(k == NC - 1))
                last.then_inc(prod_ready, 1)
            pe.wait_ge(turned_copied, 2 * NC + 1)
            for c in range(NC):
                n = NKEY + NVAL + c
                pe.wait_ge(prod_used, n - 1)
                nc.tensor.matmul(prod[n % 2][:], aT[:, c * P:(c + 1) * P], b_sb[:], start=True, stop=True).then_inc(prod_ready, 1)

        @block.scalar
        def _(act):
            at, size = tiles[NC]
            for c in range(NC):
                act.wait_ge(turned_ready, 2 * c + 1)
                nc.scalar.activation(ctxT[:, c, 0:at], turned[c % 2][:], ACT.Copy).then_inc(turned_copied, 1)
                act.wait_ge(turned_ready, 2 * c + 2)
                nc.scalar.activation(ctxT[:, c, at:rows], prod[c % 2][:, 0:size], ACT.Copy).then_inc(turned_copied, 1)
            act.wait_ge(turned_ready, 2 * NC + 1)
            nc.scalar.activation(aT[:], turned[0][0:RANK, :], ACT.Copy).then_inc(turned_copied, 1)
            for n in range(NKEY):
                act.wait_ge(k_biased, n + 1)
                wait_reuse(act, stored[n % 2], 32 * (n // 2))
                nc.scalar.activation(k_hi[:, n % 2, :], k_val[:, n % 2, :], ACT.Copy).then_inc(k_hi_ready, 1)
            for m, (at, size) in enumerate(tiles):
                act.wait_ge(prod_ready, NKEY + m + 1)
                if m >= 2:
                    act.wait_ge(stored[m % 2], 32 * (NKEY // 2 + m // 2))
                nc.scalar.activation(v_hi[0:size, m % 2, :], prod[(NKEY + m) % 2][0:size, :], ACT.Copy).then_inc(v_hi_ready, 1)
            act.wait_ge(qo_loaded, 32)
            nc.scalar.activation(w_q[0][:], raw_q[:], ACT.Copy).then_inc(w_hi_ready, 1)
            nc.scalar.activation(w_o[0][:], raw_o[:], ACT.Copy).then_inc(w_hi_ready, 1)
            for c in range(NC):
                act.wait_ge(merged_ready, c + 1)
                nc.scalar.activation(w_ffn[0][:, c, :], merged[:, c % 2, :], ACT.Copy).then_inc(merged_hi, 1)

        @block.gpsimd
        def _(pool):
            pool.wait_ge(top_ready, 1)
            nc.gpsimd.partition_all_reduce(top_all[:], top[:], P, bass.bass_isa.ReduceOp.max).then_inc(top_spread, 1)
            for n, (w, raw) in enumerate(((w_q, raw_q), (w_o, raw_o))):
                pool.wait_ge(w_hi_ready, n + 1)
                pool.wait_ge(qo_loaded, 32)
                for c in range(NC):
                    last = nc.gpsimd.tensor_tensor(w[1][:, c, :], raw[:, c, :], w[0][:, c, :].bitcast(F32), ALU.subtract)

        @block.vector
        def _(dve):
            dve.wait_ge(ffn_loaded, 48)
            nc.vector.tensor_reduce(top[:], raw_f[:].rearrange("p c n -> p (c n)"), AX.X, ALU.max,
                                    apply_absolute_value=True).then_inc(top_ready, 1)
            for n in range(NKEY):
                c = n // 2
                dve.wait_ge(prod_ready, n + 1)
                if n == 0:
                    dve.wait_ge(kv_loaded, 48)
                wait_reuse(dve, k_lo_ready, n - 1)
                nc.vector.tensor_scalar(k_val[:, n % 2, :], prod[n % 2][:, 0:half_rows], bias_k[:, c:c + 1],
                                        float(XHD) ** -0.5, ALU.add, ALU.mult).then_inc(k_biased, 1)
                dve.wait_ge(k_biased, n + 1)
                dve.sem_inc(prod_used, 1)
                dve.wait_ge(k_hi_ready, n + 1)
                nc.vector.tensor_tensor(k_lo[:, n % 2, :], k_val[:, n % 2, :], k_hi[:, n % 2, :].bitcast(F32),
                                        ALU.subtract).then_inc(k_lo_ready, 1)
            for m, (at, size) in enumerate(tiles):
                dve.wait_ge(v_hi_ready, m + 1)
                nc.vector.tensor_tensor(v_lo[0:size, m % 2, :], prod[(NKEY + m) % 2][0:size, :],
                                        v_hi[0:size, m % 2, :].bitcast(F32), ALU.subtract).then_inc(v_lo_ready, 1)
                dve.wait_ge(v_lo_ready, m + 1)
                dve.sem_inc(prod_used, 1)
            dve.wait_ge(top_spread, 1)
            nc.vector.tensor_scalar(scale[:], top_all[:], 1.0 / QMAX, None, ALU.mult).then_inc(scale_ready, 1)
            dve.wait_ge(scale_ready, 1)
            nc.vector.reciprocal(per_scale[:], scale[:]).then_inc(per_ready, 1)
            dve.wait_ge(per_ready, 1)
            nc.vector.tensor_scalar(quant[:], raw_f[:], per_scale[:], ROUND_MAGIC, ALU.mult, ALU.add).then_inc(quantized, 1)
            dve.wait_ge(quantized, 1)
            nc.vector.tensor_scalar(quant[:], quant[:], ROUND_MAGIC, -QMAX - 1, ALU.subtract, ALU.max).then_inc(quantized, 1)
            dve.wait_ge(quantized, 2)
            nc.vector.tensor_scalar(quant[:], quant[:], QMAX, scale[:], ALU.min, ALU.mult).then_inc(quantized, 1)
            dve.wait_ge(quantized, 3)
            for c in range(NC):
                n = NKEY + NVAL + c
                dve.wait_ge(prod_ready, n + 1)
                wait_reuse(dve, merged_lo, c - 1)
                nc.vector.tensor_tensor(merged[:, c % 2, :], prod[n % 2][:], quant[:, c, :], ALU.add).then_inc(merged_ready, 1)
                dve.wait_ge(merged_ready, c + 1)
                dve.sem_inc(prod_used, 1)
                dve.wait_ge(merged_hi, c + 1)
                nc.vector.tensor_tensor(w_ffn[1][:, c, :], merged[:, c % 2, :], w_ffn[0][:, c, :].bitcast(F32),
                                        ALU.subtract).then_inc(merged_lo, 1)


BACK, FRONT, NEXT = "VOTF", "P", "XQ"
RING = 4
BANK_ORDER = ["V0", "V1", "V2", "V3", "P00", "O0", "P01", "P02", "O1", "T0", "O2", "P10", "P11", "F0", "T1",
              "O3", "X0", "X1", "F1", "T2", "X2", "X3", "P12", "P20", "F2", "Q0", "P21", "Q1", "T3", "Q2",
              "P22", "F3", "P30", "Q3", "P31", "P32"]


class Shared:

    def __init__(self, i, back, front, next_):
        self.order = self.uses(back, front, next_)
        count = lambda kinds: sum(u[0] in kinds for u in BANK_ORDER)
        if isinstance(i, int):
            nexts, fronts, backs = min(i + 1, B), min(max(i, 0), B), max(i - 1, 0)
            self.before = count(NEXT) * nexts + count(FRONT) * fronts + count(BACK) * backs
            self.filled_before = self.before - count(FRONT) * fronts
            self.previous = self.uses(i - 1 >= 1, 0 <= i - 1 <= B - 1, i - 1 <= B - 2)
        else:
            self.before = i * len(BANK_ORDER) - (count(BACK) - count(NEXT))
            self.filled_before = i * (count(BACK) + count(NEXT)) - (count(BACK) - count(NEXT))
            self.previous = BANK_ORDER

    @staticmethod
    def uses(back, front, next_):
        kinds = (BACK if back else "") + (FRONT if front else "") + (NEXT if next_ else "")
        return [u for u in BANK_ORDER if u[0] in kinds]

    def bank(self, use):
        return self.order.index(use) % RING

    def filled(self, use):
        return self.filled_before + ([u for u in self.order if u[0] != "P"].index(use) + 1)

    def emptied(self, use):
        return self.before + (self.order.index(use) + 1)

    def emptied_before(self, use):
        return self.before - (len(self.previous) - 1 - self.previous.index(use))

    def reusable(self, use):
        return self.before + (self.order.index(use) + 1 - RING)


def attend(nc, ins, out, x1_dram, k_dram, v_dram, ident, half_power, w_q, w_o, w_ffn, bias_q, bias_v, bias_o, bias_f):
    with ExitStack() as ctx:
        sb = lambda n, s, d=F32: ctx.enter_context(nc.sbuf_tensor(n, s, d))
        ps = lambda n, s: ctx.enter_context(nc.psum_tensor(n, s, F32))
        sem = lambda n: ctx.enter_context(nc.semaphore(n))
        pair = lambda n, s: [sb(f"{n}_hi", s, F32R), sb(f"{n}_lo", s, F32R)]
        x1 = sb("x1", [P, NT, D])
        mask = sb("mask", [P, NT, KEYS], I32)
        hidden = sb("hidden", [P, NT, KEYS], I32)
        masked = sb("masked", [P, KEYS])
        k_block, v_block = pair("k_block", [P, GROUPS, GK]), pair("v_block", [KC[0][1], len(KC), GROUPS, P])
        qT, oT = pair("qT", [P, NC, S]), pair("oT", [P, NC, S])
        x2T = pair("x2T", [P, NC, P])
        pT = pair("pT", [P, len(KC), GROUPS, S])
        x1T = oT
        probs = sb("probs", [P, 2, XH * KEYS])
        top, total, per_total = sb("top_s", [P, 2, XH]), sb("total", [P, 2, XH]), sb("per_total", [P, 2, XH])
        res1 = sb("res1", [P, NT, D])
        y, x2, res2, y_out = sb("y", [P, 2, D]), sb("x2", [P, 2, D]), sb("res2", [P, 2, D]), sb("y_out", [P, 2, D])
        stats, mv = sb("stats", [P, 2, 6]), sb("mv", [P, 2, 2])
        ve, rstd = sb("ve", [P, 2]), sb("rstd", [P, 2])
        score_ps = ps("score_ps", [P, GROUPS, 512])
        shared_ps = [ps(f"shared_ps{n}", [P, 512]) for n in range(RING)]

        blocks_cleared, masked_set = sem("blocks_cleared"), sem("masked_set")
        x1_loaded, res1_loaded, mask_loaded, k_loaded, v_loaded = sem("x1_loaded"), sem("res1_loaded"), sem("mask_loaded"), sem("k_loaded"), sem("v_loaded")
        hidden_ready, res1_ready, res2_ready = sem("hidden_ready"), sem("res1_ready"), sem("res2_ready")
        filled, freed = sem("shared_filled"), sem("shared_freed")
        x1T_hi, q_hi, oT_hi, x2T_hi = sem("x1T_hi_ready"), sem("q_hi_ready"), sem("oT_hi_ready"), sem("x2T_hi_ready")
        scored, hid, topped, exped, totalled, normed = (sem("scored"), sem("hid"), sem("topped"), sem("exped"),
                                                       sem("per_total_ready"), sem("normed"))
        turned, turned_hi = sem("turned_p"), sem("pT_hi_ready")
        stat_done, stat_seen, aggr_done = sem("stat_done"), sem("stat_seen"), sem("aggr_done")
        var_eps, rstd_ready, x2_ready, y_ready = sem("var_eps_b"), sem("rstd_b"), sem("x2_ready"), sem("y_ready")
        y_stored = [sem(f"y_stored{n}") for n in range(2)]
        block = ctx.enter_context(nc.Block())

        def steps(eng, step):
            step(-1, False, False, True)
            step(0, False, True, True)
            step(1, True, True, True)
            with eng.Fori(2, B - 1) as i:
                step(i, True, True, True)
            step(B - 1, True, True, False)
            step(B, True, False, False)

        LN = [u for u in BANK_ORDER if u[0] in "OF"]

        def ln_count(i, use):
            return nth(i - 1, len(LN), LN.index(use))

        def turned_bank(s, t, c):
            return shared_ps[s.bank(f"P{t}{c}")][0:KC[c][1], :].rearrange("p (g n) -> p g n", g=GROUPS)

        @block.sync
        def _(sp):
            def load_mask(i):
                wait_reuse(sp, hidden_ready, i)
                sp.dma_start(mask[:], ins["mask"][i].rearrange("(t p) k -> p t k", p=P)).then_inc(mask_loaded, 16)

            def load_x1(i):
                wait_reuse(sp, x1T_hi, i * NC)
                sp.dma_start(x1[:], x1_dram[i].rearrange("(t p) d -> p t d", p=P)).then_inc(x1_loaded, 16)

            def load_residual(i, s, reuse):
                if reuse:
                    sp.wait_ge(freed, s.emptied("O3"))
                sp.dma_start(res1[:], x1_dram[i].rearrange("(t p) d -> p t d", p=P)).then_inc(res1_loaded, 16)

            def load_keys(i):
                wait_reuse(sp, scored, i * NT * 2)
                for part in range(2):
                    src = k_dram[part].rearrange("(g j d) r -> j d g r", j=GH, d=XHD)
                    for j in range(GH):
                        sp.dma_start(k_block[part][j * XHD:(j + 1) * XHD, :, j * KEYS:(j + 1) * KEYS].bitcast(F32),
                                     src[j][:, :, bass.ds(i * KEYS, KEYS)]).then_inc(k_loaded, 16)

            def load_values(i):
                wait_reuse(sp, oT_hi, i * NC)
                for part in range(2):
                    src = v_dram[part].rearrange("r (g j d) -> r g j d", g=GROUPS, j=GH)
                    for j, c, row, key, n in v_pieces():
                        sp.dma_start(v_block[part][row:row + n, c, :, j * XHD:(j + 1) * XHD].bitcast(F32),
                                     src[bass.ds(i * KEYS + key, n)][:, :, j, :]).then_inc(v_loaded, 16)

            def store(i, t):
                sp.wait_ge(y_ready, nth(i, NT, t))
                sp.dma_start(out[i, t * P:(t + 1) * P, :], y_out[:, t % 2, :]).then_inc(y_stored[t % 2], 16)

            load_x1(0)
            load_mask(0)
            sp.wait_ge(blocks_cleared, 4)
            load_keys(0)

            def step(i, back, front, next_):
                if next_:
                    load_x1(i + 1)
                    load_mask(i + 1)
                if front:
                    load_values(i)
                if back:
                    store(i - 1, 0)
                if next_:
                    load_keys(i + 1)
                if back:
                    store(i - 1, 1)
                if front:
                    load_residual(i, Shared(i, back, front, next_), back)
                if back:
                    store(i - 1, 2)
                    store(i - 1, 3)

            step(0, False, True, True)
            step(1, True, True, True)
            with sp.Fori(2, B - 1) as i:
                step(i, True, True, True)
            step(B - 1, True, True, False)
            step(B, True, False, False)
            for n in range(2):
                sp.wait_ge(y_stored[n], 16 * B * NT // 2)

        @block.tensor
        def _(pe):
            def turn_x1(i, s, c):
                if c == 0:
                    pe.wait_ge(x1_loaded, nth(i, 1, 0) * 16)
                use = f"X{c}"
                wait_reuse(pe, freed, s.reusable(use))
                for t in range(NT):
                    last = nc.tensor.transpose(shared_ps[s.bank(use)][:, t * P:(t + 1) * P],
                                               x1[:, t, c * P:(c + 1) * P], ident[:])
                last.then_inc(filled, 1)

            def project_q(i, s, c):
                use = f"Q{c}"
                if c == 0:
                    pe.wait_ge(x1T_hi, nth(i, NC, NC - 1))
                    pe.wait_ge(freed, s.emptied("X3"))
                wait_reuse(pe, freed, s.reusable(use))
                pieces = [([w[:, k, c * P:(c + 1) * P] for w in w_q], [x[:, k, :] for x in x1T]) for k in range(NC)]
                split_matmuls(nc, shared_ps[s.bank(use)][:], pieces).then_inc(filled, 1)

            def score(i, s, t, h):
                if t == 0 and h == 0:
                    pe.wait_ge(k_loaded, nth(i, 1, 0) * (16 * 2 * GH))
                    pe.wait_ge(q_hi, nth(i, NC, NC - 1))
                    pe.wait_ge(freed, s.emptied_before("Q3"))
                wait_reuse(pe, exped, i * (NT * XH) + ((t - 1) * XH + (h + 1) * XH // 2))
                tok = slice(t * P, (t + 1) * P)
                for g in (2 * h, 2 * h + 1):
                    last = split_matmuls(nc, score_ps[:, g, 0:GK],
                                         [([q[:, g, tok] for q in qT], [k[:, g, :] for k in k_block])])
                last.then_inc(scored, 1)

            def turn_probs(i, s, t, c):
                if c == 0:
                    pe.wait_ge(normed, nth(i, NT * 2, 2 * t + 1))
                use = f"P{t}{c}"
                wait_reuse(pe, freed, s.reusable(use))
                at, size = KC[c]
                for g in range(GROUPS):
                    last = nc.tensor.transpose(shared_ps[s.bank(use)][0:size, g * P:(g + 1) * P],
                                               probs[:, t % 2, g * GK + at:g * GK + at + size], ident[:])
                last.then_inc(turned, 1)

            def weigh_values(i, s, g):
                use = f"V{g}"
                if g == 0:
                    pe.wait_ge(v_loaded, nth(i, 1, 0) * (16 * 2 * len(list(v_pieces()))))
                    pe.wait_ge(freed, s.emptied_before("P32"))
                    pe.wait_ge(turned_hi, nth(i, NT * 3, NT * 3 - 1))
                wait_reuse(pe, freed, s.reusable(use))
                pieces = [([v[0:size, c, g, :] for v in v_block], [p[0:size, c, g, :] for p in pT])
                          for c, (_, size) in enumerate(KC)]
                split_matmuls(nc, shared_ps[s.bank(use)][:], pieces).then_inc(filled, 1)

            def project_o(i, s, t):
                use = f"O{t}"
                if t == 0:
                    pe.wait_ge(oT_hi, nth(i - 1, NC, NC - 1))
                    pe.wait_ge(freed, s.emptied("V3"))
                wait_reuse(pe, freed, s.reusable(use))
                tok = slice(t * P, (t + 1) * P)
                pieces = [([o[:, k, tok] for o in oT], [w[:, k, :] for w in w_o]) for k in range(NC)]
                split_matmuls(nc, shared_ps[s.bank(use)][:], pieces).then_inc(filled, 1)

            def turn_x2(i, s, t):
                use = f"T{t}"
                pe.wait_ge(x2_ready, nth(i - 1, NT, t))
                wait_reuse(pe, freed, s.reusable(use))
                for c in range(NC):
                    last = nc.tensor.transpose(shared_ps[s.bank(use)][:, c * P:(c + 1) * P],
                                               x2[:, t % 2, c * P:(c + 1) * P], ident[:])
                last.then_inc(filled, 1)

            def project_f(i, s, t):
                use = f"F{t}"
                pe.wait_ge(x2T_hi, nth(i - 1, NT, t))
                pe.wait_ge(freed, s.emptied(f"T{t}"))
                wait_reuse(pe, freed, s.reusable(use))
                pieces = [([x[:, k, :] for x in x2T], [w[:, k, :] for w in w_ffn]) for k in range(NC)]
                split_matmuls(nc, shared_ps[s.bank(use)][:], pieces).then_inc(filled, 1)

            def step(i, back, front, next_):
                s = Shared(i, back, front, next_)
                if front:
                    score(i, s, 0, 0)
                if back:
                    weigh_values(i - 1, s, 0)
                if front:
                    score(i, s, 0, 1)
                if back:
                    weigh_values(i - 1, s, 1)
                    weigh_values(i - 1, s, 2)
                    weigh_values(i - 1, s, 3)
                if front:
                    score(i, s, 1, 0)
                    score(i, s, 1, 1)
                    turn_probs(i, s, 0, 0)
                if back:
                    project_o(i, s, 0)
                if front:
                    turn_probs(i, s, 0, 1)
                    turn_probs(i, s, 0, 2)
                if back:
                    project_o(i, s, 1)
                if front:
                    score(i, s, 2, 0)
                    score(i, s, 2, 1)
                if back:
                    turn_x2(i, s, 0)
                    project_o(i, s, 2)
                if front:
                    turn_probs(i, s, 1, 0)
                    turn_probs(i, s, 1, 1)
                if back:
                    project_f(i, s, 0)
                    turn_x2(i, s, 1)
                    project_o(i, s, 3)
                if next_:
                    turn_x1(i + 1, s, 0)
                    turn_x1(i + 1, s, 1)
                if back:
                    project_f(i, s, 1)
                    turn_x2(i, s, 2)
                if next_:
                    turn_x1(i + 1, s, 2)
                    turn_x1(i + 1, s, 3)
                if front:
                    turn_probs(i, s, 1, 2)
                    score(i, s, 3, 0)
                    score(i, s, 3, 1)
                    turn_probs(i, s, 2, 0)
                if back:
                    project_f(i, s, 2)
                if next_:
                    project_q(i + 1, s, 0)
                if front:
                    turn_probs(i, s, 2, 1)
                if next_:
                    project_q(i + 1, s, 1)
                if back:
                    turn_x2(i, s, 3)
                if next_:
                    project_q(i + 1, s, 2)
                if front:
                    turn_probs(i, s, 2, 2)
                if back:
                    project_f(i, s, 3)
                if front:
                    turn_probs(i, s, 3, 0)
                if next_:
                    project_q(i + 1, s, 3)
                if front:
                    turn_probs(i, s, 3, 1)
                    turn_probs(i, s, 3, 2)

            steps(pe, step)

        @block.scalar
        def _(act):
            def split_x1(i, s, c):
                use = f"X{c}"
                act.wait_ge(filled, s.filled(use))
                nc.scalar.activation(x1T[0][:, c, :], shared_ps[s.bank(use)][:], ACT.Copy).then_inc(x1T_hi, 1)

            def split_q(i, s, c):
                use = f"Q{c}"
                act.wait_ge(filled, s.filled(use))
                nc.scalar.activation(qT[0][:, c, :], shared_ps[s.bank(use)][:], ACT.Identity,
                                     bias=bias_q[:, c:c + 1]).then_inc(q_hi, 1)

            def exponentials(i, t, h):
                act.wait_ge(topped, nth(i, NT * 2, 2 * t + h))
                if h == 0:
                    wait_reuse(act, turned, i * NT * 3 + (3 * (t - 1)))
                    wait_reuse(act, totalled, i * NT + (t - 1))
                for j in range(h * XH // 2, (h + 1) * XH // 2):
                    g, k = j // GH, j % GH
                    nc.scalar.activation(probs[:, t % 2, j * KEYS:(j + 1) * KEYS],
                                         score_ps[:, g, k * KEYS:(k + 1) * KEYS], ACT.Exp, bias=top[:, t % 2, j:j + 1],
                                         accum_out=total[:, t % 2, j:j + 1]).then_inc(exped, 1)

            def split_probs(i, s, t, c):
                act.wait_ge(turned, nth(i, NT * 3, 3 * t + c))
                size = KC[c][1]
                nc.scalar.activation(pT[0][0:size, c, :, t * P:(t + 1) * P], turned_bank(s, t, c),
                                     ACT.Copy).then_inc(turned_hi, 1)

            def split_o(i, s, g):
                use = f"V{g}"
                act.wait_ge(filled, s.filled(use))
                nc.scalar.activation(oT[0][:, g, :], shared_ps[s.bank(use)][:], ACT.Identity,
                                     bias=bias_v[:, g:g + 1]).then_inc(oT_hi, 1)

            def split_x2(i, s, t):
                use = f"T{t}"
                act.wait_ge(filled, s.filled(use))
                nc.scalar.activation(x2T[0][:], shared_ps[s.bank(use)][:].rearrange("p (c n) -> p c n", c=NC),
                                     ACT.Copy).then_inc(x2T_hi, 1)

            def step(i, back, front, next_):
                s = Shared(i, back, front, next_)
                if front:
                    exponentials(i, 0, 0)
                if back:
                    split_o(i - 1, s, 0)
                if front:
                    exponentials(i, 0, 1)
                if back:
                    split_o(i - 1, s, 1)
                    split_o(i - 1, s, 2)
                    split_o(i - 1, s, 3)
                if front:
                    split_probs(i, s, 0, 0)
                    exponentials(i, 1, 0)
                    split_probs(i, s, 0, 1)
                    split_probs(i, s, 0, 2)
                    exponentials(i, 1, 1)
                if back:
                    split_x2(i, s, 0)
                if front:
                    exponentials(i, 2, 0)
                    split_probs(i, s, 1, 0)
                    split_probs(i, s, 1, 1)
                    exponentials(i, 2, 1)
                if back:
                    split_x2(i, s, 1)
                if next_:
                    split_x1(i + 1, s, 0)
                    split_x1(i + 1, s, 1)
                if back:
                    split_x2(i, s, 2)
                if next_:
                    split_x1(i + 1, s, 2)
                    split_x1(i + 1, s, 3)
                if front:
                    split_probs(i, s, 1, 2)
                    split_probs(i, s, 2, 0)
                    exponentials(i, 3, 0)
                if next_:
                    split_q(i + 1, s, 0)
                if front:
                    split_probs(i, s, 2, 1)
                    exponentials(i, 3, 1)
                if next_:
                    split_q(i + 1, s, 1)
                if back:
                    split_x2(i, s, 3)
                if next_:
                    split_q(i + 1, s, 2)
                if front:
                    split_probs(i, s, 2, 2)
                    split_probs(i, s, 3, 0)
                if next_:
                    split_q(i + 1, s, 3)
                if front:
                    split_probs(i, s, 3, 1)
                    split_probs(i, s, 3, 2)

            steps(act, step)

        @block.gpsimd
        def _(pool):
            def root(i, use):
                n = LN.index(use) % 2
                pool.wait_ge(var_eps, ln_count(i, use))
                nc.gpsimd.tensor_tensor(rstd[:, n:n + 1], ve[:, n:n + 1], half_power[:], ALU.pow).then_inc(rstd_ready, 1)

            def normalize_probs(i, t, h):
                pool.wait_ge(totalled, nth(i, NT, t))
                pool.wait_ge(exped, nth(i, NT * XH, t * XH + XH - 1))
                heads = XH // 2
                p = probs[:, t % 2, h * heads * KEYS:(h + 1) * heads * KEYS].rearrange("p (j k) -> p j k", j=heads)
                nc.gpsimd.tensor_tensor(p, p, per_total[:, t % 2, h * heads:(h + 1) * heads].unsqueeze(2)
                                        .to_broadcast([P, heads, KEYS]), ALU.mult).then_inc(normed, 1)

            def bias_residual(i, t):
                if t == 0:
                    pool.wait_ge(res1_loaded, nth(i, 1, 0) * 16)
                nc.gpsimd.tensor_tensor(res1[:, t, :], res1[:, t, :], bias_o[:], ALU.add).then_inc(res1_ready, 1)

            def bias_x2(i, s, t):
                pool.wait_ge(x2_ready, nth(i - 1, NT, t))
                if t >= 2:
                    pool.wait_ge(freed, s.emptied(f"F{t - 2}"))
                nc.gpsimd.tensor_tensor(res2[:, t % 2, :], x2[:, t % 2, :], bias_f[:], ALU.add).then_inc(res2_ready, 1)

            def step(i, back, front, next_):
                s = Shared(i, back, front, next_)
                if back:
                    bias_residual(i - 1, 0)
                    bias_residual(i - 1, 1)
                    bias_residual(i - 1, 2)
                    bias_residual(i - 1, 3)
                if front:
                    normalize_probs(i, 0, 0)
                    normalize_probs(i, 0, 1)
                if back:
                    root(i, "O0")
                    bias_x2(i, s, 0)
                if front:
                    normalize_probs(i, 1, 0)
                if back:
                    root(i, "O1")
                if front:
                    normalize_probs(i, 1, 1)
                if back:
                    bias_x2(i, s, 1)
                    root(i, "O2")
                    bias_x2(i, s, 2)
                    root(i, "F0")
                if front:
                    normalize_probs(i, 2, 0)
                    normalize_probs(i, 2, 1)
                if back:
                    root(i, "O3")
                    bias_x2(i, s, 3)
                    root(i, "F1")
                    root(i, "F2")
                if front:
                    normalize_probs(i, 3, 0)
                    normalize_probs(i, 3, 1)
                if back:
                    root(i, "F3")

            steps(pool, step)

        @block.vector
        def _(dve):
            nc.vector.memset(masked[:], MASKED).then_inc(masked_set, 1)
            for tile in (*k_block, *v_block):
                nc.vector.memset(tile[:].bitcast(F32), 0.0).then_inc(blocks_cleared, 1)
            dve.wait_ge(masked_set, 1)

            def remainder(s, use, hi_ready, count, hi, lo, psum):
                dve.wait_ge(hi_ready, count)
                nc.vector.tensor_tensor(lo, psum, hi.bitcast(F32), ALU.subtract).then_inc(freed, 1)

            def split_x1(i, s, c):
                remainder(s, f"X{c}", x1T_hi, nth(i, NC, c), x1T[0][:, c, :], x1T[1][:, c, :],
                          shared_ps[s.bank(f"X{c}")][:])

            def biased_remainder(hi_ready, count, hi, lo, psum, bias):
                dve.wait_ge(hi_ready, count)
                nc.vector.scalar_tensor_tensor(out=lo, in0=psum, scalar=bias, in1=hi.bitcast(F32), op0=ALU.add,
                                               op1=ALU.subtract).then_inc(freed, 1)

            def split_q(i, s, c):
                biased_remainder(q_hi, nth(i, NC, c), qT[0][:, c, :], qT[1][:, c, :], shared_ps[s.bank(f"Q{c}")][:],
                                 bias_q[:, c:c + 1])

            def split_o(i, s, g):
                biased_remainder(oT_hi, nth(i, NC, g), oT[0][:, g, :], oT[1][:, g, :], shared_ps[s.bank(f"V{g}")][:],
                                 bias_v[:, g:g + 1])

            def split_x2(i, s, t):
                remainder(s, f"T{t}", x2T_hi, nth(i - 1, NT, t), x2T[0][:], x2T[1][:],
                          shared_ps[s.bank(f"T{t}")][:].rearrange("p (c n) -> p c n", c=NC))

            def split_probs(i, s, t, c):
                size = KC[c][1]
                dve.wait_ge(turned_hi, nth(i, NT * 3, 3 * t + c))
                tok = slice(t * P, (t + 1) * P)
                nc.vector.tensor_tensor(pT[1][0:size, c, :, tok], turned_bank(s, t, c),
                                        pT[0][0:size, c, :, tok].bitcast(F32), ALU.subtract).then_inc(freed, 1)

            def find_hidden(i):
                dve.wait_ge(mask_loaded, nth(i, 1, 0) * 16)
                wait_reuse(dve, hid, i * NT * 2)
                nc.vector.tensor_scalar(hidden[:], mask[:], 0.0, None, ALU.is_equal).then_inc(hidden_ready, 1)

            def softmax_top(i, t, h):
                dve.wait_ge(scored, nth(i, NT * 2, 2 * t + h))
                dve.wait_ge(hidden_ready, nth(i, 1, 0))
                dve.sem_inc(stat_seen, 1)
                shape = [P, GROUPS // 2, GH, KEYS]
                s4 = score_ps[:, 2 * h:2 * h + 2, 0:GK].rearrange("p g (j k) -> p g j k", j=GH)
                nc.vector.copy_predicated(s4, hidden[:, t, :].unsqueeze(1).unsqueeze(1).to_broadcast(shape),
                                          masked[:].unsqueeze(1).unsqueeze(1).to_broadcast(shape)).then_inc(hid, 1)
                dve.wait_ge(hid, nth(i, NT * 2, 2 * t + h))
                wait_reuse(dve, exped, i * NT * XH + (t - 1) * XH)
                nc.vector.tensor_reduce(top[:, t % 2, h * 8:(h + 1) * 8].rearrange("p (g j) -> p g j", j=GH), s4, AX.X,
                                        ALU.max, negate=True).then_inc(topped, 1)

            def invert_totals(i, t):
                dve.wait_ge(exped, nth(i, NT * XH, t * XH + XH - 1))
                wait_reuse(dve, normed, i * NT * 2 + 2 * (t - 1))
                nc.vector.reciprocal(per_total[:, t % 2, :], total[:, t % 2, :]).then_inc(totalled, 1)

            def add(i, s, use, residual, res_ready, res_count):
                n = LN.index(use) % 2
                dve.wait_ge(filled, s.filled(use))
                dve.wait_ge(res_ready, res_count)
                if LN.index(use) < 2:
                    wait_reuse(dve, y_ready, (i - 1) * NT)
                else:
                    before = LN[LN.index(use) - 2]
                    dve.wait_ge(x2_ready if before[0] == "O" else y_ready, nth(i - 1, NT, int(before[1])))
                nc.vector.tensor_tensor(y[:, n, :], shared_ps[s.bank(use)][:], residual, ALU.add).then_inc(freed, 1)

            def measure(i, s, use):
                n = LN.index(use) % 2
                dve.wait_ge(freed, s.emptied(use))
                nc.vector.bn_stats(stats[:, n, :], y[:, n, :]).then_inc(stat_done, 1)
                dve.wait_ge(stat_done, ln_count(i, use))
                dve.sem_inc(stat_seen, 1)
                nc.vector.bn_aggr(mv[:, n, :], stats[:, n, :]).then_inc(aggr_done, 1)
                dve.wait_ge(aggr_done, ln_count(i, use))
                nc.vector.tensor_scalar(ve[:, n:n + 1], mv[:, n, 1:2], EPS, None, ALU.add).then_inc(var_eps, 1)

            def add_o(i, s, t):
                add(i, s, f"O{t}", res1[:, t, :], res1_ready, nth(i - 1, NT, t))

            def add_f(i, s, t):
                add(i, s, f"F{t}", res2[:, t % 2, :], res2_ready, nth(i - 1, NT, t))

            def normalize(i, use, target, ready):
                n = LN.index(use) % 2
                dve.wait_ge(rstd_ready, ln_count(i, use))
                nc.vector.tensor_scalar(target, y[:, n, :], mv[:, n, 0:1], rstd[:, n:n + 1], ALU.subtract,
                                        ALU.mult).then_inc(ready, 1)

            def normalize_o(i, t):
                wait_reuse(dve, res2_ready, two_back(i - 1, NT, t))
                wait_reuse(dve, x2T_hi, two_back(i - 1, NT, t))
                normalize(i, f"O{t}", x2[:, t % 2, :], x2_ready)

            def normalize_f(i, t):
                wait_reuse(dve, y_stored[t % 2], (i - 1) * 32 + 16 * (t // 2))
                normalize(i, f"F{t}", y_out[:, t % 2, :], y_ready)

            def step(i, back, front, next_):
                s = Shared(i, back, front, next_)
                if front:
                    find_hidden(i)
                    softmax_top(i, 0, 0)
                    softmax_top(i, 0, 1)
                if back:
                    split_o(i - 1, s, 0)
                if front:
                    invert_totals(i, 0)
                if back:
                    split_o(i - 1, s, 1)
                    split_o(i - 1, s, 2)
                    split_o(i - 1, s, 3)
                if front:
                    softmax_top(i, 1, 0)
                    split_probs(i, s, 0, 0)
                    softmax_top(i, 1, 1)
                if back:
                    add_o(i, s, 0)
                    measure(i, s, "O0")
                if front:
                    split_probs(i, s, 0, 1)
                    split_probs(i, s, 0, 2)
                if back:
                    normalize_o(i, 0)
                    add_o(i, s, 1)
                if front:
                    invert_totals(i, 1)
                if back:
                    measure(i, s, "O1")
                if front:
                    softmax_top(i, 2, 0)
                if back:
                    split_x2(i, s, 0)
                    normalize_o(i, 1)
                    add_o(i, s, 2)
                if front:
                    softmax_top(i, 2, 1)
                    split_probs(i, s, 1, 0)
                if back:
                    measure(i, s, "O2")
                if front:
                    split_probs(i, s, 1, 1)
                if back:
                    add_f(i, s, 0)
                    normalize_o(i, 2)
                    split_x2(i, s, 1)
                    measure(i, s, "F0")
                    add_o(i, s, 3)
                if front:
                    invert_totals(i, 2)
                if next_:
                    split_x1(i + 1, s, 0)
                if back:
                    normalize_f(i, 0)
                if next_:
                    split_x1(i + 1, s, 1)
                if back:
                    measure(i, s, "O3")
                    add_f(i, s, 1)
                    split_x2(i, s, 2)
                    normalize_o(i, 3)
                if next_:
                    split_x1(i + 1, s, 2)
                if back:
                    measure(i, s, "F1")
                if next_:
                    split_x1(i + 1, s, 3)
                if front:
                    softmax_top(i, 3, 0)
                    split_probs(i, s, 1, 2)
                if back:
                    normalize_f(i, 1)
                if front:
                    split_probs(i, s, 2, 0)
                    softmax_top(i, 3, 1)
                if back:
                    add_f(i, s, 2)
                if next_:
                    split_q(i + 1, s, 0)
                if back:
                    measure(i, s, "F2")
                if front:
                    split_probs(i, s, 2, 1)
                    invert_totals(i, 3)
                if back:
                    normalize_f(i, 2)
                if next_:
                    split_q(i + 1, s, 1)
                if back:
                    split_x2(i, s, 3)
                if next_:
                    split_q(i + 1, s, 2)
                if front:
                    split_probs(i, s, 2, 2)
                if back:
                    add_f(i, s, 3)
                    measure(i, s, "F3")
                if front:
                    split_probs(i, s, 3, 0)
                if back:
                    normalize_f(i, 3)
                if next_:
                    split_q(i + 1, s, 3)
                if front:
                    split_probs(i, s, 3, 1)
                    split_probs(i, s, 3, 2)

            steps(dve, step)


def build_attention(nc, ins, out, ident_dram, x1_dram):
    with ExitStack() as ctx:
        sb = lambda n, s, d=F32: ctx.enter_context(nc.sbuf_tensor(n, s, d))
        ident, half_power = sb("ident_b", [P, P]), sb("half_power_b", [P, 1])
        bias_q, bias_v = sb("bias_q", [P, NC]), sb("bias_v", [P, NC])
        bias_o, bias_f = sb("bias_o", [P, D]), sb("bias_f", [P, D])
        w_q, w_o, w_ffn = ([sb(f"{w}_{k}", [P, NC, D], F32R) for k in ("hi", "lo")] for w in ("w_q", "w_o", "w_ffn"))
        k_dram = nc.dram_tensor("keys_split", (2, D, B * KEYS), F32).ap()
        v_dram = nc.dram_tensor("values_split", (2, B * KEYS, D), F32).ap()
        wide = lambda b: b.rearrange("(a n) -> a n", a=1).to_broadcast([P, D])
        rows = lambda b: b.rearrange("(c p) -> p c", p=P)
        load_constants(nc, ctx, [(ident, ident_dram), (bias_q, rows(ins["b_q"])), (bias_v, rows(ins["b_v"])),
                                 (bias_o, wide(ins["b_o"])), (bias_f, wide(ins["bias"]))], [(half_power, -0.5)], "b")
        prepare_attention(nc, ins, ident, w_q, w_o, w_ffn, k_dram, v_dram, bias_v)
        attend(nc, ins, out, x1_dram, k_dram, v_dram, ident, half_power, w_q, w_o, w_ffn, bias_q, bias_v, bias_o, bias_f)


def build(nc, ins, out):
    x1_dram = nc.dram_tensor("x1_between", (B, S, D), F32).ap()
    build_mixing(nc, ins["x"], ins["w_qkv"], ins["w_out"], ins["dft_forward"], ins["dft_inverse"], ins["identity"],
                 ins["product_sign"], x1_dram)
    build_attention(nc, ins, out, ins["identity"], x1_dram)


_INS = {"x": "x", "ctx": "ctx_1024", "mask": "mask_BxSxS2_ik1", "w_qkv": "L0_attn_w_qkv", "w_out": "L0_attn_w_out",
        "W_q": "L0_xattn_W_q", "b_q": "L0_xattn_b_q", "W_k": "L0_xattn_W_k", "b_k": "L0_xattn_b_k",
        "W_v": "L0_xattn_W_v", "b_v": "L0_xattn_b_v", "W_o": "L0_xattn_W_o", "b_o": "L0_xattn_b_o",
        "kernel": "L0_ffn_kernel", "bias": "L0_ffn_bias", "a": "L0_ffn_a", "b": "L0_ffn_b"}


def _constants():
    n, k = np.arange(MIX_HD)[:, None], np.arange(1, MIX_HD // 2)[None, :]
    angle = 2 * np.pi * n * k / MIX_HD
    even, odd = (1.0 + (-1.0) ** n) / 2, (1.0 - (-1.0) ** n) / 2
    fwd, inv = np.zeros((P, 2, 256)), np.zeros((P, 2, 256))
    nf = MIX_HD // 2 - 1
    for half in range(2):
        for local in range(2):
            head = 2 * half + local
            rows = slice(local * MIX_HD, (local + 1) * MIX_HD)
            re, im = slice(head * nf, (head + 1) * nf), slice(P + head * nf, P + (head + 1) * nf)
            u, w = 4 * nf + head, P + 4 * nf + head
            fwd[rows, half, re], fwd[rows, half, im] = np.cos(angle), -np.sin(angle)
            fwd[rows, half, u], fwd[rows, half, w] = even[:, 0], odd[:, 0]
            inv[rows, half, re] = np.cos(angle) * (2 / MIX_HD)
            inv[rows, half, im] = -np.sin(angle) * (2 / MIX_HD)
            inv[rows, half, u], inv[rows, half, w] = even[:, 0] * (2 / MIX_HD), odd[:, 0] * (2 / MIX_HD)
    sign = np.ones((P, 1))
    sign[4 * nf:] = -1.0
    return {"dft_forward": fwd.astype(np.float32), "dft_inverse": inv.astype(np.float32),
            "identity": np.eye(P, dtype=np.float32), "product_sign": sign.astype(np.float32)}


def kernel(**inputs):
    import concourse.bacc as bacc
    from concourse.bass_utils import run_bass_kernel_spmd

    nc = bacc.Bacc("TRN2", target_bir_lowering=False, num_devices=1)
    arrays = {short: np.ascontiguousarray(inputs[name]) for short, name in _INS.items()}
    arrays.update(_constants())
    aps = {n: nc.dram_tensor(f"in_{n}", a.shape, mybir.dt.from_np(a.dtype), kind="ExternalInput").ap()
           for n, a in arrays.items()}
    out = nc.dram_tensor("out_0", (B, S, D), F32, kind="ExternalOutput").ap()
    build(nc, aps, out)
    r = run_bass_kernel_spmd(nc, [{f"in_{n}": a for n, a in arrays.items()}], core_ids=[0])
    return r.results[0]["out_0"]
```

```python
from contextlib import ExitStack

import numpy as np
import concourse.bass as bass
from concourse import mybir

F32 = mybir.dt.float32
F32R = mybir.dt.float32r
I32 = mybir.dt.int32
ALU = mybir.AluOpType
ACT = mybir.ActivationFunctionType
AX = mybir.AxisListType

P = 128
B, S, D = 8, 512, 512
NT = S // P
NC = D // P
MIX_HEADS, MIX_HD = 8, 64
PAIRS = 2
XH, XHD = 16, 32
KEYS = 77
GROUPS = D // P
GH = XH // GROUPS
GK = GH * KEYS
KC = [(0, 103), (103, 103), (206, 102)]
RANK = 16
EPS = 1e-5
MASKED = -1000000.0
ROUND_MAGIC = 1.5 * 2.0 ** 23
QMAX = 7.0


def nth(batch, per_batch, index):
    return batch * per_batch + (index + 1)


def two_back(batch, per_batch, index):
    return batch * per_batch + max(index - 1, 0)


def wait_reuse(eng, sem, value):
    if not isinstance(value, int) or value > 0:
        eng.wait_ge(sem, value)


def v_pieces():
    for j in range(GH):
        for c, (at, size) in enumerate(KC):
            a, b = max(j * KEYS, at), min((j + 1) * KEYS, at + size)
            if a < b:
                yield j, c, a - at, a - j * KEYS, b - a


def split_matmuls(nc, out, pieces):
    terms = [(l[a], r[b]) for l, r in pieces for a, b in ((0, 0), (1, 0), (0, 1))]
    for n, (l, r) in enumerate(terms):
        last = nc.tensor.matmul(out, l, r, start=(n == 0), stop=(n == len(terms) - 1))
    return last


def prepare(nc, ins, constants, half_power, ident, w_spec, w_back, k_dram, v_dram, ffn_dram, x_first, x_loaded, ffn,
            out_slots, w_k, w_v):
    rows = B * KEYS
    half_rows = rows // 2
    tiles = [(n * P, min(P, rows - n * P)) for n in range((rows + P - 1) // P)]
    tail, tail_rows = tiles[NC]
    with ExitStack() as ctx:
        sb = lambda n, s, d=F32: ctx.enter_context(nc.sbuf_tensor(n, s, d))
        ps = lambda n, s: ctx.enter_context(nc.psum_tensor(n, s, F32))
        sem = lambda n: ctx.enter_context(nc.semaphore(n))
        wqkv_sb, wout_sb = sb("wqkv_sb", [P, NC, 3 * D]), sb("wout_sb", [P, NC, D])
        fwd = sb("fwd_sb", [P, P])
        wT = sb("wT_sb", [P, 2, NC, P])
        ctx_tail = ffn[:, 0, :]
        inv = wqkv_sb[:, 0, 0:512].rearrange("p (h n) -> p h n", h=2)
        b_sb = wqkv_sb[0:RANK, 0, D:2 * D]
        raw_k = wout_sb[:]
        raw_v = wqkv_sb[:].rearrange("p c n -> p (c n)")[:, NC * D:2 * NC * D].rearrange("p (c n) -> p c n", c=NC)
        ctxT = [sb(f"ctxT_{k}", [P, NC, rows], F32R) for k in ("hi", "lo")]
        a_sb = ffn[:, 1, 0:NC * RANK].rearrange("p (c n) -> p c n", c=NC)
        aT = sb("aT", [RANK, D])
        bias_k = sb("bias_k", [P, NC])
        k_val = wT[:].rearrange("p a c n -> p (a c n)")[:, 0:2 * half_rows].rearrange("p (a n) -> p a n", a=2)
        out_hi, out_lo = out_slots
        SLOTS = NC
        top, top_all = sb("top", [P, 1]), sb("top_all", [P, 1])
        scale, per_scale = sb("q_scale", [P, 1]), sb("q_per_scale", [P, 1])
        turned = [ps(f"turned{n}", [P, NC * P]) for n in range(2)]
        prod = [ps(f"prod{n}", [P, D]) for n in range(2)]
        ident_loaded, constants_loaded = sem("ident_loaded"), sem("constants_loaded")
        ctx_loaded, wk_loaded, wv_loaded = sem("ctx_loaded"), sem("wk_loaded"), sem("wv_loaded")
        kernel_loaded, a_loaded, b_loaded = sem("kernel_loaded"), sem("a_loaded"), sem("b_loaded")
        fwd_loaded, qkv_loaded, out_loaded = sem("fwd_loaded"), [sem(f"qkv_loaded{r}") for r in range(NC)], sem("out_loaded")
        ctx_turned, tail_turned, ctx_hi, ctx_lo = sem("ctx_turned"), sem("tail_turned"), sem("ctx_hi"), sem("ctx_lo")
        a_turned, aT_ready, w_turned, wT_ready = sem("a_turned"), sem("aT_ready"), sem("w_turned"), sem("wT_ready")
        wk_hi_ready, wk_lo_ready, wv_hi_ready, wv_lo_ready = sem("wk_hi_ready"), sem("wk_lo_ready"), sem("wv_hi_ready"), sem("wv_lo_ready")
        prod_ready, prod_used = sem("prod_ready"), sem("prod_used")
        k_biased, k_hi_ready, k_lo_ready = sem("k_biased"), sem("k_hi_ready"), sem("k_lo_ready")
        v_hi_ready, fold_hi_ready = sem("v_hi_ready"), sem("fold_hi_ready")
        stored = [sem(f"kv_stored{n}") for n in range(SLOTS)]
        scale_ready, per_scale_ready = sem("scale_ready"), sem("per_scale_ready")
        top_ready, top_spread, quantized, merged_ready, ffn_stored = (sem("top_ready"), sem("top_spread"), sem("quantized"),
                                                                      sem("merged_ready"), sem("ffn_stored"))
        block = ctx.enter_context(nc.Block())
        by_chunk = lambda w: w.rearrange("(c p) n -> p c n", p=P)
        NKEY, NVAL = 2 * NC, len(tiles)
        GROUP = [(r, s) for r in range(NC) for s in range(3)]
        AT_V = NKEY
        AT_FOLD = AT_V + NVAL
        AT_LOW = AT_FOLD + len(GROUP)
        AT_BACK = AT_LOW + NC

        def fold_target(n):
            if n < len(GROUP):
                r, s = GROUP[n]
                return [w[:, r, s, :] for w in w_spec]
            return [w[:, n - len(GROUP), :] for w in w_back]

        def fold_place(n):
            return AT_FOLD + n if n < len(GROUP) else AT_BACK + n - len(GROUP)

        @block.sync
        def _(sp):
            flat = ins["ctx"].rearrange("b k d -> (b k) d")
            sp.dma_start(ident[:], ins["identity"]).then_inc(ident_loaded, 16)
            sp.dma_start(x_first[:], flat[0:tail, :].rearrange("(n p) d -> p n d", p=P)).then_inc(ctx_loaded, 16)
            sp.dma_start(ctx_tail[0:tail_rows, :], flat[tail:rows, :]).then_inc(ctx_loaded, 16)
            sp.dma_start(raw_k, by_chunk(ins["W_k"])).then_inc(wk_loaded, 16)
            sp.dma_start(bias_k[:], ins["b_k"].rearrange("(c p) -> p c", p=P),
                         allow_slow_non_contiguous=True).then_inc(wk_loaded, 16)
            sp.dma_start(a_sb, by_chunk(ins["a"])).then_inc(a_loaded, 16)
            sp.dma_start(raw_v, by_chunk(ins["W_v"])).then_inc(wv_loaded, 16)
            sp.dma_start(fwd[:], ins["dft_forward"]).then_inc(fwd_loaded, 16)
            sp.dma_start(wqkv_sb[:, 0, :], ins["w_qkv"][0:P, :]).then_inc(qkv_loaded[0], 16)
            for n in range(NKEY):
                c, h = n // 2, n % 2
                sp.wait_ge(k_lo_ready, n + 1)
                for part, tile in enumerate((out_hi, out_lo)):
                    sp.dma_start(k_dram[part, c * P:(c + 1) * P, h * half_rows:(h + 1) * half_rows],
                                 tile[:, n % SLOTS, 0:half_rows].bitcast(F32)).then_inc(stored[n % SLOTS], 16)
                if n == NC + 1:
                    sp.wait_ge(tail_turned, NC)
                    sp.wait_ge(a_turned, 1)
                    sp.dma_start(ffn[:], by_chunk(ins["kernel"])).then_inc(kernel_loaded, 16)
                elif 1 <= n < NC:
                    sp.wait_ge(wv_lo_ready, NC)
                    sp.dma_start(wqkv_sb[:, n, :], ins["w_qkv"][n * P:(n + 1) * P, :]).then_inc(qkv_loaded[n], 16)
            for n, (at, size) in enumerate(tiles):
                sp.wait_ge(prod_used, AT_V + n + 1)
                for part, tile in enumerate((out_hi, out_lo)):
                    sp.dma_start(v_dram[part, at:at + size, :], tile[0:size, n % SLOTS, :].bitcast(F32)).then_inc(stored[n % SLOTS], 16)
                if n == 1:
                    sp.wait_ge(wk_lo_ready, NC)
                    sp.dma_start(wout_sb[:], by_chunk(ins["w_out"])).then_inc(out_loaded, 16)
            sp.wait_ge(ctx_turned, NC)
            sp.dma_start(x_first[:], ins["x"][0].rearrange("(t p) d -> p t d", p=P)).then_inc(x_loaded, 16)
            sp.wait_ge(w_turned, 3)
            sp.dma_start(inv, ins["dft_inverse"]).then_inc(out_loaded, 16)
            sp.dma_start(b_sb, ins["b"]).then_inc(b_loaded, 16)
            for tile, src in constants:
                sp.dma_start(tile[:], src, allow_slow_non_contiguous=True).then_inc(constants_loaded, 16)
            sp.wait_ge(merged_ready, NC)
            sp.dma_start(by_chunk(ffn_dram), ffn[:]).then_inc(ffn_stored, 16)
            for n in range(SLOTS):
                sp.wait_ge(stored[n], 32 * (NKEY // SLOTS + len(range(n, NVAL, SLOTS))))
            sp.wait_ge(ffn_stored, 16)
            sp.wait_ge(constants_loaded, 16 * len(constants))

        @block.tensor
        def _(pe):
            pe.wait_ge(ident_loaded, 16)
            pe.wait_ge(ctx_loaded, 32)
            for c in range(NC):
                wait_reuse(pe, ctx_lo, 2 * (c - 1))
                for n, (at, size) in enumerate(tiles[:NC]):
                    last = nc.tensor.transpose(turned[c % 2][:, n * P:n * P + size], x_first[:, n, c * P:(c + 1) * P],
                                               ident[:])
                last.then_inc(ctx_turned, 1)
                nc.tensor.transpose(prod[c % 2][:, 0:tail_rows], ctx_tail[0:tail_rows, c * P:(c + 1) * P],
                                    ident[0:tail_rows, 0:tail_rows]).then_inc(tail_turned, 1)
            pe.wait_ge(a_loaded, 16)
            pe.wait_ge(ctx_lo, 2 * (NC - 1))
            for c in range(NC):
                last = nc.tensor.transpose(turned[0][0:RANK, c * P:(c + 1) * P], a_sb[:, c, :], ident[:])
            last.then_inc(a_turned, 1)
            pe.wait_ge(ctx_hi, 2 * NC)
            pe.wait_ge(ctx_lo, 2 * NC)
            pe.wait_ge(wk_hi_ready, NC)
            pe.wait_ge(wk_lo_ready, NC)
            for n in range(NKEY):
                c, h = n // 2, n % 2
                wait_reuse(pe, prod_used, n - 1)
                cols = slice(h * half_rows, (h + 1) * half_rows)
                pieces = [([w[:, k, c * P:(c + 1) * P] for w in w_k], [t[:, k, cols] for t in ctxT]) for k in range(NC)]
                split_matmuls(nc, prod[n % 2][:, 0:half_rows], pieces).then_inc(prod_ready, 1)
            pe.wait_ge(wv_hi_ready, 1)
            pe.wait_ge(wv_lo_ready, NC)
            for m, (at, size) in enumerate(tiles):
                n = AT_V + m
                pe.wait_ge(prod_used, n - 1)
                pieces = [([t[:, k, at:at + size] for t in ctxT], [w[:, k, :] for w in w_v]) for k in range(NC)]
                split_matmuls(nc, prod[n % 2][0:size, :], pieces).then_inc(prod_ready, 1)

            def turn(n):
                r, s = GROUP[n]
                if s == 0:
                    pe.wait_ge(qkv_loaded[r], 16)
                wait_reuse(pe, wT_ready, n - 1)
                for c in range(NC):
                    at = s * D + c * P
                    last = nc.tensor.transpose(turned[(n + 1) % 2][:, c * P:(c + 1) * P], wqkv_sb[:, r, at:at + P], ident[:])
                last.then_inc(w_turned, 1)

            turn(0)
            pe.wait_ge(fwd_loaded, 16)
            for m in range(len(GROUP)):
                if m + 1 < len(GROUP):
                    turn(m + 1)
                n = AT_FOLD + m
                pe.wait_ge(wT_ready, m + 1)
                pe.wait_ge(prod_used, n - 1)
                for c in range(NC):
                    p, h = c // 2, c % 2
                    out = prod[n % 2][:, p * 256:(p + 1) * 256].rearrange("q (i h k) -> q i h k", i=2, h=2)[:, :, h, :]
                    last = nc.tensor.matmul(out, wT[:, m % 2, c, :], fwd[:].rearrange("q (i k) -> q i k", i=2),
                                            start=True, stop=True)
                last.then_inc(prod_ready, 1)
            pe.wait_ge(aT_ready, 1)
            pe.wait_ge(b_loaded, 16)
            for c in range(NC):
                n = AT_LOW + c
                pe.wait_ge(prod_used, n - 1)
                nc.tensor.matmul(prod[n % 2][:], aT[:, c * P:(c + 1) * P], b_sb, start=True, stop=True).then_inc(prod_ready, 1)
            pe.wait_ge(out_loaded, 32)
            for f in range(NC):
                n = AT_BACK + f
                p, im = f // 2, f % 2
                pe.wait_ge(prod_used, n - 1)
                for h in range(2):
                    last = nc.tensor.matmul(prod[n % 2][:], inv[:, h, im * P:(im + 1) * P], wout_sb[:, 2 * p + h, :],
                                            start=(h == 0), stop=(h == 1))
                last.then_inc(prod_ready, 1)

        @block.scalar
        def _(act):
            for c in range(NC):
                act.wait_ge(ctx_turned, c + 1)
                nc.scalar.activation(ctxT[0][:, c, 0:tail], turned[c % 2][:], ACT.Copy).then_inc(ctx_hi, 1)
                act.wait_ge(tail_turned, c + 1)
                nc.scalar.activation(ctxT[0][:, c, tail:rows], prod[c % 2][:, 0:tail_rows], ACT.Copy).then_inc(ctx_hi, 1)
            act.wait_ge(wk_loaded, 32)
            for c in range(NC):
                nc.scalar.activation(w_k[0][:, c, :], raw_k[:, c, :], ACT.Copy).then_inc(wk_hi_ready, 1)
            act.wait_ge(a_turned, 1)
            nc.scalar.activation(aT[:], turned[0][0:RANK, :], ACT.Copy).then_inc(aT_ready, 1)
            act.wait_ge(wv_loaded, 16)
            nc.scalar.activation(w_v[0][:], raw_v, ACT.Copy).then_inc(wv_hi_ready, 1)
            for n in range(NKEY):
                act.wait_ge(k_biased, n + 1)
                wait_reuse(act, stored[n % SLOTS], 32 * (n // SLOTS))
                nc.scalar.activation(out_hi[:, n % SLOTS, 0:half_rows], k_val[:, n % 2, :], ACT.Copy).then_inc(k_hi_ready, 1)
            for m, (at, size) in enumerate(tiles):
                act.wait_ge(prod_ready, AT_V + m + 1)
                act.wait_ge(stored[m % SLOTS], 32 * (NKEY // SLOTS + m // SLOTS))
                nc.scalar.activation(out_hi[0:size, m % SLOTS, :], prod[(AT_V + m) % 2][0:size, :], ACT.Copy).then_inc(v_hi_ready, 1)

            def copy_turned(n):
                act.wait_ge(w_turned, n + 1)
                if n >= 2:
                    act.wait_ge(prod_ready, AT_FOLD + n - 1)
                nc.scalar.activation(wT[:, n % 2, :, :], turned[(n + 1) % 2][:].rearrange("p (c n) -> p c n", c=NC),
                                     ACT.Copy).then_inc(wT_ready, 1)

            act.wait_ge(k_lo_ready, NKEY)
            copy_turned(0)
            for m in range(len(GROUP) + NC):
                if m + 1 < len(GROUP):
                    copy_turned(m + 1)
                n = fold_place(m)
                act.wait_ge(prod_ready, n + 1)
                nc.scalar.activation(fold_target(m)[0], prod[n % 2][:], ACT.Copy).then_inc(fold_hi_ready, 1)

        @block.gpsimd
        def _(pool):
            nc.gpsimd.memset(half_power[:], -0.5)
            pool.wait_ge(wv_loaded, 16)
            pool.wait_ge(wv_hi_ready, 1)
            for c in range(NC):
                nc.gpsimd.tensor_tensor(w_v[1][:, c, :], raw_v[:, c, :], w_v[0][:, c, :].bitcast(F32),
                                        ALU.subtract).then_inc(wv_lo_ready, 1)
            pool.wait_ge(top_ready, 1)
            nc.gpsimd.partition_all_reduce(top_all[:], top[:], P, bass.bass_isa.ReduceOp.max).then_inc(top_spread, 1)

        @block.vector
        def _(dve):
            for c in range(NC):
                dve.wait_ge(ctx_hi, 2 * c + 1)
                nc.vector.tensor_tensor(ctxT[1][:, c, 0:tail], turned[c % 2][:], ctxT[0][:, c, 0:tail].bitcast(F32),
                                        ALU.subtract).then_inc(ctx_lo, 1)
                dve.wait_ge(ctx_hi, 2 * c + 2)
                nc.vector.tensor_tensor(ctxT[1][:, c, tail:rows], prod[c % 2][:, 0:tail_rows],
                                        ctxT[0][:, c, tail:rows].bitcast(F32), ALU.subtract).then_inc(ctx_lo, 1)
            dve.wait_ge(wk_loaded, 32)
            for c in range(NC):
                dve.wait_ge(wk_hi_ready, c + 1)
                nc.vector.tensor_tensor(w_k[1][:, c, :], raw_k[:, c, :], w_k[0][:, c, :].bitcast(F32),
                                        ALU.subtract).then_inc(wk_lo_ready, 1)

            def bias_keys(n):
                dve.wait_ge(prod_ready, n + 1)
                wait_reuse(dve, k_lo_ready, n - 1)
                nc.vector.tensor_scalar(k_val[:, n % 2, :], prod[n % 2][:, 0:half_rows], bias_k[:, n // 2:n // 2 + 1],
                                        float(XHD) ** -0.5, ALU.add, ALU.mult).then_inc(k_biased, 1)
                dve.wait_ge(k_biased, n + 1)
                dve.sem_inc(prod_used, 1)

            bias_keys(0)
            for n in range(NKEY):
                if n + 1 < NKEY:
                    bias_keys(n + 1)
                dve.wait_ge(k_hi_ready, n + 1)
                wait_reuse(dve, stored[n % SLOTS], 32 * (n // SLOTS))
                nc.vector.tensor_tensor(out_lo[:, n % SLOTS, 0:half_rows], k_val[:, n % 2, :], out_hi[:, n % SLOTS, 0:half_rows].bitcast(F32),
                                        ALU.subtract).then_inc(k_lo_ready, 1)
            for m, (at, size) in enumerate(tiles):
                dve.wait_ge(v_hi_ready, m + 1)
                dve.wait_ge(stored[m % SLOTS], 32 * (NKEY // SLOTS + m // SLOTS))
                nc.vector.tensor_tensor(out_lo[0:size, m % SLOTS, :], prod[(AT_V + m) % 2][0:size, :],
                                        out_hi[0:size, m % SLOTS, :].bitcast(F32), ALU.subtract).then_inc(prod_used, 1)
                if m == 3:
                    dve.wait_ge(kernel_loaded, 16)
                    nc.vector.tensor_reduce(top[:], ffn[:].rearrange("p c n -> p (c n)"), AX.X, ALU.max,
                                            apply_absolute_value=True).then_inc(top_ready, 1)
                if m == 4:
                    dve.wait_ge(top_spread, 1)
                    nc.vector.tensor_scalar(scale[:], top_all[:], 1.0 / QMAX, None, ALU.mult).then_inc(scale_ready, 1)
                    dve.wait_ge(scale_ready, 1)
                    nc.vector.reciprocal(per_scale[:], scale[:]).then_inc(per_scale_ready, 1)

            def split_folded(m):
                dve.wait_ge(fold_hi_ready, m + 1)
                hi, lo = fold_target(m)
                nc.vector.tensor_tensor(lo, prod[fold_place(m) % 2][:], hi.bitcast(F32), ALU.subtract).then_inc(prod_used, 1)

            for m in range(len(GROUP)):
                split_folded(m)
                if m == 0:
                    dve.wait_ge(per_scale_ready, 1)
                    nc.vector.tensor_scalar(ffn[:], ffn[:], per_scale[:], ROUND_MAGIC, ALU.mult, ALU.add).then_inc(quantized, 1)
                if m == 4:
                    dve.wait_ge(quantized, 1)
                    nc.vector.tensor_scalar(ffn[:], ffn[:], ROUND_MAGIC, -QMAX - 1, ALU.subtract, ALU.max).then_inc(quantized, 1)
                if m == 8:
                    dve.wait_ge(quantized, 2)
                    nc.vector.tensor_scalar(ffn[:], ffn[:], QMAX, scale[:], ALU.min, ALU.mult).then_inc(quantized, 1)
            dve.wait_ge(quantized, 3)
            for c in range(NC):
                n = AT_LOW + c
                dve.wait_ge(prod_ready, n + 1)
                nc.vector.tensor_tensor(ffn[:, c, :], prod[n % 2][:], ffn[:, c, :], ALU.add).then_inc(merged_ready, 1)
                dve.wait_ge(merged_ready, c + 1)
                dve.sem_inc(prod_used, 1)
            for m in range(NC):
                split_folded(len(GROUP) + m)


class Handover:

    def __init__(self, nc, ctx):
        sb = lambda n, s, d=F32: ctx.enter_context(nc.sbuf_tensor(n, s, d))
        sem = lambda n: ctx.enter_context(nc.semaphore(n))
        self.x_first, self.x1 = sb("x_tok0", [P, NT, D]), sb("x1", [P, NT, D])
        self.xT = [[sb(f"xT_{k}{n}", [P, NC, S], F32R) for k in ("hi", "lo")] for n in range(2)]
        self.qT = [sb(f"qT_{k}", [P, NC, S], F32R) for k in ("hi", "lo")]
        flat = [t[:].rearrange("p c n -> p (c n)") for t in self.xT[1]]
        keys_end = GROUPS * GK
        self.k_block = [f[:, 0:keys_end].rearrange("p (g n) -> p g n", g=GROUPS) for f in flat]
        at = (keys_end + 15) // 16 * 16
        self.x2T = [f[:, at:at + NC * P].rearrange("p (c n) -> p c n", c=NC) for f in flat]
        self.mask, self.mask_loaded = sb("mask", [P, NT, KEYS], I32), sem("mask_loaded")
        self.x_loaded, self.x1_loaded = sem("x_loaded0"), sem("x1_loaded")
        self.x1_stored = [sem(f"x1_stored{n}") for n in range(2)]
        self.keys_cleared, self.k_loaded = sem("keys_cleared"), sem("k_loaded")
        self.filled, self.freed = sem("shared_filled"), sem("shared_freed")
        self.x1T_hi, self.q_hi = sem("x1T_hi_ready"), sem("q_hi_ready")


def load_keys(sp, k_dram, hand, i):
    for part in range(2):
        src = k_dram[part].rearrange("(g j d) r -> j d g r", j=GH, d=XHD)
        for j in range(GH):
            sp.dma_start(hand.k_block[part][j * XHD:(j + 1) * XHD, :, j * KEYS:(j + 1) * KEYS].bitcast(F32),
                         src[j][:, :, bass.ds(i * KEYS, KEYS)]).then_inc(hand.k_loaded, 16)


def mix_tokens(nc, x, x1_dram, k_dram, mask_dram, ident, sigma, w_spec, w_back, half_power, w_q_dram, w_q, bias_q, hand):
    x1_next, x1_loaded, x1_stored = hand.x1, hand.x1_loaded, hand.x1_stored
    x1T, qT = hand.xT[0], hand.qT
    with ExitStack() as ctx:
        sb = lambda n, s, d=F32: ctx.enter_context(nc.sbuf_tensor(n, s, d))
        ps = lambda n, s: ctx.enter_context(nc.psum_tensor(n, s, F32))
        sem = lambda n: ctx.enter_context(nc.semaphore(n))
        x_tok = [hand.x_first, sb("x_tok1", [P, NT, D])]
        x_res = sb("x_res", [P, NT, D])
        xT = hand.xT
        v_sb = sb("v_sb", [P, 2, S])
        kv = sb("kv_prod", [P, 4, S])
        state = sb("state", [P, 2, S])
        qs = sb("qs_prod", [P, 4, S])
        vals = sb("vals", [P, 2, S])
        valsT = qT
        r_sb = sb("mix_r", [P, 2, D])
        x1_sb = sb("mix_x1", [P, 2, D])
        stats = sb("mix_stats", [P, 2, 6])
        mv = sb("mix_mv", [P, 2, 2])
        ve = sb("mix_ve", [P, 2])
        rstd = sb("mix_rstd", [P, 2])
        v_ps = [ps(f"v_ps{h}", [P, S]) for h in range(2)]
        k_ps = [ps(f"k_ps{h}", [P, S]) for h in range(2)]
        q_ps = [ps(f"q_ps{h}", [P, S]) for h in range(2)]
        xT_ps = ps("xT_ps", [P, S])
        out_ps = ps("out_ps", [P, D])
        first_banks = [xT_ps, k_ps[0], k_ps[1], q_ps[0]]
        next_banks = [k_ps[0], k_ps[1], q_ps[0], q_ps[1]]
        last_banks = [out_ps, xT_ps, v_ps[0], v_ps[1]]
        x_loaded = [hand.x_loaded, sem("x_loaded1")]
        xres_loaded = sem("xres_loaded")
        wq_loaded, wq_hi, wq_lo = sem("wq_loaded"), sem("wq_hi"), sem("wq_lo")
        xT_filled, x_hi, x_lo = sem("xT_filled"), sem("x_hi"), sem("x_lo")
        v_filled, k_filled, q_filled, out_filled = sem("v_filled"), sem("k_filled"), sem("q_filled"), sem("out_filled")
        v_copied, kv_done, scanned, qs_done = sem("v_copied"), sem("kv_done"), sem("scanned"), sem("qs_done")
        vals_summed, vals_hi, vals_lo = sem("vals_summed"), sem("vals_hi"), sem("vals_lo")
        r_added, r_stats, r_aggr = sem("r_added"), sem("r_stats"), sem("r_aggr")
        var_eps, rstd_ready, x1_ready = sem("var_eps"), sem("rstd_ready"), sem("x1_ready")
        stats_seen = sem("stats_seen")
        block = ctx.enter_context(nc.Block())

        def steps(eng, step):
            step(1, 1, True, True)
            with eng.Fori(2, B - 2, 2) as i:
                step(i, 0, True, True)
                step(i + 1, 1, True, True)
            step(B - 2, 0, True, True)
            step(B - 1, 1, False, True)

        @block.sync
        def _(sp):
            def load_x(i, half, reuse):
                if reuse:
                    sp.wait_ge(xT_filled, nth(i - 2, NC, NC - 1))
                sp.dma_start(x_tok[half][:], x[i].rearrange("(t p) d -> p t d", p=P)).then_inc(x_loaded[half], 16)

            def load_residual(i):
                wait_reuse(sp, r_added, nth(i - 1, NT, NT - 1))
                sp.dma_start(x_res[:], x[i].rearrange("(t p) d -> p t d", p=P)).then_inc(xres_loaded, 16)

            def store(i):
                for t in range(NT):
                    sp.wait_ge(x1_ready, nth(i, NT, t))
                    sp.dma_start(x1_dram[i, t * P:(t + 1) * P, :], x1_sb[:, t % 2, :]).then_inc(x1_stored[t % 2], 16)

            def finish(i):
                load_residual(i)
                store(i)

            load_x(1, 1, False)
            sp.dma_start(x1_next[:], w_q_dram.rearrange("(c p) n -> p c n", p=P)).then_inc(wq_loaded, 16)
            load_x(2, 0, True)
            load_x(3, 1, True)
            finish(0)
            with sp.Fori(2, B - 3, 2) as i:
                load_x(i + 2, 0, True)
                finish(i - 1)
                load_x(i + 3, 1, True)
                finish(i)
            for i in range(B - 3, B - 1):
                finish(i)
            sp.wait_ge(wq_lo, NC)
            for n in range(2):
                sp.wait_ge(x1_stored[n], 16 * NT // 2)
            sp.dma_start(x1_next[:], x1_dram[0].rearrange("(t p) d -> p t d", p=P)).then_inc(x1_loaded, 16)
            sp.dma_start(hand.mask[:], mask_dram[0].rearrange("(t p) k -> p t k", p=P)).then_inc(hand.mask_loaded, 16)
            load_residual(B - 1)
            sp.wait_ge(hand.keys_cleared, 2)
            load_keys(sp, k_dram, hand, 0)
            store(B - 1)

        @block.tensor
        def _(pe):
            def turn(i, half, c, bank=xT_ps):
                if c == 0:
                    pe.wait_ge(x_loaded[half], i_loads(i, half))
                if bank is xT_ps:
                    wait_reuse(pe, x_lo, nth(i, NC, c - 1))
                for t in range(NT):
                    last = nc.tensor.transpose(bank[:, t * P:(t + 1) * P], x_tok[half][:, t, c * P:(c + 1) * P], ident[:])
                last.then_inc(xT_filled, 1)

            def i_loads(i, half):
                return (i - half) * 8 + 16

            def project(i, half, s, p, h):
                bank, filled, free, done = {
                    2: (v_ps, v_filled, v_copied, i * 4 + (2 * p + h - 1)),
                    1: (k_ps, k_filled, kv_done, i * 8 + (4 * p + 2 * h - 2)),
                    0: (q_ps, q_filled, qs_done, i * 8 + (4 * p + 2 * h - 2)),
                }[s]
                if p == 0 and s == 2 and h == 0:
                    pe.wait_ge(x_lo, nth(i, NC, NC - 1))
                    pe.wait_ge(x_hi, nth(i, NC, NC - 1))
                wait_reuse(pe, free, done)
                at = p * 256 + h * P
                pieces = [([w[:, c, s, at:at + P] for w in w_spec], [t[:, c, :] for t in xT[half]]) for c in range(NC)]
                split_matmuls(nc, bank[h][:], pieces).then_inc(filled, 1)

            def project_back(i, t):
                if t == 0:
                    pe.wait_ge(vals_lo, nth(i, 4, 3))
                    pe.wait_ge(vals_hi, nth(i, 4, 3))
                wait_reuse(pe, r_added, nth(i, NT, t - 1))
                tok = slice(t * P, (t + 1) * P)
                pieces = [([v[:, c, tok] for v in valsT], [w[:, c, :] for w in w_back]) for c in range(NC)]
                split_matmuls(nc, out_ps[:], pieces).then_inc(out_filled, 1)

            def step(i, half, has_next, has_last):
                project(i, half, 2, 0, 0)
                project(i, half, 2, 0, 1)
                for c, (s, h) in enumerate([(1, 0), (1, 1), (0, 0)]):
                    if has_next:
                        turn(i + 1, 1 - half, c)
                    project(i, half, s, 0, h)
                if has_next:
                    turn(i + 1, 1 - half, 3)
                if has_last:
                    project_back(i - 1, 0)
                project(i, half, 0, 0, 1)
                if has_last:
                    project_back(i - 1, 1)
                project(i, half, 2, 1, 0)
                if has_last:
                    project_back(i - 1, 2)
                project(i, half, 2, 1, 1)
                if has_last:
                    project_back(i - 1, 3)
                for s, h in [(1, 0), (1, 1), (0, 0), (0, 1)]:
                    project(i, half, s, 1, h)

            for c in range(NC):
                turn(0, 0, c, first_banks[c])
            step(0, 0, True, False)
            steps(pe, step)
            for half in range(PAIRS):
                pe.wait_ge(vals_lo, nth(B - 1, 4, 2 * half + 1))
                pe.wait_ge(vals_hi, nth(B - 1, 4, 2 * half + 1))
                for t in range(NT):
                    if half == 0:
                        if t == 0:
                            pe.wait_ge(r_added, nth(B - 2, NT, NT - 1))
                        if t == 2:
                            pe.wait_ge(v_copied, nth(B - 1, 4, 3))
                    tok = slice(t * P, (t + 1) * P)
                    chunks = (2 * half, 2 * half + 1)
                    terms = [(valsT[a][:, c, tok], w_back[b][:, c, :]) for c in chunks for a, b in ((0, 0), (1, 0), (0, 1))]
                    for n, (l, r) in enumerate(terms):
                        last = nc.tensor.matmul(last_banks[t][:], l, r, start=(half == 0 and n == 0),
                                                stop=(half == 1 and n == len(terms) - 1))
                    if half == 1:
                        last.then_inc(out_filled, 1)
                if half == 0:
                    pe.wait_ge(x1_loaded, 16)
                    pe.wait_ge(kv_done, nth(B - 1, 8, 7))
                    pe.wait_ge(qs_done, nth(B - 1, 8, 7))
                    for c in range(NC):
                        for t in range(NT):
                            last = nc.tensor.transpose(next_banks[c][:, t * P:(t + 1) * P],
                                                       x1_next[:, t, c * P:(c + 1) * P], ident[:])
                        last.then_inc(hand.filled, 1)
            pe.wait_ge(hand.x1T_hi, NC)
            pe.wait_ge(hand.freed, NC)
            for c in range(NC):
                pieces = [([w[:, k, c * P:(c + 1) * P] for w in w_q], [x[:, k, :] for x in x1T]) for k in range(NC)]
                split_matmuls(nc, next_banks[c][:], pieces).then_inc(hand.filled, 1)

        @block.scalar
        def _(act):
            def split_x(i, half, c, bank=xT_ps):
                act.wait_ge(xT_filled, nth(i, NC, c))
                nc.scalar.activation(xT[half][0][:, c, :], bank[:], ACT.Copy).then_inc(x_hi, 1)

            def copy_v(i, p, h):
                act.wait_ge(v_filled, nth(i, 4, 2 * p + h))
                wait_reuse(act, kv_done, i * 8 + 4 * p)
                nc.scalar.activation(v_sb[:, h, :], v_ps[h][:], ACT.Copy).then_inc(v_copied, 1)

            def split_vals(i, p, h):
                act.wait_ge(vals_summed, nth(i, 4, 2 * p + h))
                if p == 0 and h == 0:
                    wait_reuse(act, out_filled, i * NT)
                nc.scalar.activation(valsT[0][:, 2 * p + h, :], vals[:, h, :], ACT.Copy).then_inc(vals_hi, 1)

            def step(i, half, has_next, has_last):
                copy_v(i, 0, 0)
                copy_v(i, 0, 1)
                if has_next:
                    for c in range(NC):
                        split_x(i + 1, 1 - half, c)
                copy_v(i, 1, 0)
                copy_v(i, 1, 1)
                for p in range(PAIRS):
                    for h in range(2):
                        split_vals(i, p, h)

            for c in range(NC):
                split_x(0, 0, c, first_banks[c])
            step(0, 0, True, False)
            act.wait_ge(wq_loaded, 16)
            nc.scalar.activation(w_q[0][:], x1_next[:], ACT.Copy).then_inc(wq_hi, 1)
            steps(act, step)
            for c in range(NC):
                act.wait_ge(hand.filled, c + 1)
                nc.scalar.activation(x1T[0][:, c, :], next_banks[c][:], ACT.Copy).then_inc(hand.x1T_hi, 1)
            for c in range(NC):
                act.wait_ge(hand.filled, NC + c + 1)
                nc.scalar.activation(qT[0][:, c, :], next_banks[c][:], ACT.Identity,
                                     bias=bias_q[:, c:c + 1]).then_inc(hand.q_hi, 1)

        @block.gpsimd
        def _(pool):
            def root(i, t):
                pool.wait_ge(var_eps, nth(i, NT, t))
                wait_reuse(pool, x1_ready, two_back(i, NT, t))
                nc.gpsimd.tensor_tensor(rstd[:, t % 2:t % 2 + 1], ve[:, t % 2:t % 2 + 1], half_power[:],
                                        ALU.pow).then_inc(rstd_ready, 1)

            def sum_vals(i, p, h):
                pool.wait_ge(qs_done, nth(i, 8, 4 * p + 3))
                wait_reuse(pool, vals_lo, i * 4 + (2 * p + h - 1))
                wait_reuse(pool, vals_hi, i * 4 + (2 * p + h - 1))
                nc.gpsimd.tensor_tensor(vals[:, h, :], qs[:, 2 * h, :], qs[:, 2 * h + 1, :],
                                        ALU.subtract if h else ALU.add).then_inc(vals_summed, 1)

            def remainder(i, p, h):
                pool.wait_ge(vals_hi, nth(i, 4, 2 * p + h))
                pool.wait_ge(vals_summed, nth(i, 4, 2 * p + h))
                nc.gpsimd.tensor_tensor(valsT[1][:, 2 * p + h, :], vals[:, h, :],
                                        valsT[0][:, 2 * p + h, :].bitcast(F32), ALU.subtract).then_inc(vals_lo, 1)

            def step(i, half, has_next, has_last):
                if has_last:
                    root(i - 1, 0)
                sum_vals(i, 0, 0)
                if has_last:
                    root(i - 1, 1)
                sum_vals(i, 0, 1)
                if has_last:
                    root(i - 1, 2)
                    root(i - 1, 3)
                remainder(i, 0, 0)
                remainder(i, 0, 1)
                sum_vals(i, 1, 0)
                sum_vals(i, 1, 1)
                remainder(i, 1, 0)
                remainder(i, 1, 1)

            step(0, 0, True, False)
            pool.wait_ge(wq_hi, 1)
            pool.wait_ge(wq_loaded, 16)
            for c in range(NC):
                nc.gpsimd.tensor_tensor(w_q[1][:, c, :], x1_next[:, c, :], w_q[0][:, c, :].bitcast(F32),
                                        ALU.subtract).then_inc(wq_lo, 1)
            steps(pool, step)
            pool.wait_ge(q_filled, nth(B - 1, 4, 3))
            for tile in hand.k_block:
                nc.gpsimd.memset(tile.bitcast(F32), 0.0).then_inc(hand.keys_cleared, 1)
            for t in range(NT):
                root(B - 1, t)

        @block.vector
        def _(dve):
            def split_x(i, half, c, bank=xT_ps):
                dve.wait_ge(x_hi, nth(i, NC, c))
                nc.vector.tensor_tensor(xT[half][1][:, c, :], bank[:], xT[half][0][:, c, :].bitcast(F32),
                                        ALU.subtract).then_inc(x_lo, 1)

            def times_k(i, p, h):
                dve.wait_ge(k_filled, nth(i, 4, 2 * p + h))
                dve.wait_ge(v_copied, nth(i, 4, 2 * p + 1))
                wait_reuse(dve, scanned, i * 4 + 2 * p)
                if h == 0:
                    nc.vector.tensor_tensor(kv[:, 0, :], k_ps[0][:], v_sb[:, 0, :], ALU.mult).then_inc(kv_done, 1)
                    nc.vector.tensor_tensor(kv[:, 1, :], k_ps[0][:], v_sb[:, 1, :], ALU.mult).then_inc(kv_done, 1)
                else:
                    nc.vector.scalar_tensor_tensor(out=kv[:, 2, :], in0=k_ps[1][:], scalar=sigma[:], in1=v_sb[:, 1, :],
                                                   op0=ALU.mult, op1=ALU.mult).then_inc(kv_done, 1)
                    nc.vector.tensor_tensor(kv[:, 3, :], k_ps[1][:], v_sb[:, 0, :], ALU.mult).then_inc(kv_done, 1)

            def scan(i, p):
                dve.wait_ge(kv_done, nth(i, 8, 4 * p + 3))
                wait_reuse(dve, qs_done, i * 8 + 4 * p)
                nc.vector.tensor_tensor_scan(state[:, 0, :], kv[:, 0, :], kv[:, 2, :], 0.0, ALU.add,
                                             ALU.subtract).then_inc(scanned, 1)
                nc.vector.tensor_tensor_scan(state[:, 1, :], kv[:, 1, :], kv[:, 3, :], 0.0, ALU.add,
                                             ALU.add).then_inc(scanned, 1)

            def times_q(i, p, h):
                dve.wait_ge(q_filled, nth(i, 4, 2 * p + h))
                dve.wait_ge(scanned, nth(i, 4, 2 * p + 1))
                wait_reuse(dve, vals_summed, i * 4 + 2 * p)
                if h == 0:
                    nc.vector.tensor_tensor(qs[:, 0, :], q_ps[0][:], state[:, 0, :], ALU.mult).then_inc(qs_done, 1)
                    nc.vector.tensor_tensor(qs[:, 2, :], q_ps[0][:], state[:, 1, :], ALU.mult).then_inc(qs_done, 1)
                else:
                    nc.vector.tensor_tensor(qs[:, 1, :], q_ps[1][:], state[:, 1, :], ALU.mult).then_inc(qs_done, 1)
                    nc.vector.scalar_tensor_tensor(out=qs[:, 3, :], in0=q_ps[1][:], scalar=sigma[:], in1=state[:, 0, :],
                                                   op0=ALU.mult, op1=ALU.mult).then_inc(qs_done, 1)

            def add_residual(i, t, bank=out_ps):
                dve.wait_ge(out_filled, nth(i, NT, t))
                if t == 0:
                    dve.wait_ge(xres_loaded, nth(i, 1, 0) * 16)
                wait_reuse(dve, x1_ready, two_back(i, NT, t))
                k = t % 2
                nc.vector.tensor_tensor(r_sb[:, k, :], bank[:], x_res[:, t, :], ALU.add).then_inc(r_added, 1)
                dve.wait_ge(r_added, nth(i, NT, t))
                nc.vector.bn_stats(stats[:, k, :], r_sb[:, k, :]).then_inc(r_stats, 1)
                dve.wait_ge(r_stats, nth(i, NT, t))
                dve.sem_inc(stats_seen, 1)
                nc.vector.bn_aggr(mv[:, k, :], stats[:, k, :]).then_inc(r_aggr, 1)
                dve.wait_ge(r_aggr, nth(i, NT, t))
                wait_reuse(dve, rstd_ready, two_back(i, NT, t))
                nc.vector.tensor_scalar(ve[:, k:k + 1], mv[:, k, 1:2], EPS, None, ALU.add).then_inc(var_eps, 1)

            def normalize(i, t):
                dve.wait_ge(rstd_ready, nth(i, NT, t))
                wait_reuse(dve, x1_stored[t % 2], i * 32 + 16 * (t // 2))
                k = t % 2
                nc.vector.tensor_scalar(x1_sb[:, k, :], r_sb[:, k, :], mv[:, k, 0:1], rstd[:, k:k + 1],
                                        ALU.subtract, ALU.mult).then_inc(x1_ready, 1)

            def step(i, half, has_next, has_last):
                def turned(c):
                    if has_next:
                        split_x(i + 1, 1 - half, c)

                turned(0)
                times_k(i, 0, 0)
                turned(1)
                times_k(i, 0, 1)
                turned(2)
                scan(i, 0)
                turned(3)
                times_q(i, 0, 0)
                if has_last:
                    add_residual(i - 1, 0)
                times_q(i, 0, 1)
                if has_last:
                    add_residual(i - 1, 1)
                    normalize(i - 1, 0)
                    normalize(i - 1, 1)
                    add_residual(i - 1, 2)
                    add_residual(i - 1, 3)
                    normalize(i - 1, 2)
                    normalize(i - 1, 3)
                times_k(i, 1, 0)
                times_k(i, 1, 1)
                scan(i, 1)
                times_q(i, 1, 0)
                times_q(i, 1, 1)

            for c in range(NC):
                split_x(0, 0, c, first_banks[c])
            step(0, 0, True, False)
            steps(dve, step)
            for c in range(NC):
                dve.wait_ge(hand.x1T_hi, c + 1)
                nc.vector.tensor_tensor(x1T[1][:, c, :], next_banks[c][:], x1T[0][:, c, :].bitcast(F32),
                                        ALU.subtract).then_inc(hand.freed, 1)

            def split_q(c):
                dve.wait_ge(hand.q_hi, c + 1)
                nc.vector.scalar_tensor_tensor(out=qT[1][:, c, :], in0=next_banks[c][:], scalar=bias_q[:, c:c + 1],
                                               in1=qT[0][:, c, :].bitcast(F32), op0=ALU.add,
                                               op1=ALU.subtract).then_inc(hand.freed, 1)

            add_residual(B - 1, 0, last_banks[0])
            add_residual(B - 1, 1, last_banks[1])
            normalize(B - 1, 0)
            add_residual(B - 1, 2, last_banks[2])
            normalize(B - 1, 1)
            split_q(0)
            add_residual(B - 1, 3, last_banks[3])
            normalize(B - 1, 2)
            split_q(1)
            normalize(B - 1, 3)
            split_q(2)
            split_q(3)


BACK, FRONT, NEXT = "VOTF", "P", "XQ"
RING = 4
BANK_ORDER = ["V0", "V1", "V2", "V3", "O0", "P00", "O1", "P01", "O2", "T0", "P02", "F0", "P10", "P11", "T1",
              "O3", "X0", "X1", "X2", "F1", "X3", "T2", "P12", "Q0", "F2", "P20", "P21", "Q1", "T3", "Q2",
              "P22", "F3", "P30", "P31", "P32", "Q3"]

START_ORDER = ["P00", "P01", "P02", "X0", "X1", "X2", "X3", "P10", "P11", "P12", "Q0", "P20", "P21", "Q1",
               "P22", "Q2", "P30", "P31", "P32", "Q3"]
CLOSING_ORDER = ["V0", "V1", "V2", "V3", "O0", "P00", "O1", "P01", "P02", "T0", "O2", "P10", "P11", "P12",
                 "F0", "T1", "O3", "P20", "P21", "F1", "T2", "P22", "P30", "F2", "T3", "P31", "P32", "F3"]
END_ORDER = ["V0", "V1", "V2", "V3", "O0", "O1", "O2", "T0", "O3", "T1", "F0", "T2", "F1", "T3", "F2", "F3"]

class Shared:

    def __init__(self, i, back, front, next_):
        self.order = self.uses(back, front, next_)
        self.norms = [u for u in self.order if u[0] in "OF"]
        count = lambda kinds: sum(u[0] in kinds for u in BANK_ORDER)
        if isinstance(i, int):
            nexts, fronts, backs = min(i + 1, B), min(max(i, 0), B), max(i - 1, 0)
            self.before = count(NEXT) * nexts + count(FRONT) * fronts + count(BACK) * backs
            self.filled_before = self.before - count(FRONT) * fronts
            self.previous = self.uses(i - 1 >= 1, 0 <= i - 1 <= B - 1, i - 1 <= B - 2)
        else:
            self.before = i * len(BANK_ORDER) - (count(BACK) - count(NEXT))
            self.filled_before = i * (count(BACK) + count(NEXT)) - (count(BACK) - count(NEXT))
            self.previous = BANK_ORDER

    @staticmethod
    def uses(back, front, next_):
        if front and not back:
            return START_ORDER
        if back and not front:
            return END_ORDER
        if back and not next_:
            return CLOSING_ORDER
        kinds = (BACK if back else "") + (FRONT if front else "") + (NEXT if next_ else "")
        return [u for u in BANK_ORDER if u[0] in kinds]

    def bank(self, use):
        return self.order.index(use) % RING

    def filled(self, use):
        return self.filled_before + ([u for u in self.order if u[0] != "P"].index(use) + 1)

    def emptied(self, use):
        return self.before + (self.order.index(use) + 1)

    def emptied_before(self, use):
        return self.before - (len(self.previous) - 1 - self.previous.index(use))

    def reusable(self, use):
        return self.before + (self.order.index(use) + 1 - RING)


def attend(nc, ins, out, x1_dram, k_dram, v_dram, ffn_dram, ident, half_power, w_q, bias_q, bias_v, bias_o, bias_f,
           hand):
    with ExitStack() as ctx:
        sb = lambda n, s, d=F32: ctx.enter_context(nc.sbuf_tensor(n, s, d))
        ps = lambda n, s: ctx.enter_context(nc.psum_tensor(n, s, F32))
        sem = lambda n: ctx.enter_context(nc.semaphore(n))
        pair = lambda n, s: [sb(f"{n}_hi", s, F32R), sb(f"{n}_lo", s, F32R)]
        mask, mask_loaded = hand.mask, hand.mask_loaded
        hidden = sb("hidden", [P, NT, KEYS], I32)
        masked = sb("masked", [P, KEYS])
        v_block = pair("v_block", [KC[0][1], len(KC), GROUPS, P])
        x1, res1, k_block, qT, oT, x2T = hand.x1, hand.x_first, hand.k_block, hand.qT, hand.xT[0], hand.x2T
        x2T_odd = [q[:, :, 0:P] for q in qT]
        pT = pair("pT", [P, len(KC), GROUPS, S])
        x1T = oT
        w_o, w_ffn = ([sb(f"{w}_{k}", [P, NC, D], F32R) for k in ("hi", "lo")] for w in ("w_o", "w_ffn"))
        probs = sb("probs", [P, 2, XH * KEYS])
        top, total, per_total = sb("top_s", [P, 2, XH]), sb("total", [P, 2, XH]), sb("per_total", [P, 2, XH])
        y, x2_and_res2, y_out = sb("y", [P, 2, D]), sb("x2_and_res2", [P, 4, D]), sb("y_out", [P, 2, D])
        x2, res2 = x2_and_res2[:, 0:2, :], x2_and_res2[:, 2:4, :]
        raw_o, raw_ffn = res1[:], x2_and_res2[:]
        stats, mv = sb("stats", [P, 2, 6]), sb("mv", [P, 2, 2])
        ve, rstd = sb("ve", [P, 2]), sb("rstd", [P, 2])
        score_ps = ps("score_ps", [P, GROUPS, 512])
        shared_ps = [ps(f"shared_ps{n}", [P, 512]) for n in range(RING)]

        values_cleared, masked_set = sem("values_cleared"), sem("masked_set")
        x1_loaded, x1_stored, k_loaded, filled, freed, x1T_hi, q_hi = (hand.x1_loaded, hand.x1_stored, hand.k_loaded,
                                                                       hand.filled, hand.freed, hand.x1T_hi, hand.q_hi)
        w_loaded, w_hi, w_o_lo, w_ffn_lo = ([sem("w_o_loaded"), sem("w_ffn_loaded")], sem("w_hi"), sem("w_o_lo"),
                                          sem("w_ffn_lo"))
        res1_loaded, v_loaded = sem("res1_loaded"), sem("v_loaded")
        hidden_ready, res1_ready, res2_ready = sem("hidden_ready"), sem("res1_ready"), sem("res2_ready")
        oT_hi, x2T_hi = sem("oT_hi_ready"), sem("x2T_hi_ready")
        scored, hid, topped, exped, totalled, normed = (sem("scored"), sem("hid"), sem("topped"), sem("exped"),
                                                       sem("per_total_ready"), sem("normed"))
        turned, turned_hi = sem("turned_p"), sem("pT_hi_ready")
        stat_done, stat_seen, aggr_done = sem("stat_done"), sem("stat_seen"), sem("aggr_done")
        var_eps, rstd_ready, x2_ready, y_ready = sem("var_eps_b"), sem("rstd_b"), sem("x2_ready"), sem("y_ready")
        y_stored = [sem(f"y_stored{n}") for n in range(2)]
        block = ctx.enter_context(nc.Block())

        def steps(eng, step):
            step(1)
            with eng.Fori(2, B - 1) as i:
                step(i)

        def norm_count(i, s, use):
            return nth(i - 1, 2 * NT, s.norms.index(use))

        def x2T_of(i, t):
            return x2T_odd if isinstance(i, int) and i == B and t % 2 else x2T

        def turned_bank(s, t, c):
            return shared_ps[s.bank(f"P{t}{c}")][0:KC[c][1], :].rearrange("p (g n) -> p g n", g=GROUPS)

        @block.sync
        def _(sp):
            def load_mask(i):
                wait_reuse(sp, hidden_ready, i)
                sp.dma_start(mask[:], ins["mask"][i].rearrange("(t p) k -> p t k", p=P)).then_inc(mask_loaded, 16)

            def load_x1(i):
                wait_reuse(sp, x1T_hi, i * NC)
                sp.dma_start(x1[:], x1_dram[i].rearrange("(t p) d -> p t d", p=P)).then_inc(x1_loaded, 16)

            def load_residual(i, s, reuse):
                if reuse:
                    sp.wait_ge(freed, s.emptied("O3"))
                else:
                    sp.wait_ge(w_o_lo, NC)
                sp.dma_start(res1[:], x1_dram[i].rearrange("(t p) d -> p t d", p=P)).then_inc(res1_loaded, 16)

            def load_next_keys(i):
                wait_reuse(sp, scored, i * NT * 2)
                load_keys(sp, k_dram, hand, i)

            def load_values(i):
                wait_reuse(sp, oT_hi, i * NC)
                for part in range(2):
                    src = v_dram[part].rearrange("r (g j d) -> r g j d", g=GROUPS, j=GH)
                    for j, c, row, key, n in v_pieces():
                        sp.dma_start(v_block[part][row:row + n, c, :, j * XHD:(j + 1) * XHD].bitcast(F32),
                                     src[bass.ds(i * KEYS + key, n)][:, :, j, :]).then_inc(v_loaded, 16)

            def store(i, t):
                sp.wait_ge(y_ready, nth(i, NT, t))
                sp.dma_start(out[i, t * P:(t + 1) * P, :], y_out[:, t % 2, :]).then_inc(y_stored[t % 2], 16)

            for n in range(2):
                sp.wait_ge(x1_stored[n], 2 * 16 * NT // 2)
            load_x1(1)
            load_mask(1)
            for n, (raw, src) in enumerate(((raw_o, ins["W_o"]), (raw_ffn, ffn_dram))):
                sp.dma_start(raw, src.rearrange("(c p) n -> p c n", p=P)).then_inc(w_loaded[n], 16)
            sp.wait_ge(values_cleared, 2)
            for n in range(2):
                sp.wait_ge(x1_stored[n], 16 * B * NT // 2)

            def step(i, back, front, next_):
                if next_ and back:
                    load_x1(i + 1)
                    load_mask(i + 1)
                if front:
                    load_values(i)
                if back:
                    store(i - 1, 0)
                if next_:
                    load_next_keys(i + 1)
                if back:
                    store(i - 1, 1)
                if front:
                    load_residual(i, Shared(i, back, front, next_), back)
                if back:
                    store(i - 1, 2)
                    store(i - 1, 3)

            step(0, False, True, True)
            step(1, True, True, True)
            with sp.Fori(2, B - 1) as i:
                step(i, True, True, True)
            step(B - 1, True, True, False)
            step(B, True, False, False)
            for n in range(2):
                sp.wait_ge(y_stored[n], 16 * B * NT // 2)

        @block.tensor
        def _(pe):
            def turn_x1(i, s, c):
                if c == 0:
                    pe.wait_ge(x1_loaded, nth(i, 1, 0) * 16)
                use = f"X{c}"
                wait_reuse(pe, freed, s.reusable(use))
                for t in range(NT):
                    last = nc.tensor.transpose(shared_ps[s.bank(use)][:, t * P:(t + 1) * P],
                                               x1[:, t, c * P:(c + 1) * P], ident[:])
                last.then_inc(filled, 1)

            def project_q(i, s, c):
                use = f"Q{c}"
                if c == 0:
                    pe.wait_ge(x1T_hi, nth(i, NC, NC - 1))
                    pe.wait_ge(freed, s.emptied("X3"))
                wait_reuse(pe, freed, s.reusable(use))
                pieces = [([w[:, k, c * P:(c + 1) * P] for w in w_q], [x[:, k, :] for x in x1T]) for k in range(NC)]
                split_matmuls(nc, shared_ps[s.bank(use)][:], pieces).then_inc(filled, 1)

            def score(i, s, t, h):
                if t == 0:
                    pe.wait_ge(k_loaded, nth(i, 1, 0) * (16 * 2 * GH))
                    pe.wait_ge(q_hi, nth(i, NC, 2 * h + 1))
                    pe.wait_ge(freed, s.emptied_before(f"Q{2 * h + 1}"))
                wait_reuse(pe, exped, i * (NT * XH) + ((t - 1) * XH + (h + 1) * XH // 2))
                tok = slice(t * P, (t + 1) * P)
                for g in (2 * h, 2 * h + 1):
                    last = split_matmuls(nc, score_ps[:, g, 0:GK],
                                         [([q[:, g, tok] for q in qT], [k[:, g, :] for k in k_block])])
                last.then_inc(scored, 1)

            def turn_probs(i, s, t, c):
                if c == 0:
                    pe.wait_ge(normed, nth(i, NT * 2, 2 * t + 1))
                use = f"P{t}{c}"
                wait_reuse(pe, freed, s.reusable(use))
                at, size = KC[c]
                for g in range(GROUPS):
                    last = nc.tensor.transpose(shared_ps[s.bank(use)][0:size, g * P:(g + 1) * P],
                                               probs[:, t % 2, g * GK + at:g * GK + at + size], ident[:])
                last.then_inc(turned, 1)

            def weigh_values(i, s, g):
                use = f"V{g}"
                if g == 0:
                    pe.wait_ge(v_loaded, nth(i, 1, 0) * (16 * 2 * len(list(v_pieces()))))
                    pe.wait_ge(freed, s.emptied_before("P32"))
                    pe.wait_ge(turned_hi, nth(i, NT * 3, NT * 3 - 1))
                wait_reuse(pe, freed, s.reusable(use))
                pieces = [([v[0:size, c, g, :] for v in v_block], [p[0:size, c, g, :] for p in pT])
                          for c, (_, size) in enumerate(KC)]
                split_matmuls(nc, shared_ps[s.bank(use)][:], pieces).then_inc(filled, 1)

            def project_o(i, s, t):
                use = f"O{t}"
                if t == 0:
                    pe.wait_ge(w_o_lo, NC)
                    pe.wait_ge(oT_hi, nth(i - 1, NC, NC - 1))
                    pe.wait_ge(freed, s.emptied("V3"))
                wait_reuse(pe, freed, s.reusable(use))
                tok = slice(t * P, (t + 1) * P)
                pieces = [([o[:, k, tok] for o in oT], [w[:, k, :] for w in w_o]) for k in range(NC)]
                split_matmuls(nc, shared_ps[s.bank(use)][:], pieces).then_inc(filled, 1)

            def turn_x2(i, s, t):
                use = f"T{t}"
                pe.wait_ge(x2_ready, nth(i - 1, NT, t))
                wait_reuse(pe, freed, s.reusable(use))
                for c in range(NC):
                    last = nc.tensor.transpose(shared_ps[s.bank(use)][:, c * P:(c + 1) * P],
                                               x2[:, t % 2, c * P:(c + 1) * P], ident[:])
                last.then_inc(filled, 1)

            def project_f(i, s, t):
                use = f"F{t}"
                if t == 0:
                    pe.wait_ge(w_ffn_lo, NC)
                pe.wait_ge(x2T_hi, nth(i - 1, NT, t))
                pe.wait_ge(freed, s.emptied(f"T{t}"))
                wait_reuse(pe, freed, s.reusable(use))
                pieces = [([x[:, k, :] for x in x2T_of(i, t)], [w[:, k, :] for w in w_ffn]) for k in range(NC)]
                split_matmuls(nc, shared_ps[s.bank(use)][:], pieces).then_inc(filled, 1)

            def step(i):
                s = Shared(i, True, True, True)
                score(i, s, 0, 0)
                weigh_values(i - 1, s, 0)
                score(i, s, 0, 1)
                weigh_values(i - 1, s, 1)
                weigh_values(i - 1, s, 2)
                weigh_values(i - 1, s, 3)
                score(i, s, 1, 0)
                score(i, s, 1, 1)
                project_o(i, s, 0)
                turn_probs(i, s, 0, 0)
                project_o(i, s, 1)
                turn_probs(i, s, 0, 1)
                project_o(i, s, 2)
                turn_x2(i, s, 0)
                turn_probs(i, s, 0, 2)
                score(i, s, 2, 0)
                project_f(i, s, 0)
                turn_probs(i, s, 1, 0)
                turn_probs(i, s, 1, 1)
                turn_x2(i, s, 1)
                project_o(i, s, 3)
                score(i, s, 2, 1)
                turn_x1(i + 1, s, 0)
                turn_x1(i + 1, s, 1)
                turn_x1(i + 1, s, 2)
                project_f(i, s, 1)
                turn_x1(i + 1, s, 3)
                turn_x2(i, s, 2)
                turn_probs(i, s, 1, 2)
                score(i, s, 3, 0)
                score(i, s, 3, 1)
                project_q(i + 1, s, 0)
                project_f(i, s, 2)
                turn_probs(i, s, 2, 0)
                turn_probs(i, s, 2, 1)
                project_q(i + 1, s, 1)
                turn_x2(i, s, 3)
                project_q(i + 1, s, 2)
                turn_probs(i, s, 2, 2)
                project_f(i, s, 3)
                turn_probs(i, s, 3, 0)
                turn_probs(i, s, 3, 1)
                turn_probs(i, s, 3, 2)
                project_q(i + 1, s, 3)

            s = Shared(0, False, True, True)
            score(0, s, 0, 0)
            score(0, s, 0, 1)
            score(0, s, 1, 0)
            score(0, s, 1, 1)
            score(0, s, 2, 0)
            turn_probs(0, s, 0, 0)
            turn_probs(0, s, 0, 1)
            turn_probs(0, s, 0, 2)
            turn_x1(1, s, 0)
            score(0, s, 2, 1)
            turn_x1(1, s, 1)
            score(0, s, 3, 0)
            turn_x1(1, s, 2)
            turn_x1(1, s, 3)
            turn_probs(0, s, 1, 0)
            turn_probs(0, s, 1, 1)
            turn_probs(0, s, 1, 2)
            score(0, s, 3, 1)
            project_q(1, s, 0)
            turn_probs(0, s, 2, 0)
            turn_probs(0, s, 2, 1)
            project_q(1, s, 1)
            turn_probs(0, s, 2, 2)
            project_q(1, s, 2)
            turn_probs(0, s, 3, 0)
            turn_probs(0, s, 3, 1)
            turn_probs(0, s, 3, 2)
            project_q(1, s, 3)
            steps(pe, step)
            s = Shared(B - 1, True, True, False)
            score(B - 1, s, 0, 0)
            weigh_values(B - 2, s, 0)
            score(B - 1, s, 0, 1)
            weigh_values(B - 2, s, 1)
            weigh_values(B - 2, s, 2)
            weigh_values(B - 2, s, 3)
            score(B - 1, s, 1, 0)
            score(B - 1, s, 1, 1)
            project_o(B - 1, s, 0)
            turn_probs(B - 1, s, 0, 0)
            project_o(B - 1, s, 1)
            turn_probs(B - 1, s, 0, 1)
            turn_probs(B - 1, s, 0, 2)
            turn_x2(B - 1, s, 0)
            score(B - 1, s, 2, 0)
            project_o(B - 1, s, 2)
            score(B - 1, s, 2, 1)
            turn_probs(B - 1, s, 1, 0)
            turn_probs(B - 1, s, 1, 1)
            turn_probs(B - 1, s, 1, 2)
            score(B - 1, s, 3, 0)
            project_f(B - 1, s, 0)
            score(B - 1, s, 3, 1)
            turn_x2(B - 1, s, 1)
            project_o(B - 1, s, 3)
            turn_probs(B - 1, s, 2, 0)
            turn_probs(B - 1, s, 2, 1)
            project_f(B - 1, s, 1)
            turn_x2(B - 1, s, 2)
            turn_probs(B - 1, s, 2, 2)
            turn_probs(B - 1, s, 3, 0)
            project_f(B - 1, s, 2)
            turn_x2(B - 1, s, 3)
            turn_probs(B - 1, s, 3, 1)
            turn_probs(B - 1, s, 3, 2)
            project_f(B - 1, s, 3)
            s = Shared(B, True, False, False)
            weigh_values(B - 1, s, 0)
            weigh_values(B - 1, s, 1)
            weigh_values(B - 1, s, 2)
            weigh_values(B - 1, s, 3)
            project_o(B, s, 0)
            project_o(B, s, 1)
            project_o(B, s, 2)
            turn_x2(B, s, 0)
            project_o(B, s, 3)
            turn_x2(B, s, 1)
            project_f(B, s, 0)
            turn_x2(B, s, 2)
            project_f(B, s, 1)
            turn_x2(B, s, 3)
            project_f(B, s, 2)
            project_f(B, s, 3)

        @block.scalar
        def _(act):
            def split_x1(i, s, c):
                use = f"X{c}"
                act.wait_ge(filled, s.filled(use))
                nc.scalar.activation(x1T[0][:, c, :], shared_ps[s.bank(use)][:], ACT.Copy).then_inc(x1T_hi, 1)

            def split_q(i, s, c):
                use = f"Q{c}"
                act.wait_ge(filled, s.filled(use))
                nc.scalar.activation(qT[0][:, c, :], shared_ps[s.bank(use)][:], ACT.Identity,
                                     bias=bias_q[:, c:c + 1]).then_inc(q_hi, 1)

            def exponentials(i, t, h):
                act.wait_ge(topped, nth(i, NT * 2, 2 * t + h))
                if h == 0:
                    wait_reuse(act, turned, i * NT * 3 + (3 * (t - 1)))
                    wait_reuse(act, totalled, i * NT + (t - 1))
                for j in range(h * XH // 2, (h + 1) * XH // 2):
                    g, k = j // GH, j % GH
                    nc.scalar.activation(probs[:, t % 2, j * KEYS:(j + 1) * KEYS],
                                         score_ps[:, g, k * KEYS:(k + 1) * KEYS], ACT.Exp, bias=top[:, t % 2, j:j + 1],
                                         accum_out=total[:, t % 2, j:j + 1]).then_inc(exped, 1)

            def split_probs(i, s, t, c):
                act.wait_ge(turned, nth(i, NT * 3, 3 * t + c))
                size = KC[c][1]
                nc.scalar.activation(pT[0][0:size, c, :, t * P:(t + 1) * P], turned_bank(s, t, c),
                                     ACT.Copy).then_inc(turned_hi, 1)

            def split_o(i, s, g):
                use = f"V{g}"
                act.wait_ge(filled, s.filled(use))
                nc.scalar.activation(oT[0][:, g, :], shared_ps[s.bank(use)][:], ACT.Identity,
                                     bias=bias_v[:, g:g + 1]).then_inc(oT_hi, 1)

            def split_x2(i, s, t):
                use = f"T{t}"
                act.wait_ge(filled, s.filled(use))
                nc.scalar.activation(x2T_of(i, t)[0], shared_ps[s.bank(use)][:].rearrange("p (c n) -> p c n", c=NC),
                                     ACT.Copy).then_inc(x2T_hi, 1)

            def step(i):
                s = Shared(i, True, True, True)
                split_o(i - 1, s, 0)
                exponentials(i, 0, 0)
                split_o(i - 1, s, 1)
                exponentials(i, 0, 1)
                split_o(i - 1, s, 2)
                split_o(i - 1, s, 3)
                exponentials(i, 1, 0)
                split_probs(i, s, 0, 0)
                exponentials(i, 1, 1)
                split_probs(i, s, 0, 1)
                split_x2(i, s, 0)
                split_probs(i, s, 0, 2)
                split_probs(i, s, 1, 0)
                split_probs(i, s, 1, 1)
                split_x2(i, s, 1)
                exponentials(i, 2, 0)
                split_x1(i + 1, s, 0)
                split_x1(i + 1, s, 1)
                split_x1(i + 1, s, 2)
                exponentials(i, 2, 1)
                split_x1(i + 1, s, 3)
                split_x2(i, s, 2)
                split_probs(i, s, 1, 2)
                split_q(i + 1, s, 0)
                exponentials(i, 3, 0)
                split_probs(i, s, 2, 0)
                split_probs(i, s, 2, 1)
                exponentials(i, 3, 1)
                split_q(i + 1, s, 1)
                split_x2(i, s, 3)
                split_q(i + 1, s, 2)
                split_probs(i, s, 2, 2)
                split_probs(i, s, 3, 0)
                split_probs(i, s, 3, 1)
                split_probs(i, s, 3, 2)
                split_q(i + 1, s, 3)

            s = Shared(0, False, True, True)
            exponentials(0, 0, 0)
            exponentials(0, 0, 1)
            exponentials(0, 1, 0)
            exponentials(0, 1, 1)
            exponentials(0, 2, 0)
            split_probs(0, s, 0, 0)
            split_probs(0, s, 0, 1)
            split_probs(0, s, 0, 2)
            split_x1(1, s, 0)
            exponentials(0, 2, 1)
            split_x1(1, s, 1)
            split_x1(1, s, 2)
            split_x1(1, s, 3)
            split_probs(0, s, 1, 0)
            split_probs(0, s, 1, 1)
            split_probs(0, s, 1, 2)
            exponentials(0, 3, 0)
            exponentials(0, 3, 1)
            split_q(1, s, 0)
            split_probs(0, s, 2, 0)
            split_probs(0, s, 2, 1)
            split_q(1, s, 1)
            split_probs(0, s, 2, 2)
            act.wait_ge(w_loaded[0], 16)
            nc.scalar.activation(w_o[0][:], raw_o, ACT.Copy).then_inc(w_hi, 1)
            split_q(1, s, 2)
            split_probs(0, s, 3, 0)
            split_probs(0, s, 3, 1)
            split_probs(0, s, 3, 2)
            act.wait_ge(w_loaded[1], 16)
            nc.scalar.activation(w_ffn[0][:], raw_ffn, ACT.Copy).then_inc(w_hi, 1)
            split_q(1, s, 3)
            steps(act, step)
            s = Shared(B - 1, True, True, False)
            split_o(B - 2, s, 0)
            exponentials(B - 1, 0, 0)
            split_o(B - 2, s, 1)
            exponentials(B - 1, 0, 1)
            split_o(B - 2, s, 2)
            split_o(B - 2, s, 3)
            exponentials(B - 1, 1, 0)
            split_probs(B - 1, s, 0, 0)
            exponentials(B - 1, 1, 1)
            split_probs(B - 1, s, 0, 1)
            split_probs(B - 1, s, 0, 2)
            split_x2(B - 1, s, 0)
            exponentials(B - 1, 2, 0)
            split_probs(B - 1, s, 1, 0)
            split_probs(B - 1, s, 1, 1)
            split_probs(B - 1, s, 1, 2)
            exponentials(B - 1, 2, 1)
            exponentials(B - 1, 3, 0)
            split_x2(B - 1, s, 1)
            exponentials(B - 1, 3, 1)
            split_probs(B - 1, s, 2, 0)
            split_probs(B - 1, s, 2, 1)
            split_x2(B - 1, s, 2)
            split_probs(B - 1, s, 2, 2)
            split_probs(B - 1, s, 3, 0)
            split_x2(B - 1, s, 3)
            split_probs(B - 1, s, 3, 1)
            split_probs(B - 1, s, 3, 2)
            s = Shared(B, True, False, False)
            split_o(B - 1, s, 0)
            split_o(B - 1, s, 1)
            split_o(B - 1, s, 2)
            split_o(B - 1, s, 3)
            split_x2(B, s, 0)
            split_x2(B, s, 1)
            split_x2(B, s, 2)
            split_x2(B, s, 3)

        @block.gpsimd
        def _(pool):
            def root(i, s, use):
                n = s.norms.index(use) % 2
                pool.wait_ge(var_eps, norm_count(i, s, use))
                nc.gpsimd.tensor_tensor(rstd[:, n:n + 1], ve[:, n:n + 1], half_power[:], ALU.pow).then_inc(rstd_ready, 1)

            def normalize_probs(i, t, h):
                pool.wait_ge(totalled, nth(i, NT, t))
                pool.wait_ge(exped, nth(i, NT * XH, t * XH + XH - 1))
                heads = XH // 2
                p = probs[:, t % 2, h * heads * KEYS:(h + 1) * heads * KEYS].rearrange("p (j k) -> p j k", j=heads)
                nc.gpsimd.tensor_tensor(p, p, per_total[:, t % 2, h * heads:(h + 1) * heads].unsqueeze(2)
                                        .to_broadcast([P, heads, KEYS]), ALU.mult).then_inc(normed, 1)

            def bias_residual(i, t):
                if t == 0:
                    pool.wait_ge(res1_loaded, nth(i, 1, 0) * 16)
                nc.gpsimd.tensor_tensor(res1[:, t, :], res1[:, t, :], bias_o[:], ALU.add).then_inc(res1_ready, 1)

            def bias_x2(i, s, t):
                pool.wait_ge(x2_ready, nth(i - 1, NT, t))
                if t >= 2:
                    pool.wait_ge(freed, s.emptied(f"F{t - 2}"))
                nc.gpsimd.tensor_tensor(res2[:, t % 2, :], x2[:, t % 2, :], bias_f[:], ALU.add).then_inc(res2_ready, 1)

            def step(i):
                s = Shared(i, True, True, True)
                bias_residual(i - 1, 0)
                bias_residual(i - 1, 1)
                bias_residual(i - 1, 2)
                bias_residual(i - 1, 3)
                normalize_probs(i, 0, 0)
                normalize_probs(i, 0, 1)
                root(i, s, "O0")
                bias_x2(i, s, 0)
                root(i, s, "O1")
                normalize_probs(i, 1, 0)
                normalize_probs(i, 1, 1)
                bias_x2(i, s, 1)
                root(i, s, "O2")
                bias_x2(i, s, 2)
                root(i, s, "F0")
                root(i, s, "O3")
                bias_x2(i, s, 3)
                normalize_probs(i, 2, 0)
                root(i, s, "F1")
                normalize_probs(i, 2, 1)
                root(i, s, "F2")
                normalize_probs(i, 3, 0)
                normalize_probs(i, 3, 1)
                root(i, s, "F3")

            for tile in v_block:
                nc.gpsimd.memset(tile[:].bitcast(F32), 0.0).then_inc(values_cleared, 1)

            normalize_probs(0, 0, 0)
            normalize_probs(0, 0, 1)
            normalize_probs(0, 1, 0)
            normalize_probs(0, 1, 1)
            normalize_probs(0, 2, 0)
            normalize_probs(0, 2, 1)
            normalize_probs(0, 3, 0)
            normalize_probs(0, 3, 1)
            pool.wait_ge(w_hi, 2)
            pool.wait_ge(w_loaded[1], 16)
            for c in range(NC):
                nc.gpsimd.tensor_tensor(w_ffn[1][:, c, :], raw_ffn[:, c, :], w_ffn[0][:, c, :].bitcast(F32),
                                        ALU.subtract).then_inc(w_ffn_lo, 1)
            steps(pool, step)
            s = Shared(B - 1, True, True, False)
            bias_residual(B - 2, 0)
            bias_residual(B - 2, 1)
            bias_residual(B - 2, 2)
            bias_residual(B - 2, 3)
            normalize_probs(B - 1, 0, 0)
            normalize_probs(B - 1, 0, 1)
            root(B - 1, s, "O0")
            bias_x2(B - 1, s, 0)
            root(B - 1, s, "O1")
            normalize_probs(B - 1, 1, 0)
            normalize_probs(B - 1, 1, 1)
            bias_x2(B - 1, s, 1)
            root(B - 1, s, "O2")
            normalize_probs(B - 1, 2, 0)
            normalize_probs(B - 1, 2, 1)
            bias_x2(B - 1, s, 2)
            root(B - 1, s, "F0")
            normalize_probs(B - 1, 3, 0)
            normalize_probs(B - 1, 3, 1)
            root(B - 1, s, "O3")
            bias_x2(B - 1, s, 3)
            root(B - 1, s, "F1")
            root(B - 1, s, "F2")
            root(B - 1, s, "F3")
            s = Shared(B, True, False, False)
            bias_residual(B - 1, 0)
            bias_residual(B - 1, 1)
            bias_residual(B - 1, 2)
            bias_residual(B - 1, 3)
            root(B, s, "O0")
            bias_x2(B, s, 0)
            root(B, s, "O1")
            bias_x2(B, s, 1)
            root(B, s, "O2")
            root(B, s, "O3")
            bias_x2(B, s, 2)
            root(B, s, "F0")
            bias_x2(B, s, 3)
            root(B, s, "F1")
            root(B, s, "F2")
            root(B, s, "F3")

        @block.vector
        def _(dve):
            nc.vector.memset(masked[:], MASKED).then_inc(masked_set, 1)
            dve.wait_ge(masked_set, 1)

            def remainder(s, use, hi_ready, count, hi, lo, psum):
                dve.wait_ge(hi_ready, count)
                nc.vector.tensor_tensor(lo, psum, hi.bitcast(F32), ALU.subtract).then_inc(freed, 1)

            def split_x1(i, s, c):
                remainder(s, f"X{c}", x1T_hi, nth(i, NC, c), x1T[0][:, c, :], x1T[1][:, c, :],
                          shared_ps[s.bank(f"X{c}")][:])

            def biased_remainder(hi_ready, count, hi, lo, psum, bias):
                dve.wait_ge(hi_ready, count)
                nc.vector.scalar_tensor_tensor(out=lo, in0=psum, scalar=bias, in1=hi.bitcast(F32), op0=ALU.add,
                                               op1=ALU.subtract).then_inc(freed, 1)

            def split_q(i, s, c):
                biased_remainder(q_hi, nth(i, NC, c), qT[0][:, c, :], qT[1][:, c, :], shared_ps[s.bank(f"Q{c}")][:],
                                 bias_q[:, c:c + 1])

            def split_o(i, s, g):
                biased_remainder(oT_hi, nth(i, NC, g), oT[0][:, g, :], oT[1][:, g, :], shared_ps[s.bank(f"V{g}")][:],
                                 bias_v[:, g:g + 1])

            def split_x2(i, s, t):
                remainder(s, f"T{t}", x2T_hi, nth(i - 1, NT, t), x2T_of(i, t)[0], x2T_of(i, t)[1],
                          shared_ps[s.bank(f"T{t}")][:].rearrange("p (c n) -> p c n", c=NC))

            def split_probs(i, s, t, c):
                size = KC[c][1]
                dve.wait_ge(turned_hi, nth(i, NT * 3, 3 * t + c))
                tok = slice(t * P, (t + 1) * P)
                nc.vector.tensor_tensor(pT[1][0:size, c, :, tok], turned_bank(s, t, c),
                                        pT[0][0:size, c, :, tok].bitcast(F32), ALU.subtract).then_inc(freed, 1)

            def find_hidden(i):
                dve.wait_ge(mask_loaded, nth(i, 1, 0) * 16)
                wait_reuse(dve, hid, i * NT * 2)
                nc.vector.tensor_scalar(hidden[:], mask[:], 0.0, None, ALU.is_equal).then_inc(hidden_ready, 1)

            def softmax_top(i, t, h):
                dve.wait_ge(scored, nth(i, NT * 2, 2 * t + h))
                dve.wait_ge(hidden_ready, nth(i, 1, 0))
                dve.sem_inc(stat_seen, 1)
                shape = [P, GROUPS // 2, GH, KEYS]
                s4 = score_ps[:, 2 * h:2 * h + 2, 0:GK].rearrange("p g (j k) -> p g j k", j=GH)
                nc.vector.copy_predicated(s4, hidden[:, t, :].unsqueeze(1).unsqueeze(1).to_broadcast(shape),
                                          masked[:].unsqueeze(1).unsqueeze(1).to_broadcast(shape)).then_inc(hid, 1)
                dve.wait_ge(hid, nth(i, NT * 2, 2 * t + h))
                wait_reuse(dve, exped, i * NT * XH + (t - 1) * XH)
                nc.vector.tensor_reduce(top[:, t % 2, h * 8:(h + 1) * 8].rearrange("p (g j) -> p g j", j=GH), s4, AX.X,
                                        ALU.max, negate=True).then_inc(topped, 1)

            def invert_totals(i, t):
                dve.wait_ge(exped, nth(i, NT * XH, t * XH + XH - 1))
                wait_reuse(dve, normed, i * NT * 2 + 2 * (t - 1))
                nc.vector.reciprocal(per_total[:, t % 2, :], total[:, t % 2, :]).then_inc(totalled, 1)

            def add(i, s, use, residual, res_ready, res_count):
                n = s.norms.index(use) % 2
                dve.wait_ge(filled, s.filled(use))
                dve.wait_ge(res_ready, res_count)
                if s.norms.index(use) < 2:
                    wait_reuse(dve, y_ready, (i - 1) * NT)
                else:
                    before = s.norms[s.norms.index(use) - 2]
                    dve.wait_ge(x2_ready if before[0] == "O" else y_ready, nth(i - 1, NT, int(before[1])))
                nc.vector.tensor_tensor(y[:, n, :], shared_ps[s.bank(use)][:], residual, ALU.add).then_inc(freed, 1)

            def measure(i, s, use):
                n = s.norms.index(use) % 2
                dve.wait_ge(freed, s.emptied(use))
                nc.vector.bn_stats(stats[:, n, :], y[:, n, :]).then_inc(stat_done, 1)
                dve.wait_ge(stat_done, norm_count(i, s, use))
                dve.sem_inc(stat_seen, 1)
                nc.vector.bn_aggr(mv[:, n, :], stats[:, n, :]).then_inc(aggr_done, 1)
                dve.wait_ge(aggr_done, norm_count(i, s, use))
                nc.vector.tensor_scalar(ve[:, n:n + 1], mv[:, n, 1:2], EPS, None, ALU.add).then_inc(var_eps, 1)

            def add_o(i, s, t):
                add(i, s, f"O{t}", res1[:, t, :], res1_ready, nth(i - 1, NT, t))

            def add_f(i, s, t):
                add(i, s, f"F{t}", res2[:, t % 2, :], res2_ready, nth(i - 1, NT, t))

            def normalize(i, s, use, target, ready):
                n = s.norms.index(use) % 2
                dve.wait_ge(rstd_ready, norm_count(i, s, use))
                nc.vector.tensor_scalar(target, y[:, n, :], mv[:, n, 0:1], rstd[:, n:n + 1], ALU.subtract,
                                        ALU.mult).then_inc(ready, 1)

            def normalize_o(i, s, t):
                wait_reuse(dve, res2_ready, two_back(i - 1, NT, t))
                wait_reuse(dve, x2T_hi, two_back(i - 1, NT, t))
                normalize(i, s, f"O{t}", x2[:, t % 2, :], x2_ready)

            def normalize_f(i, s, t):
                wait_reuse(dve, y_stored[t % 2], (i - 1) * 32 + 16 * (t // 2))
                normalize(i, s, f"F{t}", y_out[:, t % 2, :], y_ready)

            def step(i):
                s = Shared(i, True, True, True)
                softmax_top(i, 0, 0)
                split_o(i - 1, s, 0)
                softmax_top(i, 0, 1)
                split_o(i - 1, s, 1)
                invert_totals(i, 0)
                split_o(i - 1, s, 2)
                split_o(i - 1, s, 3)
                softmax_top(i, 1, 0)
                softmax_top(i, 1, 1)
                add_o(i, s, 0)
                measure(i, s, "O0")
                split_probs(i, s, 0, 0)
                add_o(i, s, 1)
                normalize_o(i, s, 0)
                measure(i, s, "O1")
                split_probs(i, s, 0, 1)
                invert_totals(i, 1)
                add_o(i, s, 2)
                normalize_o(i, s, 1)
                split_x2(i, s, 0)
                measure(i, s, "O2")
                split_probs(i, s, 0, 2)
                softmax_top(i, 2, 0)
                add_f(i, s, 0)
                normalize_o(i, s, 2)
                split_probs(i, s, 1, 0)
                measure(i, s, "F0")
                split_probs(i, s, 1, 1)
                split_x2(i, s, 1)
                normalize_f(i, s, 0)
                add_o(i, s, 3)
                softmax_top(i, 2, 1)
                split_x1(i + 1, s, 0)
                measure(i, s, "O3")
                split_x1(i + 1, s, 1)
                split_x1(i + 1, s, 2)
                normalize_o(i, s, 3)
                add_f(i, s, 1)
                invert_totals(i, 2)
                split_x1(i + 1, s, 3)
                measure(i, s, "F1")
                split_x2(i, s, 2)
                softmax_top(i, 3, 0)
                split_probs(i, s, 1, 2)
                normalize_f(i, s, 1)
                split_q(i + 1, s, 0)
                softmax_top(i, 3, 1)
                add_f(i, s, 2)
                find_hidden(i + 1)
                split_probs(i, s, 2, 0)
                measure(i, s, "F2")
                split_probs(i, s, 2, 1)
                invert_totals(i, 3)
                normalize_f(i, s, 2)
                split_q(i + 1, s, 1)
                split_x2(i, s, 3)
                split_q(i + 1, s, 2)
                split_probs(i, s, 2, 2)
                add_f(i, s, 3)
                measure(i, s, "F3")
                split_probs(i, s, 3, 0)
                split_probs(i, s, 3, 1)
                normalize_f(i, s, 3)
                split_probs(i, s, 3, 2)
                split_q(i + 1, s, 3)

            find_hidden(0)
            s = Shared(0, False, True, True)
            softmax_top(0, 0, 0)
            softmax_top(0, 0, 1)
            softmax_top(0, 1, 0)
            invert_totals(0, 0)
            softmax_top(0, 1, 1)
            softmax_top(0, 2, 0)
            invert_totals(0, 1)
            softmax_top(0, 2, 1)
            split_probs(0, s, 0, 0)
            split_probs(0, s, 0, 1)
            split_probs(0, s, 0, 2)
            split_x1(1, s, 0)
            softmax_top(0, 3, 0)
            invert_totals(0, 2)
            split_x1(1, s, 1)
            split_x1(1, s, 2)
            split_x1(1, s, 3)
            softmax_top(0, 3, 1)
            split_probs(0, s, 1, 0)
            split_probs(0, s, 1, 1)
            split_probs(0, s, 1, 2)
            find_hidden(1)
            invert_totals(0, 3)
            split_q(1, s, 0)
            split_probs(0, s, 2, 0)
            split_probs(0, s, 2, 1)
            split_q(1, s, 1)
            split_probs(0, s, 2, 2)
            split_q(1, s, 2)
            split_probs(0, s, 3, 0)
            split_probs(0, s, 3, 1)
            split_probs(0, s, 3, 2)
            dve.wait_ge(w_hi, 1)
            dve.wait_ge(w_loaded[0], 16)
            for c in range(NC):
                nc.vector.tensor_tensor(w_o[1][:, c, :], raw_o[:, c, :], w_o[0][:, c, :].bitcast(F32),
                                        ALU.subtract).then_inc(w_o_lo, 1)
            split_q(1, s, 3)
            steps(dve, step)
            s = Shared(B - 1, True, True, False)
            softmax_top(B - 1, 0, 0)
            split_o(B - 2, s, 0)
            softmax_top(B - 1, 0, 1)
            split_o(B - 2, s, 1)
            invert_totals(B - 1, 0)
            split_o(B - 2, s, 2)
            split_o(B - 2, s, 3)
            softmax_top(B - 1, 1, 0)
            softmax_top(B - 1, 1, 1)
            add_o(B - 1, s, 0)
            measure(B - 1, s, "O0")
            split_probs(B - 1, s, 0, 0)
            add_o(B - 1, s, 1)
            normalize_o(B - 1, s, 0)
            measure(B - 1, s, "O1")
            split_probs(B - 1, s, 0, 1)
            invert_totals(B - 1, 1)
            softmax_top(B - 1, 2, 0)
            split_probs(B - 1, s, 0, 2)
            normalize_o(B - 1, s, 1)
            split_x2(B - 1, s, 0)
            softmax_top(B - 1, 2, 1)
            add_o(B - 1, s, 2)
            softmax_top(B - 1, 3, 0)
            split_probs(B - 1, s, 1, 0)
            measure(B - 1, s, "O2")
            split_probs(B - 1, s, 1, 1)
            invert_totals(B - 1, 2)
            softmax_top(B - 1, 3, 1)
            split_probs(B - 1, s, 1, 2)
            normalize_o(B - 1, s, 2)
            add_f(B - 1, s, 0)
            split_x2(B - 1, s, 1)
            measure(B - 1, s, "F0")
            add_o(B - 1, s, 3)
            invert_totals(B - 1, 3)
            split_probs(B - 1, s, 2, 0)
            normalize_f(B - 1, s, 0)
            split_probs(B - 1, s, 2, 1)
            measure(B - 1, s, "O3")
            add_f(B - 1, s, 1)
            split_x2(B - 1, s, 2)
            normalize_o(B - 1, s, 3)
            split_probs(B - 1, s, 2, 2)
            measure(B - 1, s, "F1")
            split_probs(B - 1, s, 3, 0)
            add_f(B - 1, s, 2)
            normalize_f(B - 1, s, 1)
            split_x2(B - 1, s, 3)
            measure(B - 1, s, "F2")
            split_probs(B - 1, s, 3, 1)
            split_probs(B - 1, s, 3, 2)
            normalize_f(B - 1, s, 2)
            add_f(B - 1, s, 3)
            measure(B - 1, s, "F3")
            normalize_f(B - 1, s, 3)
            s = Shared(B, True, False, False)
            split_o(B - 1, s, 0)
            split_o(B - 1, s, 1)
            split_o(B - 1, s, 2)
            split_o(B - 1, s, 3)
            add_o(B, s, 0)
            measure(B, s, "O0")
            add_o(B, s, 1)
            normalize_o(B, s, 0)
            measure(B, s, "O1")
            add_o(B, s, 2)
            normalize_o(B, s, 1)
            measure(B, s, "O2")
            split_x2(B, s, 0)
            add_o(B, s, 3)
            normalize_o(B, s, 2)
            measure(B, s, "O3")
            split_x2(B, s, 1)
            add_f(B, s, 0)
            normalize_o(B, s, 3)
            measure(B, s, "F0")
            split_x2(B, s, 2)
            add_f(B, s, 1)
            normalize_f(B, s, 0)
            measure(B, s, "F1")
            split_x2(B, s, 3)
            add_f(B, s, 2)
            normalize_f(B, s, 1)
            measure(B, s, "F2")
            add_f(B, s, 3)
            normalize_f(B, s, 2)
            measure(B, s, "F3")
            normalize_f(B, s, 3)


def build(nc, ins, out):
    x1_dram = nc.dram_tensor("x1_between", (B, S, D), F32).ap()
    k_dram = nc.dram_tensor("keys_split", (2, D, B * KEYS), F32).ap()
    v_dram = nc.dram_tensor("values_split", (2, B * KEYS, D), F32).ap()
    ffn_dram = nc.dram_tensor("ffn_weight", (D, D), F32).ap()
    with ExitStack() as ctx:
        sb = lambda n, s, d=F32: ctx.enter_context(nc.sbuf_tensor(n, s, d))
        sem = lambda n: ctx.enter_context(nc.semaphore(n))
        ident, half_power, sigma = sb("ident", [P, P]), sb("half_power", [P, 1]), sb("sigma", [P, 1])
        bias_q, bias_v = sb("bias_q", [P, NC]), sb("bias_v", [P, NC])
        bias_o, bias_f = sb("bias_o", [P, D]), sb("bias_f", [P, D])
        w_q = [sb(f"w_q_{k}", [P, NC, D], F32R) for k in ("hi", "lo")]
        wide = lambda b: b.rearrange("(a n) -> a n", a=1).to_broadcast([P, D])
        rows = lambda b: b.rearrange("(c p) -> p c", p=P)
        constants = [(sigma, ins["product_sign"]), (bias_q, rows(ins["b_q"])), (bias_v, rows(ins["b_v"])),
                     (bias_o, wide(ins["b_o"])), (bias_f, wide(ins["bias"]))]
        hand = Handover(nc, ctx)
        with ExitStack() as mixing:
            w_spec, w_back = ([mixing.enter_context(nc.sbuf_tensor(f"{w}_{k}", shape, F32R)) for k in ("hi", "lo")]
                              for w, shape in (("w_spec", [P, NC, 3, D]), ("w_back", [P, NC, D])))
            prepare(nc, ins, constants, half_power, ident, w_spec, w_back, k_dram, v_dram, ffn_dram, hand.x_first,
                    hand.x_loaded, hand.x1, w_q, hand.xT[0], hand.xT[1])
            mix_tokens(nc, ins["x"], x1_dram, k_dram, ins["mask"], ident, sigma, w_spec, w_back, half_power, ins["W_q"], w_q,
                       bias_q, hand)
        attend(nc, ins, out, x1_dram, k_dram, v_dram, ffn_dram, ident, half_power, w_q, bias_q, bias_v, bias_o, bias_f,
               hand)


_INS = {"x": "x", "ctx": "ctx_1024", "mask": "mask_BxSxS2_ik1", "w_qkv": "L0_attn_w_qkv", "w_out": "L0_attn_w_out",
        "W_q": "L0_xattn_W_q", "b_q": "L0_xattn_b_q", "W_k": "L0_xattn_W_k", "b_k": "L0_xattn_b_k",
        "W_v": "L0_xattn_W_v", "b_v": "L0_xattn_b_v", "W_o": "L0_xattn_W_o", "b_o": "L0_xattn_b_o",
        "kernel": "L0_ffn_kernel", "bias": "L0_ffn_bias", "a": "L0_ffn_a", "b": "L0_ffn_b"}


def _constants():
    n, k = np.arange(MIX_HD)[:, None], np.arange(1, MIX_HD // 2)[None, :]
    angle = 2 * np.pi * n * k / MIX_HD
    even, odd = (1.0 + (-1.0) ** n) / 2, (1.0 - (-1.0) ** n) / 2
    half = P // 2
    fwd, inv = np.zeros((P, P)), np.zeros((P, 2, 256))
    nf = MIX_HD // 2 - 1
    for local in range(2):
        rows = slice(local * MIX_HD, (local + 1) * MIX_HD)
        re, im = slice(local * nf, (local + 1) * nf), slice(half + local * nf, half + (local + 1) * nf)
        u, w = 2 * nf + local, half + 2 * nf + local
        fwd[rows, re], fwd[rows, im], fwd[rows, u], fwd[rows, w] = np.cos(angle), -np.sin(angle), even[:, 0], odd[:, 0]
    for pair in range(2):
        inv[:, pair, pair * half:(pair + 1) * half] = fwd[:, :half] * (2 / MIX_HD)
        inv[:, pair, P + pair * half:P + (pair + 1) * half] = fwd[:, half:] * (2 / MIX_HD)
    sign = np.ones((P, 1))
    sign[2 * nf:half] = sign[half + 2 * nf:] = -1.0
    return {"dft_forward": fwd.astype(np.float32), "dft_inverse": inv.astype(np.float32),
            "identity": np.eye(P, dtype=np.float32), "product_sign": sign.astype(np.float32)}


def kernel(**inputs):
    import concourse.bacc as bacc
    from concourse.bass_utils import run_bass_kernel_spmd

    nc = bacc.Bacc("TRN2", target_bir_lowering=False, num_devices=1)
    arrays = {short: np.ascontiguousarray(inputs[name]) for short, name in _INS.items()}
    arrays.update(_constants())
    aps = {n: nc.dram_tensor(f"in_{n}", a.shape, mybir.dt.from_np(a.dtype), kind="ExternalInput").ap()
           for n, a in arrays.items()}
    out = nc.dram_tensor("out_0", (B, S, D), F32, kind="ExternalOutput").ap()
    build(nc, aps, out)
    r = run_bass_kernel_spmd(nc, [{f"in_{n}": a for n, a in arrays.items()}], core_ids=[0])
    return r.results[0]["out_0"]
```
